# Optimizing a Trainium2 kernel written in Bass

```python
import numpy as np
import jax
import jax.numpy as jnp

def _softmax(x, axis=-1):
    return jax.nn.softmax(x, axis=axis)

def _gelu(x):
    return jax.nn.gelu(x, approximate=True)

def _silu(x):
    return jax.nn.silu(x)

def _sigmoid(x):
    return jax.nn.sigmoid(x)

def _layernorm(x, axis=-1, eps=1e-05):
    m = jnp.mean(x, axis=axis, keepdims=True)
    v = jnp.var(x, axis=axis, keepdims=True)
    return (x - m) / jnp.sqrt(v + eps)

def _scatter_add(tgt, idx, src, axis=0):
    return tgt.at[idx].add(src)

def _segment_sum(src, seg, n):
    return jax.ops.segment_sum(src, seg, n)
kernel_name = 'mk_decoder_preln_d2_seqx_r8_41e21a'

def setup_inputs(seed: int=0):
    np.random.seed(seed)
    _w = jnp.asarray

    def _rec_inputs():
        import jax
        import jax.numpy as jnp
        _rk = jax.random.key(seed)
        x = -0.0002928 + 1 * jax.random.normal(jax.random.fold_in(_rk, 1), (64, 64, 128), jnp.float32)
        _lenS = 64 - jax.random.randint(jax.random.fold_in(_rk, 7), (64,), 0, max(1, 64 // 4) + 1, jnp.int32)
        _lenS2 = 64 - jax.random.randint(jax.random.fold_in(_rk, 8), (64,), 0, max(1, 64 // 4) + 1, jnp.int32)
        _ctx_1024P = jax.random.normal(jax.random.fold_in(_rk, 11), (64, 16, 128), jnp.float32)
        _ctx_1024c = jax.random.dirichlet(jax.random.fold_in(_rk, 511), 0.3 * jnp.ones((16,), jnp.float32), (64, 64))
        _ctx_1024t = jnp.einsum('bsk,bkd->bsd', _ctx_1024c, _ctx_1024P)
        _ctx_1024t = _ctx_1024t * jax.lax.rsqrt(jnp.mean(jnp.square(_ctx_1024t)) + 1e-12) * 0.953939
        ctx_1024 = -1.39393e-06 + 0.999914 * (_ctx_1024t + 0.3 * jax.random.normal(jax.random.fold_in(_rk, 611), (64, 64, 128), jnp.float32))
        _validS = jnp.arange(64)[None, :] < _lenS[:, None]
        _validS2 = jnp.arange(64)[None, :] < _lenS2[:, None]
        _causal = jnp.tril(jnp.ones((64, 64), dtype=bool))
        mask_BxS2_bf0 = jnp.logical_not(jnp.ones((64, 64), dtype=bool))
        mask_BxS2_ik1 = jnp.where(jnp.broadcast_to(_validS2[:, :], (64, 64)), 1, 0).astype(jnp.int32)
        return (x, ctx_1024, mask_BxS2_bf0, mask_BxS2_ik1)
    x, ctx_1024, mask_BxS2_bf0, mask_BxS2_ik1 = _rec_inputs()

    def _L0_attn_setup():
        import jax, jax.numpy as jnp
        import numpy as np
        from jax import lax
        B, L, D = (2, 256, 128)
        E, N, D_DELTA, D_CONV = (256, 16, 64, 4)
        EPS = 1e-05
        key = jax.random.key(seed)
        ks = jax.random.split(key, 16)
        s = lambda fan_in: 1.0 / np.sqrt(fan_in)
        return {'resid': jax.random.normal(ks[0], (B, L, D), jnp.float32), 'norm_w': jnp.ones((D,), jnp.float32), 'skip_w': jax.random.normal(ks[1], (E, D), jnp.float32) * s(D), 'in_w': jax.random.normal(ks[2], (E, D), jnp.float32) * s(D), 'conv_w': jax.random.normal(ks[3], (E, 1, D_CONV), jnp.float32) * s(D_CONV), 'conv_b': jnp.zeros((E,), jnp.float32), 'wd1': jax.random.normal(ks[4], (D_DELTA, E), jnp.float32) * s(E), 'wd2': jax.random.normal(ks[5], (E, D_DELTA), jnp.float32) * s(D_DELTA), 'wd2_b': jnp.zeros((E,), jnp.float32), 'wb': jax.random.normal(ks[6], (N, E), jnp.float32) * s(E), 'wc': jax.random.normal(ks[7], (N, E), jnp.float32) * s(E), 'A_log': jnp.log(jax.random.uniform(ks[8], (E, N), jnp.float32, 0.5, 1.5)), 'W_D': jnp.ones((E,), jnp.float32), 'out_w': jax.random.normal(ks[9], (D, E), jnp.float32) * s(E)}
    _L0_attn_all = _L0_attn_setup()
    _L0_attn_in = {k: v for k, v in _L0_attn_all.items() if k in ('norm_w', 'skip_w', 'in_w', 'conv_w', 'conv_b', 'wd1', 'wd2', 'wd2_b', 'wb', 'wc', 'A_log', 'W_D', 'out_w')}
    del _L0_attn_all

    def _L0_xattn_setup():
        import jax, jax.numpy as jnp
        import numpy as np
        import math
        D_MODEL = 128
        NUM_HEADS = 16
        D_K = D_MODEL // NUM_HEADS
        MAX_REL = 64
        B, L = (2, 256)
        key = jax.random.key(seed)
        ks = jax.random.split(key, 12)
        s = 1.0 / math.sqrt(D_MODEL)
        inp = {'query': jax.random.normal(ks[0], (B, L, D_MODEL), jnp.float32), 'key': jax.random.normal(ks[1], (B, L, D_MODEL), jnp.float32), 'value': jax.random.normal(ks[2], (B, L, D_MODEL), jnp.float32), 'key_padding_mask': jnp.zeros((B, L), dtype=bool), 'Wq': jax.random.normal(ks[3], (D_MODEL, D_MODEL), jnp.float32) * s, 'bq': jnp.zeros((D_MODEL,), jnp.float32), 'Wk': jax.random.normal(ks[4], (D_MODEL, D_MODEL), jnp.float32) * s, 'bk': jnp.zeros((D_MODEL,), jnp.float32), 'Wv': jax.random.normal(ks[5], (D_MODEL, D_MODEL), jnp.float32) * s, 'bv': jnp.zeros((D_MODEL,), jnp.float32), 'Wo': jax.random.normal(ks[6], (D_MODEL, D_MODEL), jnp.float32) * s, 'bo': jnp.zeros((D_MODEL,), jnp.float32), 'rel_bias': jax.random.normal(ks[7], (NUM_HEADS, 2 * MAX_REL - 1), jnp.float32) * 0.1}
        return inp
    _L0_xattn_all = _L0_xattn_setup()
    _L0_xattn_in = {k: v for k, v in _L0_xattn_all.items() if k in ('Wq', 'bq', 'Wk', 'bk', 'Wv', 'bv', 'Wo', 'bo', 'rel_bias')}
    del _L0_xattn_all

    def _L0_ffn_setup():
        import math
        import jax, jax.numpy as jnp
        import numpy as np
        B, L, D, F_FF, E = (4, 256, 128, 512, 8)
        TOP_K = 1
        CAPACITY_FACTOR = 1.25
        key = jax.random.key(seed)
        ks = jax.random.split(key, 4)
        h = jax.random.normal(ks[0], (B, L, D), dtype=jnp.float32)
        gate_w = jax.random.normal(ks[1], (E, D), dtype=jnp.float32) * 0.02
        gate_b = jnp.zeros((E,), dtype=jnp.float32)
        w1 = jax.random.normal(ks[2], (E, D, F_FF), dtype=jnp.float32) * 0.02
        b1 = jnp.zeros((E, F_FF), dtype=jnp.float32)
        w2 = jax.random.normal(ks[3], (E, F_FF, D), dtype=jnp.float32) * 0.02
        b2 = jnp.zeros((E, D), dtype=jnp.float32)
        return {'h': h, 'gate_w': gate_w, 'gate_b': gate_b, 'w1': w1, 'b1': b1, 'w2': w2, 'b2': b2}
    _L0_ffn_all = _L0_ffn_setup()
    _L0_ffn_in = {k: v for k, v in _L0_ffn_all.items() if k in ('gate_w', 'gate_b', 'w1', 'b1', 'w2', 'b2')}
    del _L0_ffn_all

    def _L1_attn_setup():
        import jax, jax.numpy as jnp
        import numpy as np
        B, S, D, H = (8, 128, 128, 128)
        NBLOCKS = 2
        EPS = 1e-05

        def _xavier(key, shape):
            fan_out, fan_in = shape
            lim = float(np.sqrt(6.0 / (fan_in + fan_out)))
            return jax.random.uniform(key, shape, jnp.float32, -lim, lim)

        def _slstm(x, W, R, b):
            Hh = R.shape[1]
            Bn = x.shape[0]
            xp = jnp.swapaxes(jnp.einsum('bsd,gd->bsg', x, W) + b, 0, 1)
            zeros = jnp.zeros((Bn, Hh), x.dtype)

            def step(carry, xpt):
                h, c, n, m = carry
                pre = xpt + h @ R.T
                i_pre, f_pre, z_pre, o_pre = jnp.split(pre, 4, axis=-1)
                m_new = jnp.maximum(f_pre + m, i_pre)
                i_g = jnp.exp(i_pre - m_new)
                f_g = jnp.exp(f_pre + m - m_new)
                c_new = f_g * c + i_g * jnp.tanh(z_pre)
                n_new = f_g * n + i_g
                h_new = jax.nn.sigmoid(o_pre) * (c_new / n_new)
                return ((h_new, c_new, n_new, m_new), h_new)
            _, hs = jax.lax.scan(step, (zeros, zeros, zeros, zeros), xp)
            return jnp.swapaxes(hs, 0, 1)

        def _layernorm(x, g, bta):
            mu = jnp.mean(x, axis=-1, keepdims=True)
            var = jnp.var(x, axis=-1, keepdims=True)
            return (x - mu) * jax.lax.rsqrt(var + EPS) * g + bta
        key = jax.random.key(seed)
        ks = jax.random.split(key, 1 + NBLOCKS * 4)
        inp = {'input_seq': jax.random.normal(ks[0], (B, S, D), jnp.float32)}
        for i in range(NBLOCKS):
            din = D
            k = ks[1 + 4 * i:1 + 4 * (i + 1)]
            inp[f'W{i}'] = _xavier(k[0], (4 * H, din))
            inp[f'R{i}'] = _xavier(k[1], (4 * H, H))
            inp[f'b{i}'] = jnp.zeros((4 * H,), jnp.float32)
            inp[f'projW{i}'] = _xavier(k[2], (din, H))
            inp[f'projb{i}'] = jnp.zeros((din,), jnp.float32)
            inp[f'gamma{i}'] = jnp.ones((din,), jnp.float32)
            inp[f'beta{i}'] = jnp.zeros((din,), jnp.float32)
        return inp
    _L1_attn_all = _L1_attn_setup()
    _L1_attn_in = {k: v for k, v in _L1_attn_all.items() if k in ('W0', 'R0', 'b0', 'projW0', 'projb0', 'gamma0', 'beta0', 'W1', 'R1', 'b1', 'projW1', 'projb1', 'gamma1', 'beta1')}
    del _L1_attn_all

    def _L1_xattn_setup():
        import jax, jax.numpy as jnp
        import numpy as np
        MASK_FILL = -99999.0
        key = jax.random.key(seed)
        k1, k2, k3, k4, k5, k6, k7 = jax.random.split(key, 7)
        B, S, H = (8, 256, 128)
        query = jax.random.normal(k1, (B, S, H), dtype=jnp.float32)
        key_t = jax.random.normal(k2, (B, S, H), dtype=jnp.float32)
        value = jax.random.normal(k3, (B, S, H), dtype=jnp.float32)
        mask = jax.random.randint(k4, (B, S), 0, 2, dtype=jnp.int32)
        s = 1.0 / np.sqrt(H)
        Wq = jax.random.uniform(k5, (H, H), dtype=jnp.float32, minval=-s, maxval=s)
        Wk = jax.random.uniform(k6, (H, H), dtype=jnp.float32, minval=-s, maxval=s)
        Wv = jax.random.uniform(k7, (H, H), dtype=jnp.float32, minval=-s, maxval=s)
        return {'query': query, 'key': key_t, 'value': value, 'Wq': Wq, 'Wk': Wk, 'Wv': Wv, 'mask': mask}
    _L1_xattn_all = _L1_xattn_setup()
    _L1_xattn_in = {k: v for k, v in _L1_xattn_all.items() if k in ('Wq', 'Wk', 'Wv')}
    del _L1_xattn_all

    def _L1_ffn_setup():
        import jax, jax.numpy as jnp
        import numpy as np
        key = jax.random.key(seed)
        k0, k1, k2, k3 = jax.random.split(key, 4)
        B, S, D, F, E = (8, 256, 128, 256, 8)
        x = jax.random.normal(k0, (B, S, D), dtype=jnp.float32)
        Wg = jax.random.normal(k1, (D, E), dtype=jnp.float32) * 0.02
        W1 = jax.random.normal(k2, (E, D, F), dtype=jnp.float32) * 0.02
        W2 = jax.random.normal(k3, (E, F, D), dtype=jnp.float32) * 0.02
        return {'x': x, 'Wg': Wg, 'W1': W1, 'W2': W2}
    _L1_ffn_all = _L1_ffn_setup()
    _L1_ffn_in = {k: v for k, v in _L1_ffn_all.items() if k in ('Wg', 'W1', 'W2')}
    del _L1_ffn_all
    return {'x': x, 'ctx_1024': ctx_1024, 'mask_BxS2_bf0': mask_BxS2_bf0, 'mask_BxS2_ik1': mask_BxS2_ik1, 'L0_attn_norm_w': _L0_attn_in['norm_w'], 'L0_attn_skip_w': _L0_attn_in['skip_w'], 'L0_attn_in_w': _L0_attn_in['in_w'], 'L0_attn_conv_w': _L0_attn_in['conv_w'], 'L0_attn_conv_b': _L0_attn_in['conv_b'], 'L0_attn_wd1': _L0_attn_in['wd1'], 'L0_attn_wd2': _L0_attn_in['wd2'], 'L0_attn_wd2_b': _L0_attn_in['wd2_b'], 'L0_attn_wb': _L0_attn_in['wb'], 'L0_attn_wc': _L0_attn_in['wc'], 'L0_attn_A_log': _L0_attn_in['A_log'], 'L0_attn_W_D': _L0_attn_in['W_D'], 'L0_attn_out_w': _L0_attn_in['out_w'], 'L0_xattn_Wq': _L0_xattn_in['Wq'], 'L0_xattn_bq': _L0_xattn_in['bq'], 'L0_xattn_Wk': _L0_xattn_in['Wk'], 'L0_xattn_bk': _L0_xattn_in['bk'], 'L0_xattn_Wv': _L0_xattn_in['Wv'], 'L0_xattn_bv': _L0_xattn_in['bv'], 'L0_xattn_Wo': _L0_xattn_in['Wo'], 'L0_xattn_bo': _L0_xattn_in['bo'], 'L0_xattn_rel_bias': _L0_xattn_in['rel_bias'], 'L0_ffn_gate_w': _L0_ffn_in['gate_w'], 'L0_ffn_gate_b': _L0_ffn_in['gate_b'], 'L0_ffn_w1': _L0_ffn_in['w1'], 'L0_ffn_b1': _L0_ffn_in['b1'], 'L0_ffn_w2': _L0_ffn_in['w2'], 'L0_ffn_b2': _L0_ffn_in['b2'], 'L1_attn_W0': _L1_attn_in['W0'], 'L1_attn_R0': _L1_attn_in['R0'], 'L1_attn_b0': _L1_attn_in['b0'], 'L1_attn_projW0': _L1_attn_in['projW0'], 'L1_attn_projb0': _L1_attn_in['projb0'], 'L1_attn_gamma0': _L1_attn_in['gamma0'], 'L1_attn_beta0': _L1_attn_in['beta0'], 'L1_attn_W1': _L1_attn_in['W1'], 'L1_attn_R1': _L1_attn_in['R1'], 'L1_attn_b1': _L1_attn_in['b1'], 'L1_attn_projW1': _L1_attn_in['projW1'], 'L1_attn_projb1': _L1_attn_in['projb1'], 'L1_attn_gamma1': _L1_attn_in['gamma1'], 'L1_attn_beta1': _L1_attn_in['beta1'], 'L1_xattn_Wq': _L1_xattn_in['Wq'], 'L1_xattn_Wk': _L1_xattn_in['Wk'], 'L1_xattn_Wv': _L1_xattn_in['Wv'], 'L1_ffn_Wg': _L1_ffn_in['Wg'], 'L1_ffn_W1': _L1_ffn_in['W1'], 'L1_ffn_W2': _L1_ffn_in['W2']}

def reference(x, ctx_1024, mask_BxS2_bf0, mask_BxS2_ik1, L0_attn_norm_w, L0_attn_skip_w, L0_attn_in_w, L0_attn_conv_w, L0_attn_conv_b, L0_attn_wd1, L0_attn_wd2, L0_attn_wd2_b, L0_attn_wb, L0_attn_wc, L0_attn_A_log, L0_attn_W_D, L0_attn_out_w, L0_xattn_Wq, L0_xattn_bq, L0_xattn_Wk, L0_xattn_bk, L0_xattn_Wv, L0_xattn_bv, L0_xattn_Wo, L0_xattn_bo, L0_xattn_rel_bias, L0_ffn_gate_w, L0_ffn_gate_b, L0_ffn_w1, L0_ffn_b1, L0_ffn_w2, L0_ffn_b2, L1_attn_W0, L1_attn_R0, L1_attn_b0, L1_attn_projW0, L1_attn_projb0, L1_attn_gamma0, L1_attn_beta0, L1_attn_W1, L1_attn_R1, L1_attn_b1, L1_attn_projW1, L1_attn_projb1, L1_attn_gamma1, L1_attn_beta1, L1_xattn_Wq, L1_xattn_Wk, L1_xattn_Wv, L1_ffn_Wg, L1_ffn_W1, L1_ffn_W2):
    import jax
    import jax.numpy as jnp

    def _L0_attn_ref(resid, norm_w, skip_w, in_w, conv_w, conv_b, wd1, wd2, wd2_b, wb, wc, A_log, W_D, out_w):
        import jax, jax.numpy as jnp
        import numpy as np
        from jax import lax
        B, L, D = (2, 256, 128)
        E, N, D_DELTA, D_CONV = (256, 16, 64, 4)
        EPS = 1e-05
        Bt, Lt, Dt = resid.shape
        x = resid * lax.rsqrt(jnp.mean(resid * resid, -1, keepdims=True) + EPS) * norm_w
        skip = x @ skip_w.T
        xe = x @ in_w.T
        xt = xe.transpose(0, 2, 1)
        xc = lax.conv_general_dilated(xt, conv_w, window_strides=(1,), padding=[(D_CONV - 1, 0)], feature_group_count=conv_w.shape[0])
        xc = xc + conv_b[None, :, None]
        xs = jax.nn.silu(xc.transpose(0, 2, 1))
        delta = jax.nn.softplus(xs @ wd1.T @ wd2.T + wd2_b)
        A = -jnp.exp(A_log)
        Bm = xs @ wb.T
        Cm = xs @ wc.T

        def step(h, inp):
            d_l, b_l, c_l, x_l = inp
            h = jnp.exp(d_l[:, :, None] * A) * h + (d_l * x_l)[:, :, None] * b_l[:, None, :]
            y_l = jnp.einsum('ben,bn->be', h, c_l)
            return (h, y_l)
        h0 = jnp.zeros((Bt, xs.shape[-1], A.shape[-1]), xs.dtype)
        _, ys = lax.scan(step, h0, (delta.transpose(1, 0, 2), Bm.transpose(1, 0, 2), Cm.transpose(1, 0, 2), xs.transpose(1, 0, 2)))
        y = ys.transpose(1, 0, 2)
        y = y + xs * W_D
        y = y * jax.nn.silu(skip)
        y = y @ out_w.T
        return resid + y

    def _L0_xattn_ref(query, key, value, key_padding_mask, Wq, bq, Wk, bk, Wv, bv, Wo, bo, rel_bias):
        import jax, jax.numpy as jnp
        import numpy as np
        import math
        D_MODEL = 128
        NUM_HEADS = 16
        D_K = D_MODEL // NUM_HEADS
        MAX_REL = 64
        B, L = (2, 256)
        Bsz, S, _ = query.shape
        Q = (query @ Wq + bq).reshape(Bsz, S, NUM_HEADS, D_K)
        K = (key @ Wk + bk).reshape(Bsz, S, NUM_HEADS, D_K)
        V = (value @ Wv + bv).reshape(Bsz, S, NUM_HEADS, D_K)
        scores = jnp.einsum('bqhd,bkhd->bhqk', Q, K) / math.sqrt(D_K)
        r = jnp.arange(S)
        rel_pos = jnp.clip(r[:, None] - r[None, :], -MAX_REL + 1, MAX_REL - 1) + MAX_REL - 1
        bias = rel_bias[:, rel_pos]
        scores = scores + bias[None]
        scores = jnp.where(key_padding_mask[:, None, None, :], -jnp.inf, scores)
        attn = jax.nn.softmax(scores, axis=-1)
        out = jnp.einsum('bhqk,bkhd->bqhd', attn, V).reshape(Bsz, S, D_MODEL)
        return out @ Wo + bo

    def _L0_ffn_ref(h, gate_w, gate_b, w1, b1, w2, b2):
        import math
        import jax, jax.numpy as jnp
        import numpy as np
        B, L, D, F_FF, E = (4, 256, 128, 512, 8)
        TOP_K = 1
        CAPACITY_FACTOR = 1.25
        Bh, Lh, Dh = h.shape
        T = Bh * Lh
        capacity = max(1, math.ceil(CAPACITY_FACTOR * (T * TOP_K / E)))
        x = h.reshape(T, Dh)
        logits = x @ gate_w.T + gate_b
        probs = jax.nn.softmax(logits, axis=-1)
        idx = jnp.argmax(probs, axis=-1)
        top_prob = jnp.max(probs, axis=-1)
        one_hot = jax.nn.one_hot(idx, E, dtype=jnp.int32)
        pos = jnp.take_along_axis(jnp.cumsum(one_hot, axis=0), idx[:, None], axis=1)[:, 0] - 1
        keep = pos < capacity
        safe_pos = jnp.where(keep, pos, 0)
        buf = jnp.zeros((E, capacity, Dh), dtype=x.dtype)
        buf = buf.at[idx, safe_pos].add(x * keep[:, None].astype(x.dtype))
        hdn = jax.nn.relu(jnp.einsum('ecd,edf->ecf', buf, w1) + b1[:, None, :])
        eout = jnp.einsum('ecf,efd->ecd', hdn, w2) + b2[:, None, :]
        gathered = eout[idx, safe_pos]
        out = gathered * (top_prob * keep.astype(x.dtype))[:, None]
        return out.reshape(Bh, Lh, Dh)

    def _L1_attn_ref(input_seq, W0, R0, b0, projW0, projb0, gamma0, beta0, W1, R1, b1, projW1, projb1, gamma1, beta1):
        import jax, jax.numpy as jnp
        import numpy as np
        B, S, D, H = (8, 128, 128, 128)
        NBLOCKS = 2
        EPS = 1e-05

        def _xavier(key, shape):
            fan_out, fan_in = shape
            lim = float(np.sqrt(6.0 / (fan_in + fan_out)))
            return jax.random.uniform(key, shape, jnp.float32, -lim, lim)

        def _slstm(x, W, R, b):
            Hh = R.shape[1]
            Bn = x.shape[0]
            xp = jnp.swapaxes(jnp.einsum('bsd,gd->bsg', x, W) + b, 0, 1)
            zeros = jnp.zeros((Bn, Hh), x.dtype)

            def step(carry, xpt):
                h, c, n, m = carry
                pre = xpt + h @ R.T
                i_pre, f_pre, z_pre, o_pre = jnp.split(pre, 4, axis=-1)
                m_new = jnp.maximum(f_pre + m, i_pre)
                i_g = jnp.exp(i_pre - m_new)
                f_g = jnp.exp(f_pre + m - m_new)
                c_new = f_g * c + i_g * jnp.tanh(z_pre)
                n_new = f_g * n + i_g
                h_new = jax.nn.sigmoid(o_pre) * (c_new / n_new)
                return ((h_new, c_new, n_new, m_new), h_new)
            _, hs = jax.lax.scan(step, (zeros, zeros, zeros, zeros), xp)
            return jnp.swapaxes(hs, 0, 1)

        def _layernorm(x, g, bta):
            mu = jnp.mean(x, axis=-1, keepdims=True)
            var = jnp.var(x, axis=-1, keepdims=True)
            return (x - mu) * jax.lax.rsqrt(var + EPS) * g + bta
        x = input_seq
        for W, R, b, pW, pb, g, bt in ((W0, R0, b0, projW0, projb0, gamma0, beta0), (W1, R1, b1, projW1, projb1, gamma1, beta1)):
            hseq = _slstm(x, W, R, b)
            y = jax.nn.gelu(hseq @ pW.T + pb, approximate=False)
            x = _layernorm(y + x, g, bt)
        return x

    def _L1_xattn_ref(query, key, value, Wq, Wk, Wv, mask):
        import jax, jax.numpy as jnp
        import numpy as np
        MASK_FILL = -99999.0
        q = jnp.einsum('bsh,oh->bso', query, Wq)
        k = jnp.einsum('bsh,oh->bso', key, Wk)
        v = jnp.einsum('bsh,oh->bso', value, Wv)
        score = jnp.einsum('bqh,bkh->bqk', q, k)
        m = mask[:, None, :]
        score = jnp.where(m == 0, jnp.float32(MASK_FILL), score)
        attn = jax.nn.softmax(score, axis=-1)
        context = jnp.einsum('bqk,bkh->bqh', attn, v)
        return context

    def _L1_ffn_ref(x, Wg, W1, W2):
        import jax, jax.numpy as jnp
        import numpy as np
        B, S, D = x.shape
        E = Wg.shape[1]
        T = B * S
        cap = max(1, T // E)
        xt = x.reshape(T, D)
        logits = xt @ Wg
        probs = jax.nn.softmax(logits, axis=-1)
        pT = probs.T
        _, top_idx = jax.lax.top_k(pT, cap)
        sel = jnp.zeros((E, T), dtype=bool).at[jnp.arange(E)[:, None], top_idx].set(True)
        masked = jnp.where(sel, pT, -jnp.inf)
        assigned = sel.any(axis=0)
        tok2exp = jnp.where(assigned, jnp.argmax(masked, axis=0), jnp.argmax(pT, axis=0))
        weights = jnp.take_along_axis(probs, tok2exp[:, None], axis=1)[:, 0]
        out = jnp.zeros_like(xt)
        for e in range(E):
            gate = jnp.where(tok2exp == e, weights, 0.0)
            h = jax.nn.gelu(xt @ W1[e], approximate=False) @ W2[e]
            out = out + gate[:, None] * h
        return out.reshape(B, S, D)
    x = x + _L0_attn_ref(_layernorm(x, axis=-1), L0_attn_norm_w, L0_attn_skip_w, L0_attn_in_w, L0_attn_conv_w, L0_attn_conv_b, L0_attn_wd1, L0_attn_wd2, L0_attn_wd2_b, L0_attn_wb, L0_attn_wc, L0_attn_A_log, L0_attn_W_D, L0_attn_out_w)
    x = x + _L0_xattn_ref(_layernorm(x, axis=-1), ctx_1024, ctx_1024, mask_BxS2_bf0, L0_xattn_Wq, L0_xattn_bq, L0_xattn_Wk, L0_xattn_bk, L0_xattn_Wv, L0_xattn_bv, L0_xattn_Wo, L0_xattn_bo, L0_xattn_rel_bias)
    x = x + _L0_ffn_ref(_layernorm(x, axis=-1), L0_ffn_gate_w, L0_ffn_gate_b, L0_ffn_w1, L0_ffn_b1, L0_ffn_w2, L0_ffn_b2)
    x = x + _L1_attn_ref(_layernorm(x, axis=-1), L1_attn_W0, L1_attn_R0, L1_attn_b0, L1_attn_projW0, L1_attn_projb0, L1_attn_gamma0, L1_attn_beta0, L1_attn_W1, L1_attn_R1, L1_attn_b1, L1_attn_projW1, L1_attn_projb1, L1_attn_gamma1, L1_attn_beta1)
    x = x + _L1_xattn_ref(_layernorm(x, axis=-1), ctx_1024, ctx_1024, L1_xattn_Wq, L1_xattn_Wk, L1_xattn_Wv, mask_BxS2_ik1)
    x = x + _L1_ffn_ref(_layernorm(x, axis=-1), L1_ffn_Wg, L1_ffn_W1, L1_ffn_W2)
    return x

_drawn_inputs = setup_inputs


def setup_inputs(seed=0):
    import zlib

    import numpy as np

    out = dict(_drawn_inputs(seed))
    spreads = {'L0_attn_norm_w': (1.0, 0.2),
     'L0_attn_conv_b': (0.0, 0.1),
     'L0_attn_wd2_b': (0.0, 0.553),
     'L0_attn_W_D': (1.0, 0.2),
     'L0_xattn_bq': (0.0, 0.613),
     'L0_xattn_bk': (0.0, 0.8),
     'L0_xattn_bv': (0.0, 0.1),
     'L0_xattn_bo': (0.0, 0.1),
     'L0_ffn_gate_b': (0.0, 0.8),
     'L0_ffn_b1': (0.0, 0.8),
     'L0_ffn_b2': (0.0, 0.8),
     'L1_attn_b0': (0.0, 0.8),
     'L1_attn_projb0': (0.0, 0.451),
     'L1_attn_gamma0': (1.0, 0.2),
     'L1_attn_beta0': (0.0, 0.274),
     'L1_attn_b1': (0.0, 0.8),
     'L1_attn_projb1': (0.0, 0.462),
     'L1_attn_gamma1': (1.0, 0.2),
     'L1_attn_beta1': (0.0, 0.1)}
    factors = {'L0_xattn_rel_bias': 8.0,
     'L0_ffn_gate_w': 6.605,
     'L0_ffn_w1': 8.0,
     'L0_ffn_w2': 8.0,
     'L1_attn_R0': 8.0,
     'L1_attn_R1': 8.0,
     'L1_ffn_Wg': 8.0,
     'L1_ffn_W1': 8.0,
     'L1_ffn_W2': 8.0}
    for name, (base, spread) in spreads.items():
        noise = np.random.default_rng([zlib.crc32(name.encode()), seed]).standard_normal(out[name].shape)
        drawn = base * np.exp(spread * noise) if base else spread * noise
        out[name] = jnp.asarray(drawn.astype(out[name].dtype))
    for name, factor in factors.items():
        out[name] = (out[name] * factor).astype(out[name].dtype)
    return out
```

```python
from contextlib import ExitStack

import numpy as np

import concourse.bass as bass
from concourse import mybir

ALU = mybir.AluOpType
ACT = mybir.ActivationFunctionType
F32 = mybir.dt.float32
BF16 = mybir.dt.bfloat16
I32 = mybir.dt.int32
U32 = mybir.dt.uint32
AX_X = mybir.AxisListType.X

P = 128
B, S, D = 64, 64, 128
T = B * S
NT = T // P
CH = 512
NC = T // CH
TPC = CH // P
BPC = CH // S
E0 = 256
NS = 16
DD = 64
KC = 4
EPS = 1e-5
BIG = 1.0e30



class Core:
    pass


class Chain:

    def __init__(self, eng, sem):
        self.eng, self.sem, self.n = eng, sem, 0
        self.i, self.per = None, 0

    def enter(self, i, per):
        self.i, self.per, self.base, self.n = i, per, self.n, 0

    def leave(self, times):
        assert self.n == self.per, (self.n, self.per)
        self.n, self.i = self.base + times * self.per, None

    def value(self):
        return self.n if self.i is None else self.i * self.per + (self.base + self.n)

    def inc(self, ins):
        ins.then_inc(self.sem, 1)
        self.n += 1

    def link(self, ins):
        self.inc(ins)
        self.eng.wait_ge(self.sem, self.value())


def alone(eng):
    eng.nop(nofuse=True)


def sem_maker(nc, ctx, tag):
    made = []

    def clear():
        for s in made:
            nc.sync.sem_clear(s)
        nc.all_engine_barrier()

    ctx.callback(clear)

    def make(name):
        made.append(ctx.enter_context(nc.semaphore(f"{tag}_{name}")))
        return made[-1]

    return make


def norm_stage(nc, g, tag, rms=False, gain=None, keep=False, place=None):
    with ExitStack() as ctx:
        sem = sem_maker(nc, ctx, tag)
        sb = lambda name, shape, dt=F32: ctx.enter_context(nc.sbuf_tensor(f"{tag}_{name}", shape, dt))
        stat, vchain, var_ready, rstd_ready = sem("stat"), sem("vchain"), sem("var_ready"), sem("rstd_ready")
        rows_ready, turned, evac = sem("rows_ready"), sem("turned"), sem("evac")
        st = sb("st", [P, NT, 6])
        a, b, mean, var, rstd, rr = (sb(n, [P, NT]) for n in ("a", "b", "mean", "var", "rstd", "rr"))
        xn = sb("xn", [P, 2, TPC, D])
        xnorm, xadd, kept = sem("xnorm"), sem("xadd"), sem("kept")
        turned_credit = evac
        row = lambda t, k, j: t[:, k, j:j + 1, :]
        with nc.Block() as block:

            @block.vector
            def _(ve):
                ch = Chain(ve, vchain)
                with ve.Fori(0, NT) as i:
                    ve.bn_stats(st[:, bass.ds(i, 1), :], g.X[:, bass.ds(i, 1), :]).then_inc(stat, 1)
                ve.wait_ge(stat, NT)
                ve.tensor_tensor(a[:], st[:, :, 1], st[:, :, 4], ALU.add).then_inc(vchain, 1)
                ve.tensor_tensor(b[:], st[:, :, 1], st[:, :, 4], ALU.subtract).then_inc(vchain, 1)
                ve.tensor_tensor(var[:], st[:, :, 2], st[:, :, 5], ALU.add).then_inc(vchain, 1)
                ch.n = 3
                ve.wait_ge(vchain, 3)
                ch.link(ve.scalar_tensor_tensor(b[:], b[:], 0.25, b[:], ALU.mult, ALU.mult))
                ch.link(ve.scalar_tensor_tensor(var[:], var[:], 1.0 / D, b[:], ALU.mult, ALU.add))
                ch.link(ve.tensor_scalar(mean[:], a[:], 0.5, None, ALU.mult))
                ve.tensor_scalar(a[:], var[:], EPS, None, ALU.add).then_inc(var_ready, 1)
                ve.wait_ge(rstd_ready, 1)
                if rms:
                    ch.link(ve.tensor_tensor(b[:], rstd[:], rstd[:], ALU.mult))
                    ch.link(ve.tensor_tensor(b[:], b[:], var[:], ALU.mult))
                    ve.tensor_scalar(b[:], b[:], EPS, None, ALU.add).then_inc(var_ready, 1)
                if rms:
                    ve.wait_ge(rstd_ready, 2)
                ve.sem_inc(xadd, 1)
                with ve.Fori(0, NC // 2) as pair:
                    c = pair * 2
                    for k in range(2):
                        ve.wait_ge(turned_credit, c + (k + 1))
                        for j in range(TPC):
                            i = c * TPC + (k * TPC + j)
                            ve.tensor_scalar(row(xn, k, j), g.X[:, bass.ds(i, 1), :], mean[:, bass.ds(i, 1)],
                                             rstd[:, bass.ds(i, 1)], ALU.subtract, ALU.mult).then_inc(xnorm if rms else rows_ready, 1)
                        if keep:
                            ve.wait_ge(rows_ready, c * TPC + TPC * (k + 1))
                            ve.tensor_copy(g.rows[:, bass.ds(c * TPC + k * TPC, TPC), :], xn[:, k]).then_inc(kept, 1)
                        if rms:
                            ve.wait_ge(xnorm, c * TPC + TPC * (k + 1))
                            xc = g.X[:, bass.ds(c * TPC + k * TPC, TPC), :]
                            ve.tensor_tensor(xc, xc, xn[:, k, :, :], ALU.add).then_inc(xadd, 1)
                            ve.wait_ge(xadd, c + (k + 2))
                            for j in range(TPC):
                                i = c * TPC + (k * TPC + j)
                                ve.tensor_scalar(row(xn, k, j), row(xn, k, j), rr[:, bass.ds(i, 1)],
                                                 None, ALU.mult).then_inc(rows_ready, 1)

            @block.gpsimd
            def _(pool):
                pool.wait_ge(var_ready, 1)
                pool.tensor_tensor(rstd[:], a[:], g.neghalf[:], ALU.pow).then_inc(rstd_ready, 1)
                if rms:
                    pool.wait_ge(var_ready, 2)
                    pool.tensor_tensor(rr[:], b[:], g.neghalf[:], ALU.pow).then_inc(rstd_ready, 1)

            @block.tensor
            def _(pe):
                with pe.Fori(0, NC // 2) as pair:
                    c = pair * 2
                    for k in range(2):
                        pe.wait_ge(rows_ready, c * TPC + TPC * (k + 1))
                        pe.wait_ge(evac, c + (k + 1))
                        for j in range(TPC):
                            ins = pe.transpose(g.bank[k][:, j * P:(j + 1) * P],
                                               xn[:, k, j, :], g.ident[:])
                        ins.then_inc(turned, 1)

            @block.scalar
            def _(act):
                act.sem_inc(evac, 2)
                with act.Fori(0, NC // 2) as pair:
                    c = pair * 2
                    for k in range(2):
                        act.wait_ge(turned, c + (k + 1))
                        out = place(c + k) if place else g.xT[:, bass.ts(c + k, CH)]
                        src = g.bank[k] if place is None else g.bank[k].rearrange("p (b s) -> p b s", s=S)
                        act.activation(out, src, ACT.Identity, scale=gain if gain is not None else 1.0).then_inc(evac, 1)


def scan_stage(nc, g):
    H = E0 // P
    tag = "scan"
    norm_stage(nc, g, "n0", rms=True, gain=g.w("norm_w"))
    with ExitStack() as ctx:
        sem = sem_maker(nc, ctx, tag)
        sb = lambda name, shape, dt=F32: ctx.enter_context(nc.sbuf_tensor(f"{tag}_{name}", shape, dt))
        xs = sb("xs", [P, H, T])
        delta = sb("delta", [P, H, T])
        parts = sb("parts", [P, T], BF16)
        sel = sb("sel", [P, 2 * NS, P], BF16)
        negA = sb("negA", [P, H * NS])
        sel_in = sem("sel_in")

        with ExitStack() as c2:
            sem2 = sem_maker(nc, c2, "proj")
            wk = c2.enter_context(nc.sbuf_tensor("proj_wk", [P, KC, E0], F32))
            scaled, conv, silu, vch = sem2("scaled"), sem2("conv"), sem2("silu"), sem2("vch")
            exped, negd = sem2("exped"), sem2("negd")
            with nc.Block() as block:

                @block.sync
                def _(sp):
                    sp.dma_start(sel[:], g.sel_dram).then_inc(sel_in, 16)

                @block.vector
                def _(ve):
                    for k in range(KC):
                        ve.tensor_tensor(wk[:, k, :], g.w("inT"), g.w("convrow")[:, k * E0:(k + 1) * E0], ALU.mult).then_inc(scaled, 1)
                    ve.wait_ge(exped, 1)
                    ve.tensor_scalar(negA[:], negA[:], -1.0, None, ALU.mult).then_inc(negd, 1)
                    ve.wait_ge(sel_in, 16)

                @block.tensor
                def _(pe):
                    pe.wait_ge(scaled, KC)
                    with pe.Fori(0, NC) as c:
                        for h in range(H):
                            pe.wait_ge(silu, c * H + (h + 1))
                            for k in range(KC):
                                out = g.bank[h][:].rearrange("p (b s) -> p b s", s=S)[:, :, k:S]
                                src = g.xT[:, bass.ts(c, CH)].rearrange("p (b s) -> p b s", s=S)[:, :, 0:S - k]
                                ins = pe.matmul(out, wk[:, KC - 1 - k, h * P:(h + 1) * P], src,
                                                start=(k == 0), stop=(k == KC - 1), skip_group_check=True)
                            ins.then_inc(conv, 1)

                @block.scalar
                def _(act):
                    act.activation(negA[:], g.w("A_log"), ACT.Exp).then_inc(exped, 1)
                    act.sem_inc(silu, H)
                    with act.Fori(0, NC) as c:
                        for h in range(H):
                            act.wait_ge(conv, c * H + (h + 1))
                            act.activation(xs[:, h, bass.ts(c, CH)], g.bank[h][:], ACT.Silu,
                                           bias=g.w("conv_b")[:, h:h + 1]).then_inc(silu, 1)

        with ExitStack() as c2:
            sem2 = sem_maker(nc, c2, "dl")
            t1 = c2.enter_context(nc.sbuf_tensor("dl_t1", [DD, 2, CH], F32))
            xb = c2.enter_context(nc.sbuf_tensor("dl_xb", [P, H, CH], F32))
            lg = c2.enter_context(nc.sbuf_tensor("dl_lg", [P, H, CH], F32))
            res = c2.enter_context(nc.sbuf_tensor("dl_res", [P, CH], F32))
            d1, d1c, d2, bc, clampd, ex, ln_, dl, vch = (sem2(n) for n in ("d1", "d1c", "d2", "bc", "clampd", "ex", "ln", "dl", "vch"))
            with nc.Block() as block:

                @block.tensor
                def _(pe):
                    with pe.Fori(0, NC) as c:
                        pe.wait_ge(d1c, c + 1)
                        for h in range(H):
                            ins = pe.matmul(g.bank[0][0:DD, :], g.w("wd1T")[:, h * DD:(h + 1) * DD], xs[:, h, bass.ts(c, CH)],
                                            start=(h == 0), stop=(h == H - 1))
                        ins.then_inc(d1, 1)
                        pe.wait_ge(vch, c * 6 + 6)
                        for h in range(H):
                            ins = pe.matmul(g.bank[3][:], g.w("wbcT")[:, h * P:(h + 1) * P], xs[:, h, bass.ts(c, CH)],
                                            start=(h == 0), stop=(h == H - 1))
                        ins.then_inc(bc, 1)
                        pe.wait_ge(d1c, c + 2)
                        pe.wait_ge(dl, c + 1)
                        for h in range(H):
                            ins = pe.matmul(g.bank[1 + h][:], g.w("wd2T")[0:DD, h * P:(h + 1) * P], t1[:, 0, :], start=True, stop=True)
                        ins.then_inc(d2, 1)

                @block.scalar
                def _(act):
                    act.sem_inc(d1c, 1)
                    with act.Fori(0, NC) as c:
                        act.wait_ge(d1, c + 1)
                        act.wait_ge(d2, c)
                        act.activation(t1[:, 0, :], g.bank[0][0:DD, :], ACT.Copy).then_inc(d1c, 1)
                        act.wait_ge(clampd, c + 1)
                        act.activation(xb[:], xb[:], ACT.Exp).then_inc(ex, 1)
                        act.wait_ge(ex, c + 1)
                        act.activation(lg[:], xb[:], ACT.Ln, bias=1.0).then_inc(ln_, 1)

                @block.vector
                def _(ve):
                    ve.sem_inc(vch, 6)
                    ve.sem_inc(dl, 1)
                    with ve.Fori(0, NC) as c:
                        ve.wait_ge(bc, c + 1)
                        cs = bass.ts(c, CH)
                        steps = (
                            lambda: ve.tensor_copy(parts[:, cs], g.bank[3][:]),
                            lambda: ve.tensor_tensor(res[:], g.bank[3][:], parts[:, cs], ALU.subtract),
                            lambda: ve.tensor_copy(parts[64:128, cs], res[64:128, :]),
                            lambda: ve.tensor_tensor(res[96:128, :], res[96:128, :], parts[96:128, cs], ALU.subtract),
                            lambda: ve.tensor_copy(parts[96:128, cs], res[96:128, :]),
                        )
                        for k, f in enumerate(steps):
                            alone(ve)
                            f().then_inc(vch, 1)
                            ve.wait_ge(vch, c * 6 + (7 + k))
                        ve.wait_ge(d2, c + 1)
                        for h in range(H):
                            ins = ve.tensor_scalar(xb[:, h, :], g.bank[1 + h][:], g.w("wd2_b")[:, h:h + 1], 40.0, ALU.add, ALU.min)
                            if h == 0:
                                ins.then_inc(vch, 1)
                        ins.then_inc(clampd, 1)
                        ve.wait_ge(ln_, c + 1)
                        for h in range(H):
                            ins = ve.scalar_tensor_tensor(delta[:, h, cs], g.bank[1 + h][:], g.w("wd2_b")[:, h:h + 1],
                                                          lg[:, h, :], ALU.add, ALU.max)
                        ins.then_inc(dl, 1)

        with ExitStack() as c2:
            sem2 = sem_maker(nc, c2, "rec")
            sb2 = lambda name, shape, dt=F32: c2.enter_context(nc.sbuf_tensor(f"rec_{name}", shape, dt))
            dx = sb2("dx", [P, 2, H * CH])
            dec = sb2("dec", [P, 2, H * CH])
            u = sb2("u", [P, 2, H * CH])
            hst = sb2("hst", [P, 2, H * CH])
            hc = sb2("hc", [P, 2, H * CH])
            cb = sb2("cb", [P, 2, CH])
            bready, cready, decay, ccopy, uready, hready, hcready, summed, dxr, reset, yout = (
                sem2(n) for n in ("bready", "cready", "decay", "ccopy", "uready", "hready", "hcready", "summed", "dxr", "reset", "yout"))
            with nc.Block() as block:

                @block.tensor
                def _(pe):
                    with pe.Fori(0, NC) as c:
                        def broadcasts(n):
                            q = n % 2
                            cs = bass.ts(c, CH)
                            if n >= 2:
                                pe.wait_ge(uready, c * NS + (n - 1))
                                pe.wait_ge(ccopy, c * NS + (n - 1))
                            else:
                                pe.wait_ge(uready, c * NS)
                                pe.wait_ge(ccopy, c * NS)
                            pe.matmul(g.bank[q][:], sel[:, n, :], parts[:, cs], start=True, stop=True).then_inc(bready, 1)
                            pe.matmul(g.bank[2 + q][:], sel[:, NS + n, :], parts[:, cs], start=True, stop=True).then_inc(cready, 1)

                        broadcasts(0)
                        broadcasts(1)
                        pe.wait_ge(yout, c)
                        for n in range(NS):
                            if n + 2 < NS:
                                broadcasts(n + 2)
                            pe.wait_ge(hcready, c * NS + (n + 1))
                            for h in range(H):
                                ins = pe.matmul(g.bank[4 + h][:], g.ident[:], hc[:, n % 2, h * CH:(h + 1) * CH],
                                                start=(n == 0), stop=(n == NS - 1))
                            ins.then_inc(summed, 1)

                @block.scalar
                def _(act):
                    with act.Fori(0, NC) as c:
                        act.wait_ge(reset, c + 1)
                        for n in range(NS):
                            k = c * NS + n
                            act.wait_ge(hready, c * NS + max(n - 1, 0))
                            alone(act)
                            for h in range(H):
                                ins = act.activation(dec[:, n % 2, h * CH:(h + 1) * CH], delta[:, h, bass.ts(c, CH)],
                                                     ACT.Exp, scale=negA[:, h * NS + n:h * NS + n + 1])
                            ins.then_inc(decay, 1)
                            act.wait_ge(cready, c * NS + (n + 1))
                            act.wait_ge(hcready, c * NS + max(n - 1, 0))
                            act.activation(cb[:, n % 2, :], g.bank[2 + n % 2][:], ACT.Copy).then_inc(ccopy, 1)

                @block.vector
                def _(ve):
                    with ve.Fori(0, NC // 2) as pair:
                        c0 = pair * 2
                        for cc in range(2):
                            c = c0 + cc
                            ve.wait_ge(dxr, c + 1)
                            def form_u(n):
                                ve.wait_ge(bready, c * NS + (n + 1))
                                ve.wait_ge(hready, c * NS + max(n - 1, 0))
                                ve.tensor_tensor(u[:, n % 2, :].rearrange("p (h t) -> p h t", h=H),
                                                 dx[:, cc, :].rearrange("p (h t) -> p h t", h=H),
                                                 g.bank[n % 2][:].rearrange("p (o t) -> p o t", o=1).broadcast_to([P, H, CH]),
                                                 ALU.mult).then_inc(uready, 1)
                            form_u(0)
                            for n in range(NS):
                                if n + 1 < NS:
                                    form_u(n + 1)
                                ve.wait_ge(decay, c * NS + (n + 1))
                                ve.wait_ge(uready, c * NS + (n + 1))
                                ve.wait_ge(hcready, c * NS + max(n - 1, 0))
                                ve.tensor_tensor_scan(hst[:, n % 2, :], dec[:, n % 2, :], u[:, n % 2, :], 0.0,
                                                      ALU.mult, ALU.add).then_inc(hready, 1)
                            ve.wait_ge(summed, c * NS + NS)
                            for h in range(H):
                                ins = ve.scalar_tensor_tensor(xs[:, h, bass.ts(c, CH)], xs[:, h, bass.ts(c, CH)],
                                                              g.w("W_D")[:, h:h + 1], g.bank[4 + h][:], ALU.mult, ALU.add)
                            ins.then_inc(yout, 1)

                @block.gpsimd
                def _(pool):
                    def prepare(c, q):
                        for h in range(H):
                            ins = pool.tensor_tensor(dx[:, q, h * CH:(h + 1) * CH], delta[:, h, bass.ts(c, CH)],
                                                     xs[:, h, bass.ts(c, CH)], ALU.mult)
                        ins.then_inc(dxr, 1)

                    with pool.Fori(0, NC // 2) as pair:
                        c0 = pair * 2
                        for cc in range(2):
                            c = c0 + cc
                            prepare(c, cc)
                            pool.wait_ge(dxr, c + 1)
                            alone(pool)
                            pool.tensor_copy(delta[:, :, bass.ts(c, CH)].rearrange("p h (b s) -> p h b s", s=S)[:, :, :, 0],
                                             g.w("big")[:, 0:H * BPC].rearrange("p (h b) -> p h b", h=H)).then_inc(reset, 1)
                            for n in range(NS):
                                pool.wait_ge(hready, c * NS + (n + 1))
                                pool.wait_ge(ccopy, c * NS + (n + 1))
                                pool.wait_ge(summed, c * NS + max(n - 1, 0))
                                pool.tensor_tensor(hc[:, n % 2, :].rearrange("p (h t) -> p h t", h=H),
                                                   hst[:, n % 2, :].rearrange("p (h t) -> p h t", h=H),
                                                   cb[:, n % 2, :].rearrange("p (o t) -> p o t", o=1).broadcast_to([P, H, CH]),
                                                   ALU.mult).then_inc(hcready, 1)

        with ExitStack() as c2:
            sem2 = sem_maker(nc, c2, "go")
            gate = c2.enter_context(nc.sbuf_tensor("go_gate", [P, H, CH], F32))
            yg = c2.enter_context(nc.sbuf_tensor("go_yg", [P, H, CH], F32))
            skip, gated, mult, proj, added = (sem2(n) for n in ("skip", "gated", "mult", "proj", "added"))
            with nc.Block() as block:

                @block.tensor
                def _(pe):
                    with pe.Fori(0, NC) as c:
                        pe.wait_ge(gated, c * H)
                        for h in range(H):
                            pe.matmul(g.bank[h][:], g.w("skipT")[:, h * P:(h + 1) * P], g.xT[:, bass.ts(c, CH)],
                                      start=True, stop=True).then_inc(skip, 1)
                        pe.wait_ge(mult, c + 1)
                        pe.wait_ge(added, c)
                        for j in range(TPC):
                            for h in range(H):
                                ins = pe.matmul(g.bank[2][:, j * P:(j + 1) * P], yg[:, h, j * P:(j + 1) * P],
                                                g.w("outT")[:, h * D:(h + 1) * D], start=(h == 0), stop=(h == H - 1))
                        ins.then_inc(proj, 1)

                @block.scalar
                def _(act):
                    with act.Fori(0, NC) as c:
                        act.wait_ge(mult, c)
                        for h in range(H):
                            act.wait_ge(skip, c * H + (h + 1))
                            act.activation(gate[:, h, :], g.bank[h][:], ACT.Silu).then_inc(gated, 1)

                @block.vector
                def _(ve):
                    with ve.Fori(0, NC) as c:
                        ve.wait_ge(gated, c * H + H)
                        ve.wait_ge(added, c)
                        ve.tensor_tensor(yg[:], xs[:, :, bass.ts(c, CH)], gate[:], ALU.mult).then_inc(mult, 1)
                        ve.wait_ge(proj, c + 1)
                        xc = g.X[:, bass.ts(c, TPC), :].rearrange("p a d -> p (a d)")
                        ve.tensor_tensor(xc, xc, g.bank[2][:], ALU.add).then_inc(added, 1)


NH, DK = 16, 8
HG = 4
NG = NH // HG
VW = 2 * (DK + 1)


def cross_stage(nc, g):
    norm_stage(nc, g, "n1")
    with ExitStack() as ctx:
        sem = sem_maker(nc, ctx, "ca")
        sb = lambda name, shape, dt=F32: ctx.enter_context(nc.sbuf_tensor(f"ca_{name}", shape, dt))
        R = 2
        qg = sb("qg", [P, R, NG, CH])
        kd = sb("kd", [P, R, BPC, HG, S])
        vT = sb("vT", [P, R, BPC, 2, S])
        vd = sb("vd", [P, R, BPC, NH // 2, VW])
        bias = sb("bias", [P, NH, S])
        mask8 = sb("mask8", [2, T // 8], I32)
        maskneg = sb("maskneg", [2, NT, S], BF16)
        kbias = sb("kbias", [P, HG])
        qbias = sb("qbias", [P, 1])
        sc = sb("sc", [P, 2, NH, S])
        pr = sb("pr", [P, 2, NH * S])
        mx = sb("mx", [P, 2, NH])
        pT = sb("pT", [P, 2, NH // 2, P])
        ri = sb("ri", [P, 2, NH])
        o = sb("o", [P, 2, D])
        oT = sb("oT", [P, 2, D])
        bias_in, init, kb = sem("bias_in"), sem("init"), sem("kb")
        with nc.Block() as block:

            @block.sync
            def _(sp):
                sp.dma_start(bias[:], g.bias_dram).then_inc(bias_in, 16)
                sp.dma_start(mask8[:], g.mask8_dram).then_inc(bias_in, 16)
                sp.wait_ge(bias_in, 32)

            @block.gpsimd
            def _(pool):
                pool.memset(qg[:], 0.0).then_inc(init, 1)
                pool.memset(vd[:], 0.0).then_inc(init, 1)
                pool.wait_ge(init, 2)
                for h2 in range(2):
                    col = h2 * (DK + 1) + DK
                    pool.memset(vd[h2 * S:(h2 + 1) * S, :, :, :, col:col + 1].rearrange("p r b j o -> p (r b j) o"), 1.0).then_inc(init, 1)

            @block.vector
            def _(ve):
                ve.tensor_scalar(qbias[:], g.w("bq"), DK ** -0.5, None, ALU.mult).then_inc(kb, 1)
                ve.tensor_scalar(kbias[:], g.w("headrow"), g.w("bk"), None, ALU.mult).then_inc(kb, 1)
                ve.wait_ge(bias_in, 32)
                ve.tensor_scalar(maskneg[:], mask8[:].bitcast(mybir.dt.uint8).rearrange("a (n k) -> a n k", k=S), -1.0e30, None, ALU.mult).then_inc(kb, 1)

        proj, qkv, vt, vcopy = sem("proj"), sem("qkv"), sem("vt"), sem("vcopy")
        scored, biased, maxed, shifted, exped, turned, tcopy, pv, rinv, normed, oturned, ocopy, outp, added = (
            sem(n) for n in ("scored", "biased", "maxed", "shifted", "exped", "turned", "tcopy", "pv", "rinv", "normed",
                             "oturned", "ocopy", "outp", "added"))
        PPC = BPC // 2
        bank_s = [g.ps[:, 1:3, :], g.ps[:, 3:5, :]]
        bank_t = g.ps[:, 5:7, :]
        bank_o = g.bank[7]
        bank_f = g.bank[0]
        T_AT, F_AT = 0, P
        with nc.Block() as block:

            @block.tensor
            def _(pe):
                with pe.Fori(0, NC // R) as pair:
                    for r in range(R):
                        c = pair * R + r
                        cs = bass.ts(c, CH)
                        for k, (w, src) in enumerate((("Wq", g.xT), ("Wk", g.ctxT), ("Wv", g.ctxT))):
                            pe.wait_ge(qkv, c * 3 + (k + 1))
                            if k == 0:
                                pe.wait_ge(vcopy, c * 2)
                                pe.wait_ge(added, c * PPC)
                            pe.matmul(g.bank[0], g.w(w), src[:, cs], start=True, stop=True).then_inc(proj, 1)
                        pe.wait_ge(qkv, c * 3 + 4)
                        for q in range(2):
                            pe.wait_ge(vcopy, c * 2 + q)
                            for b in range(4):
                                ins = pe.transpose(g.bank[0][:, b * P:(b + 1) * P],
                                                   vT[:, r, q * 4 + b].rearrange("p o k -> p (o k)"), g.ident)
                            ins.then_inc(vt, 1)

                        def scores(p):
                            n = c * PPC + p
                            pe.wait_ge(biased, n * 1 + 1 - 0)
                            sbk = bank_s[p % 2]
                            for k in range(2):
                                m = maskneg[:, bass.ds(n, 1), :].broadcast_to([2, NH // 2, S])
                                pe.matmul(sbk[:, k, :], g.pairsel[:], m, start=True, stop=False, skip_group_check=True)
                            for b in range(2):
                                for gr in range(NG):
                                    q = qg[:, r, gr, (2 * p + b) * S:(2 * p + b + 1) * S]
                                    kk = kd[:, r, 2 * p + b, :, :]
                                    ins = pe.matmul(sbk[b * S:(b + 1) * S, gr // 2, gr % 2 * 256:gr % 2 * 256 + 256], q, kk,
                                                    start=False, stop=True, skip_group_check=True)
                            ins.then_inc(scored, 1)

                        def rest(p):
                            n = c * PPC + p
                            pe.wait_ge(exped, n + 1)
                            pe.wait_ge(tcopy, n)
                            for j in range(NH // 2):
                                ins = pe.transpose(bank_t[:, j // 4, j % 4 * P:(j % 4 + 1) * P], pr[:, p % 2, j * P:(j + 1) * P], g.ident)
                            ins.then_inc(turned, 1)
                            pe.wait_ge(tcopy, n + 1)
                            pe.wait_ge(normed, n)
                            if p == 0:
                                pe.wait_ge(vcopy, c * 2 + 2)
                            for b in range(2):
                                for j in range(NH // 2):
                                    ins = pe.matmul(bank_o[b * S:(b + 1) * S, j * VW:(j + 1) * VW],
                                                    pT[:, p % 2, j, b * S:(b + 1) * S], vd[:, r, 2 * p + b, j, :], start=True, stop=True)
                            ins.then_inc(pv, 1)

                        def output(p):
                            n = c * PPC + p
                            pe.wait_ge(normed, n + 1)
                            pe.wait_ge(added, n)
                            pe.transpose(bank_f[:, T_AT:T_AT + P], o[:, p % 2, :], g.ident).then_inc(oturned, 1)
                            pe.wait_ge(ocopy, n + 1)
                            pe.matmul(bank_f[:, F_AT:F_AT + D], oT[:, p % 2, :], g.w("Wo"), start=True, stop=False)
                            pe.matmul(bank_f[:, F_AT:F_AT + D], g.w("ones")[0:1, :], g.w("bo")[0:1, :], start=False, stop=True).then_inc(outp, 1)

                        scores(0)
                        for p in range(PPC):
                            if p + 1 < PPC:
                                scores(p + 1)
                            rest(p)
                            if p >= 1:
                                output(p - 1)
                        output(PPC - 1)

            @block.scalar
            def _(act):
                act.sem_inc(qkv, 1)
                with act.Fori(0, NC // R) as pair:
                    for r in range(R):
                        c = pair * R + r
                        act.wait_ge(proj, c * 3 + 1)
                        for gr in range(NG):
                            rows = slice(32 * gr, 32 * gr + 32)
                            ins = act.activation(qg[rows, r, gr, :], g.bank[0][rows, :], ACT.Identity,
                                                 bias=qbias[rows, :], scale=DK ** -0.5)
                        ins.then_inc(qkv, 1)
                        act.wait_ge(proj, c * 3 + 2)
                        for h in range(HG):
                            ins = act.activation(kd[:, r, :, h, :], g.bank[0].rearrange("p (b k) -> p b k", k=S), ACT.Identity,
                                                 bias=kbias[:, h:h + 1], scale=g.w("headrow")[:, h:h + 1])
                        ins.then_inc(qkv, 1)
                        act.wait_ge(proj, c * 3 + 3)
                        act.activation(vT[:, r], g.bank[0].rearrange("p (b o k) -> p b o k", o=1, k=S).broadcast_to([P, BPC, 2, S]), ACT.Identity, bias=g.w("bv")).then_inc(qkv, 1)
                        for q in range(2):
                            act.wait_ge(vt, c * 2 + (q + 1))
                            for h2 in range(2):
                                half = slice(h2 * S, (h2 + 1) * S)
                                src = g.bank[0][half, :].rearrange("p (b j t d) -> p b j t d", b=4, t=2, d=DK)[:, :, :, h2, :]
                                for b in range(4):
                                    ins = act.activation(vd[half, r, q * 4 + b, :, h2 * (DK + 1):h2 * (DK + 1) + DK], src[:, b], ACT.Copy)
                            ins.then_inc(vcopy, 1)

                        def output_copy(p):
                            act.wait_ge(oturned, c * PPC + (p + 1))
                            act.activation(oT[:, p % 2, :], bank_f[:, T_AT:T_AT + P], ACT.Copy).then_inc(ocopy, 1)

                        for p in range(PPC):
                            n = c * PPC + p
                            act.wait_ge(shifted, n + 1)
                            act.activation(pr[:, p % 2, :], sc[:, p % 2, :, :].rearrange("p h k -> p (h k)"), ACT.Exp).then_inc(exped, 1)
                            act.wait_ge(turned, n + 1)
                            act.activation(pT[:, p % 2, :, :].rearrange("p j q -> p (j q)"), bank_t.rearrange("p a b -> p (a b)"), ACT.Copy).then_inc(tcopy, 1)
                            if p >= 1:
                                output_copy(p - 1)
                        output_copy(PPC - 1)

            @block.vector
            def _(ve):
                ve.sem_inc(biased, 2)
                with ve.Fori(0, NC) as c:
                    def softmax(p):
                        n = c * PPC + p
                        q = p % 2
                        ve.wait_ge(scored, n + 1)
                        ve.tensor_tensor(sc[:, q].rearrange("p h k -> p (h k)"), bank_s[q].rearrange("p a b -> p (a b)"),
                                         bias[:].rearrange("p h k -> p (h k)"), ALU.add).then_inc(biased, 1)
                        ve.wait_ge(biased, n + 3)
                        ve.tensor_reduce(mx[:, q, :], sc[:, q], AX_X, ALU.max).then_inc(maxed, 1)
                        ve.wait_ge(maxed, n + 1)
                        ve.tensor_tensor(sc[:, q], sc[:, q], mx[:, q, :].rearrange("p (h o) -> p h o", o=1).broadcast_to([P, NH, S]),
                                         ALU.subtract).then_inc(shifted, 1)

                    def finish(p):
                        n = c * PPC + p
                        q = p % 2
                        ve.wait_ge(pv, n + 1)
                        res = bank_o[:, :NH // 2 * VW].rearrange("p (h w) -> p h w", w=DK + 1)
                        ve.reciprocal(ri[:, q, :], res[:, :, DK]).then_inc(rinv, 1)
                        ve.wait_ge(rinv, n + 1)
                        ve.tensor_tensor(o[:, q, :].rearrange("p (h d) -> p h d", d=DK), res[:, :, 0:DK],
                                         ri[:, q, :].rearrange("p (h o) -> p h o", o=1).broadcast_to([P, NH, DK]), ALU.mult).then_inc(normed, 1)

                    def add(p):
                        n = c * PPC + p
                        ve.wait_ge(outp, n + 1)
                        x = g.X[:, bass.ds(n, 1), :].rearrange("p a d -> p (a d)")
                        ve.tensor_tensor(x, x, bank_f[:, F_AT:F_AT + D], ALU.add).then_inc(added, 1)

                    softmax(0)
                    for p in range(PPC):
                        if p + 1 < PPC:
                            softmax(p + 1)
                        finish(p)
                        if p >= 1:
                            add(p - 1)
                    add(PPC - 1)


GATES = 4


def recurrence(nc, g, tag, layer, xin, hs):
    with ExitStack() as ctx:
        sem = sem_maker(nc, ctx, tag)
        sb = lambda name, shape, dt=F32: ctx.enter_context(nc.sbuf_tensor(f"{tag}_{name}", shape, dt))
        fm = sb("fm", [P, B])
        m = sb("m", [P, 2, B])
        pre = sb("pre", [P, 2, B])
        ga = sb("ga", [P, 3, B])
        tz, eo = sb("tz", [P, B]), sb("eo", [P, B])
        nc_ = sb("nc", [P, 2, B])
        sc = sb("sc", [P, 2, B])
        den, inv = sb("den", [P, B]), sb("inv", [P, B])
        nbo = sb("nbo", [P, 1])
        w, r, bias = g.w(f"sW{layer}"), g.w(f"sR{layer}"), g.w(f"sb{layer}")
        bi, bf, bz = (bias[:, k:k + 1] for k in range(3))
        negated = sem("negated")
        gates_if, gates_zo, hready, dve, gexp, zexp, init, predone = (
            sem(n) for n in ("gates_if", "gates_zo", "hready", "dve", "gexp", "zexp", "init", "predone"))
        gate = lambda q, k: g.ps[:, 2 * (k // 2) + q, k % 2 * B:(k % 2 + 1) * B]
        PER = 8
        with nc.Block() as block:

            @block.gpsimd
            def _(pool):
                pool.memset(hs[:, 0:B], 0.0).then_inc(init, 1)
                pool.memset(m[:, 1, :], 0.0).then_inc(init, 1)
                pool.memset(nc_[:], 0.0).then_inc(init, 1)

            @block.tensor
            def _(pe):
                def from_input(s, q):
                    pe.wait_ge(predone, s + 1)
                    pe.wait_ge(zexp, s + 1)
                    for k in range(GATES):
                        pe.matmul(gate(q, k), w[:, k * P:(k + 1) * P], xin[:, bass.ts(s, B)],
                                  start=(k % 2 == 0), stop=False, skip_group_check=True)

                def from_state(s, q):
                    pe.wait_ge(hready, s + 1)
                    for k in range(GATES):
                        ins = pe.matmul(gate(q, k), r[:, k * P:(k + 1) * P], hs[:, bass.ts(s, B)],
                                        start=False, stop=(k % 2 == 1), skip_group_check=True)
                        if k % 2 == 1:
                            ins.then_inc((gates_if, gates_zo)[k // 2], 1)

                pe.wait_ge(init, 3)
                with pe.Fori(0, S // 2) as pair:
                    for q in range(2):
                        s = pair * 2 + q
                        from_input(s, q)
                        from_state(s, q)

            @block.scalar
            def _(act):
                act.sem_inc(zexp, 2)
                act.wait_ge(negated, 1)
                with act.Fori(0, S // 2) as pair:
                    for q in range(2):
                        s = pair * 2 + q
                        act.wait_ge(gates_zo, s + 1)
                        act.wait_ge(dve, s * PER)
                        act.activation(tz[:], gate(q, 2), ACT.Tanh, bias=bz)
                        act.activation(eo[:], gate(q, 3), ACT.Exp, bias=nbo[:], scale=-1.0).then_inc(zexp, 1)
                        act.wait_ge(predone, s + 3)
                        act.activation(ga[:, 0:2, :], pre[:], ACT.Exp).then_inc(gexp, 1)

            @block.vector
            def _(ve):
                ve.sem_inc(predone, 2)
                ve.sem_inc(hready, 1)
                ve.tensor_scalar(nbo[:], bias[:, 3:4], -1.0, None, ALU.mult).then_inc(negated, 1)
                ve.wait_ge(init, 3)
                ch = Chain(ve, dve)
                with ve.Fori(0, S // 2) as pair:
                    ch.enter(pair, 2 * PER)
                    for q in range(2):
                        s = pair * 2 + q
                        new, old = m[:, q, :], m[:, 1 - q, :]
                        ve.wait_ge(gates_if, s + 1)
                        ch.link(ve.scalar_tensor_tensor(fm[:], gate(q, 1), bf, old, ALU.add, ALU.add))
                        ch.link(ve.scalar_tensor_tensor(new, gate(q, 0), bi, fm[:], ALU.add, ALU.max))
                        ch.inc(ve.tensor_tensor(pre[:, 0, :], fm[:], new, ALU.subtract))
                        ve.scalar_tensor_tensor(pre[:, 1, :], gate(q, 0), bi, new, ALU.add, ALU.subtract).then_inc(predone, 1)
                        ve.wait_ge(gexp, s + 1)
                        ve.wait_ge(zexp, s + 3)
                        ch.inc(ve.tensor_tensor(ga[:, 2, :], ga[:, 1, :], tz[:], ALU.mult))
                        ch.link(ve.tensor_tensor(sc[:], nc_[:], ga[:, 0:1, :].broadcast_to([P, 2, B]), ALU.mult))
                        ch.link(ve.tensor_tensor(nc_[:], sc[:], ga[:, 1:3, :], ALU.add))
                        ch.link(ve.scalar_tensor_tensor(den[:], eo[:], 1.0, nc_[:, 0, :], ALU.add, ALU.mult))
                        ch.link(ve.reciprocal(inv[:], den[:]))
                        ve.tensor_tensor(hs[:, bass.ts(s + 1, B)], nc_[:, 1, :], inv[:], ALU.mult).then_inc(hready, 1)
                    ch.leave(S // 2)


def mix_norm(nc, g, tag, layer, xin, hs, xout):
    last = xout is None
    with ExitStack() as ctx:
        sem = sem_maker(nc, ctx, tag)
        sb = lambda name, shape, dt=F32: ctx.enter_context(nc.sbuf_tensor(f"{tag}_{name}", shape, dt))
        R = 2
        gl = sb("gl", [P, R, CH])
        z = sb("z", [P, R, CH])
        zn = sb("zn", [P, R, TPC, D])
        st = sb("st", [P, R, TPC, 6])
        a, b, mean, var, rstd = (sb(n, [P, R, TPC]) for n in ("a", "b", "mean", "var", "rstd"))
        proj, gelu, zready, turned, stat, vch, var_ready, rstd_ready, nready, back, done, scaled = (
            sem(n) for n in ("proj", "gelu", "zready", "turned", "stat", "vch", "var_ready", "rstd_ready", "nready", "back", "done", "scaled"))

        def view(t, c):
            if last:
                return t.rearrange("p (s b) -> p b s", b=B)[:, bass.ts(c, BPC), :]
            return t[:, bass.ts(c, CH)].rearrange("p (s b) -> p s b", b=B)
        three = lambda t: t.rearrange("p (a k) -> p a k", k=B)
        bank_p, bank_z, bank_b = g.bank[0:2], g.bank[2:4], g.bank[4:6]
        with nc.Block() as block:

            @block.tensor
            def _(pe):
                with pe.Fori(0, NC // R) as pair:
                    for r in range(R):
                        c = pair * R + r
                        pe.wait_ge(gelu, c + 1)
                        pe.matmul(three(bank_p[r]), g.w(f"sP{layer}"), view(hs, c), start=True, stop=True).then_inc(proj, 1)
                        pe.wait_ge(zready, c + 1)
                        pe.wait_ge(nready, c * TPC)
                        for j in range(TPC):
                            ins = pe.transpose(bank_z[r][:, j * P:(j + 1) * P], z[:, r, j * P:(j + 1) * P], g.ident)
                        ins.then_inc(turned, 1)
                        if not last:
                            pe.wait_ge(nready, (c + 1) * TPC)
                            pe.wait_ge(done, c + 1)
                            for j in range(TPC):
                                ins = pe.transpose(bank_b[r][:, j * P:(j + 1) * P], zn[:, r, j, :], g.ident)
                            ins.then_inc(back, 1)

            @block.scalar
            def _(act):
                act.sem_inc(gelu, 1)
                if not last:
                    act.sem_inc(done, 1)
                with act.Fori(0, NC // R) as pair:
                    for r in range(R):
                        c = pair * R + r
                        act.wait_ge(proj, c + 1)
                        if r == 0:
                            act.wait_ge(zready, c)
                        act.activation(gl[:, r, :], bank_p[r], ACT.Gelu, bias=g.w(f"spb{layer}")).then_inc(gelu, 1)
                        if not last:
                            act.wait_ge(back, c + 1)
                            act.activation(xout[:, bass.ts(c, CH)], bank_b[r], ACT.Identity, bias=g.w(f"sbe{layer}"),
                                           scale=g.w(f"sga{layer}")).then_inc(done, 1)

            @block.gpsimd
            def _(pool):
                with pool.Fori(0, NC // R) as pair:
                    for r in range(R):
                        c = pair * R + r
                        pool.wait_ge(var_ready, c + 1)
                        pool.tensor_tensor(rstd[:, r, :], a[:, r, :], g.neghalf[:, 0:TPC], ALU.pow).then_inc(rstd_ready, 1)

            @block.vector
            def _(ve):
                ch = Chain(ve, vch)
                per = 6 + (3 if last else 0)
                with ve.Fori(0, NC // R) as pair:
                    ch.enter(pair, R * per)
                    for r in range(R):
                        c = pair * R + r
                        ve.wait_ge(gelu, c + 2)
                        ve.tensor_tensor(three(z[:, r, :]), three(gl[:, r, :]), view(xin, c), ALU.add).then_inc(zready, 1)
                        ve.wait_ge(turned, c + 1)
                        for j in range(TPC):
                            ve.bn_stats(st[:, r, j, :], bank_z[r][:, j * P:(j + 1) * P]).then_inc(stat, 1)
                        ve.wait_ge(stat, (c + 1) * TPC)
                        ve_a, ve_b, ve_m, ve_v = a[:, r, :], b[:, r, :], mean[:, r, :], var[:, r, :]
                        ch.inc(ve.tensor_tensor(ve_a, st[:, r, :, 1], st[:, r, :, 4], ALU.add))
                        ch.inc(ve.tensor_tensor(ve_b, st[:, r, :, 1], st[:, r, :, 4], ALU.subtract))
                        ch.link(ve.tensor_tensor(ve_v, st[:, r, :, 2], st[:, r, :, 5], ALU.add))
                        ch.link(ve.scalar_tensor_tensor(ve_b, ve_b, 0.25, ve_b, ALU.mult, ALU.mult))
                        ch.link(ve.scalar_tensor_tensor(ve_v, ve_v, 1.0 / D, ve_b, ALU.mult, ALU.add))
                        ch.link(ve.tensor_scalar(ve_m, ve_a, 0.5, None, ALU.mult))
                        ve.tensor_scalar(ve_a, ve_v, EPS, None, ALU.add).then_inc(var_ready, 1)
                        ve.wait_ge(rstd_ready, c + 1)
                        if not last:
                            ve.wait_ge(back, c)
                        for j in range(TPC):
                            ve.tensor_scalar(zn[:, r, j, :], bank_z[r][:, j * P:(j + 1) * P], mean[:, r, j:j + 1],
                                             rstd[:, r, j:j + 1], ALU.subtract, ALU.mult).then_inc(nready, 1)
                        if last:
                            ve.wait_ge(nready, (c + 1) * TPC)
                            row = lambda n: g.w(n).rearrange("p (o d) -> p o d", o=1).broadcast_to([P, TPC, D])
                            ch.link(ve.tensor_tensor(zn[:, r], zn[:, r], row("garow"), ALU.mult))
                            ch.link(ve.tensor_tensor(zn[:, r], zn[:, r], row("berow"), ALU.add))
                            xc = g.X[:, bass.ts(c, TPC), :]
                            ch.link(ve.tensor_tensor(xc, xc, zn[:, r], ALU.add))
                    ch.leave(NC // R)


def lstm_stage(nc, g):
    by_step = lambda c: g.xT[:, :].rearrange("p (s b) -> p b s", b=B)[:, bass.ts(c, BPC), :]
    norm_stage(nc, g, "n3", place=by_step)
    with ExitStack() as ctx:
        hs = ctx.enter_context(nc.sbuf_tensor("lstm_h", [P, T + B], F32))
        x1 = ctx.enter_context(nc.sbuf_tensor("lstm_x1", [P, T], F32))
        recurrence(nc, g, "r0", 0, g.xT, hs)
        mix_norm(nc, g, "m0", 0, g.xT[:, :], hs[:, B:], x1)
        recurrence(nc, g, "r1", 1, x1, hs)
        mix_norm(nc, g, "m1", 1, x1[:, :], hs[:, B:], None)


NX = 8
CAP = T * 5 // (4 * NX)
TILES = T // P + NX
RING = 4
BITS = 30


class Router:

    def __init__(self, nc, g, ctx, tag):
        self.nc, self.g, self.tag = nc, g, tag
        self.sem = sem_maker(nc, ctx, tag)
        self.sb = lambda name, shape, dt=F32: ctx.enter_context(nc.sbuf_tensor(f"{tag}_{name}", shape, dt))
        self.p = self.sb("p", [P, NT, NX])
        self.oh = self.sb("oh", [P, NT, NX])
        self.t = self.sb("t", [P, NT, NX])
        self.pos = self.sb("pos", [P, NT, NX])
        self.incl = self.sb("incl", [P, NX, NT])
        self.m = self.sb("m", [P, NT])
        self.m2 = self.sb("m2", [P, NT])
        self.slot = self.sb("slot", [P, NT])
        self.slot_u = self.sb("slot_u", [P, NT], U32)
        self.weight = self.sb("weight", [P, NT])

    def over_experts(self, a):
        return a.rearrange("p (n o) -> p n o", o=1).broadcast_to([P, NT, NX])

    def over_tiles(self, a):
        return a.rearrange("p (o e) -> p o e", o=1).broadcast_to([P, NT, NX])

    def pick(self, ve, ch, score, best):
        over, r = self.over_experts, self
        ch.link(ve.tensor_tensor(r.t[:], score, over(best), ALU.is_ge))
        ch.link(ve.scalar_tensor_tensor(r.t[:], r.t[:], -float(NX), r.over_tiles(r.g.w("eidx")), ALU.mult, ALU.add))
        ch.link(ve.tensor_reduce(r.m2[:], r.t[:], AX_X, ALU.min))
        ch.link(ve.tensor_tensor(r.oh[:], r.t[:], over(r.m2[:]), ALU.is_equal))

    def ranks(self, ve, ch, counted, times):
        r, g = self, self.g
        ve.wait_ge(counted, times)
        cnt = g.bank[1][:, 0:NT * NX].rearrange("p (n e) -> p e n", e=NX)
        for e in range(NX):
            ch.inc(ve.tensor_tensor_scan(r.incl[:, e, :], g.w("onerow"), cnt[:, e, :], 0.0, ALU.mult, ALU.add))
        ve.wait_ge(ch.sem, ch.value())
        incl = r.incl[:].rearrange("p e n -> p n e")
        flat = lambda k: g.bank[k][:, 0:NT * NX].rearrange("p (n e) -> p n e", e=NX)
        ch.link(ve.tensor_tensor(r.pos[:], incl, flat(1), ALU.subtract))
        ch.link(ve.tensor_tensor(r.pos[:], r.pos[:], flat(0), ALU.add))


def count_flags(pe, g, flags):
    f = flags[:].rearrange("p n e -> p (n e)")
    pe.matmul(g.bank[0][:, 0:NT * NX], g.w("before"), f, start=True, stop=True)
    return pe.matmul(g.bank[1][:, 0:NT * NX], g.w("allones"), f, start=True, stop=True)


def softmax_block(nc, g, r, gate, bias):
    logits, chain, sub, exped = (r.sem(n) for n in ("logits", "chain", "sub", "exped"))
    with nc.Block() as block:

        @block.tensor
        def _(pe):
            for n in range(NT):
                ins = pe.matmul(g.bank[2][:, n * NX:(n + 1) * NX], g.xT[:, n * P:(n + 1) * P], gate, start=True, stop=True)
            ins.then_inc(logits, 1)

        @block.scalar
        def _(act):
            act.wait_ge(sub, 1)
            act.activation(r.p[:], r.p[:], ACT.Exp).then_inc(exped, 1)

        @block.vector
        def _(ve):
            ch = Chain(ve, chain)
            lg = g.bank[2][:, 0:NT * NX].rearrange("p (n e) -> p n e", e=NX)
            ve.wait_ge(logits, 1)
            if bias is not None:
                ch.link(ve.tensor_tensor(r.p[:], lg, r.over_tiles(bias), ALU.add))
            else:
                ch.link(ve.tensor_copy(r.p[:], lg))
            ch.link(ve.tensor_reduce(r.m[:], r.p[:], AX_X, ALU.max))
            ve.tensor_tensor(r.p[:], r.p[:], r.over_experts(r.m[:]), ALU.subtract).then_inc(sub, 1)
            ve.wait_ge(exped, 1)
            ch.link(ve.tensor_reduce(r.m[:], r.p[:], AX_X, ALU.add))
            ch.link(ve.reciprocal(r.m[:], r.m[:]))
            ch.link(ve.tensor_tensor(r.p[:], r.p[:], r.over_experts(r.m[:]), ALU.mult))
            ch.link(ve.tensor_reduce(r.m[:], r.p[:], AX_X, ALU.max))


def dispatch(nc, g, tag, r, slots):
    with ExitStack() as ctx:
        sem = sem_maker(nc, ctx, tag)
        zero = ctx.enter_context(nc.sbuf_tensor(f"{tag}_zero", [P, CH], F32))
        zeroed, filled = sem("zeroed"), sem("filled")
        scattered = g.lasting(f"{tag}_scattered")
        rows = (TILES + 1) * P
        with nc.Block() as block:

            @block.vector
            def _(ve):
                ve.memset(zero[:], 0.0).then_inc(zeroed, 1)

            @block.sync
            def _(sp):
                sp.wait_ge(zeroed, 1)
                view = g.buf[0:rows, :].rearrange("(a p) d -> p a d", p=P)
                count = 0
                for a in range(0, TILES + 1, TPC):
                    w = min(TPC, TILES + 1 - a)
                    sp.dma_start(view[:, a:a + w, :], zero[:, 0:w * D].rearrange("p (a d) -> p a d", d=D)).then_inc(filled, 16)
                    count += 16
                sp.wait_ge(filled, count)

            @block.gpsimd
            def _(pool):
                pool.wait_ge(filled, 16 * ((TILES + TPC) // TPC))
                for n in range(NT):
                    pool.indirect_dma_start(g.buf, bass.IndirectOffsetOnAxis(ap=slots[:, n:n + 1], axis=0), g.rows[:, n, :], None).then_inc(scattered, 16)
                pool.wait_ge(scattered, 16 * NT)


def experts(nc, g, tag, F, w1, w2, owner, func, b1=None, b2=None):
    FB = F // P
    with ExitStack() as ctx:
        sem = sem_maker(nc, ctx, tag)
        sb = lambda name, shape, dt=F32: ctx.enter_context(nc.sbuf_tensor(f"{tag}_{name}", shape, dt))
        xr = sb("xr", [P, RING, D])
        xT = sb("xT", [P, 2, P])
        h = sb("h", [P, 2, F])
        hT = sb("hT", [P, 2, FB, P])
        y = sb("y", [P, RING, D])
        row_in = [sem(f"row_in{k}") for k in range(RING)]
        out_done = [g.lasting(f"{tag}_out_done{k}") for k in range(RING)]
        turned, xcopy, mm1, hready, hturned, hcopy, mm2, yready = (
            sem(n) for n in ("turned", "xcopy", "mm1", "hready", "hturned", "hcopy", "mm2", "yready"))
        bank_x, bank_h, bank_t, bank_y = g.bank[0:2], g.bank[2:4], g.bank[4:6], g.bank[6:8]
        with nc.Block() as block:

            @block.sync
            def _(sp):
                def load(k, r):
                    sp.dma_start(xr[:, r, :], g.buf[bass.ts(k, P), :]).then_inc(row_in[r], 16)

                for k in range(RING):
                    load(k, k)
                with sp.Fori(0, TILES // RING - 1) as i:
                    for r in range(RING):
                        sp.wait_ge(turned, i * RING + (r + 1))
                        load(i * RING + (RING + r), r)
                sp.wait_ge(turned, TILES - RING + 1)
                load(TILES, 0)

            @block.tensor
            def _(pe):
                def first(k, r, uses):
                    pe.wait_ge(row_in[r], uses * 16)
                    pe.wait_ge(xcopy, k + 1)
                    pe.transpose(bank_x[r % 2][:, 0:P], xr[:, r, :], g.ident).then_inc(turned, 1)
                    e = pe.value_load(owner[0:1, bass.ds(k, 1)], min_val=0, max_val=NX - 1)
                    pe.wait_ge(xcopy, k + 3)
                    pe.wait_ge(hready, k + 1)
                    pe.matmul(bank_h[r % 2][:, 0:F], xT[:, r % 2, :], w1[:, bass.ts(e, F)], start=True, stop=True).then_inc(mm1, 1)

                def second(k, r):
                    pe.wait_ge(hready, k + 3)
                    pe.wait_ge(hcopy, k + 1)
                    for f in range(FB):
                        ins = pe.transpose(bank_t[r % 2][:, f * P:(f + 1) * P], h[:, r % 2, f * P:(f + 1) * P], g.ident)
                    ins.then_inc(hturned, 1)
                    e = pe.value_load(owner[0:1, bass.ds(k, 1)], min_val=0, max_val=NX - 1)
                    pe.wait_ge(hcopy, k + 3)
                    pe.wait_ge(yready, k + 1)
                    for f in range(FB):
                        ins = pe.matmul(bank_y[r % 2][:, 0:D], hT[:, r % 2, f, :], w2[:, bass.ds(e * (FB * D) + f * D, D)],
                                        start=(f == 0), stop=(f == FB - 1))
                    ins.then_inc(mm2, 1)

                first(0, 0, 1)
                with pe.Fori(0, TILES // RING) as i:
                    for r in range(RING):
                        k = i * RING + r
                        first(k + 1, (r + 1) % RING, i + (1 if r + 1 < RING else 2))
                        second(k, r)

            @block.scalar
            def _(act):
                act.sem_inc(xcopy, 2)
                act.sem_inc(hcopy, 2)

                def first(k, r):
                    act.wait_ge(turned, k + 1)
                    act.activation(xT[:, r % 2, :], bank_x[r % 2][:, 0:P], ACT.Copy).then_inc(xcopy, 1)
                    if b1 is None:
                        act.wait_ge(mm1, k + 1)
                        act.wait_ge(hturned, k)
                        act.activation(h[:, r % 2, :], bank_h[r % 2][:, 0:F], func).then_inc(hready, 1)

                def second(k, r):
                    act.wait_ge(hturned, k + 1)
                    act.wait_ge(mm2, k)
                    act.activation(hT[:, r % 2].rearrange("p f t -> p (f t)"), bank_t[r % 2][:, 0:F], func).then_inc(hcopy, 1)

                if b1 is None:
                    act.sem_inc(hready, 2)
                first(0, 0)
                with act.Fori(0, TILES // RING) as i:
                    for r in range(RING):
                        k = i * RING + r
                        first(k + 1, (r + 1) % RING)
                        if b1 is not None:
                            second(k, r)

            @block.vector
            def _(ve):
                ve.sem_inc(yready, 2)
                if b1 is not None:
                    ve.sem_inc(hready, 2)

                def first(k, r):
                    e = ve.value_load(owner[0:1, bass.ds(k, 1)], min_val=0, max_val=NX - 1)
                    ve.wait_ge(mm1, k + 1)
                    ve.wait_ge(hturned, k)
                    ve.tensor_tensor(h[:, r % 2, :], bank_h[r % 2][:, 0:F], b1[:, bass.ts(e, F)], ALU.add).then_inc(hready, 1)

                def second(k, r, uses):
                    if b1 is None:
                        ve.wait_ge(hturned, k + 1)
                        ve.wait_ge(mm2, k)
                        ve.tensor_copy(hT[:, r % 2].rearrange("p f t -> p (f t)"), bank_t[r % 2][:, 0:F]).then_inc(hcopy, 1)
                    if b2 is not None:
                        e = ve.value_load(owner[0:1, bass.ds(k, 1)], min_val=0, max_val=NX - 1)
                    ve.wait_ge(out_done[r], uses * 16)
                    ve.wait_ge(mm2, k + 1)
                    if b2 is not None:
                        ve.tensor_tensor(y[:, r, :], bank_y[r % 2][:, 0:D], b2[:, bass.ts(e, D)], ALU.add).then_inc(yready, 1)
                    else:
                        ve.tensor_copy(y[:, r, :], bank_y[r % 2][:, 0:D]).then_inc(yready, 1)

                if b1 is not None:
                    first(0, 0)
                with ve.Fori(0, TILES // RING) as i:
                    for r in range(RING):
                        k = i * RING + r
                        if b1 is not None:
                            first(k + 1, (r + 1) % RING)
                        second(k, r, i)

            @block.gpsimd
            def _(pool):
                with pool.Fori(0, TILES // RING) as i:
                    for r in range(RING):
                        k = i * RING + r
                        pool.wait_ge(yready, k + 3)
                        pool.dma_start(g.out[bass.ts(k, P), :], y[:, r, :]).then_inc(out_done[r], 16)
                for r in range(RING):
                    pool.wait_ge(out_done[r], 16 * (TILES // RING))


def combine(nc, g, tag, places, weight):
    G = 8
    with ExitStack() as ctx:
        sem = sem_maker(nc, ctx, tag)
        row = ctx.enter_context(nc.sbuf_tensor(f"{tag}_row", [P, G, D], F32))
        got = [g.lasting(f"{tag}_got{k}") for k in range(G)]
        added = sem("added")
        with nc.Block() as block:

            @block.gpsimd
            def _(pool):
                for n in range(NT):
                    if n >= G:
                        pool.wait_ge(added, n - G + 1)
                    pool.indirect_dma_start(row[:, n % G, :], None, g.out, bass.IndirectOffsetOnAxis(ap=places[:, n:n + 1], axis=0)).then_inc(got[n % G], 16)

            @block.vector
            def _(ve):
                for n in range(NT):
                    ve.wait_ge(got[n % G], 16 * (n // G + 1))
                    ve.scalar_tensor_tensor(g.X[:, n, :], row[:, n % G, :], weight[:, n:n + 1], g.X[:, n, :],
                                            ALU.mult, ALU.add).then_inc(added, 1)


def switch_stage(nc, g):
    with ExitStack() as ctx:
        g.rows = ctx.enter_context(nc.sbuf_tensor("sw_rows", [P, NT, D], F32))
        norm_stage(nc, g, "n2", keep=True)
        r = Router(nc, g, ctx, "sw")
        sb = r.sb
        w1, w2, b1, b2 = sb("w1", [P, NX * 512]), sb("w2", [P, NX * 512]), sb("b1", [P, NX * 512]), sb("b2", [P, NX * D])
        place = sb("place", [P, NT])
        place_u = sb("place_u", [P, NT], U32)
        owner = sb("owner", [1, TILES + 1], I32)
        softmax_block(nc, g, r, g.w("gate0"), g.w("gateb0"))
        win, picked, counted, chain = (r.sem(n) for n in ("win", "picked", "counted", "chain2"))
        with nc.Block() as block:

            @block.sync
            def _(sp):
                for t, d in ((w1, g.moe0["w1"]), (w2, g.moe0["w2"]), (b1, g.moe0["b1"]), (b2, g.moe0["b2"]), (owner, g.moe0["owner"])):
                    sp.dma_start(t[:], d).then_inc(win, 16)
                sp.wait_ge(win, 80)

            @block.tensor
            def _(pe):
                pe.wait_ge(picked, 1)
                count_flags(pe, g, r.oh).then_inc(counted, 1)

            @block.vector
            def _(ve):
                ch = Chain(ve, chain)
                r.pick(ve, ch, r.p[:], r.m[:])
                ve.sem_inc(picked, 1)
                r.ranks(ve, ch, counted, 1)
                ch.link(ve.tensor_tensor(r.t[:], r.oh[:], r.pos[:], ALU.mult))
                ch.link(ve.tensor_reduce(r.slot[:], r.t[:], AX_X, ALU.add))
                ch.link(ve.tensor_tensor(r.t[:], r.oh[:], r.over_tiles(g.w("eidx")), ALU.mult))
                ch.link(ve.tensor_reduce(r.m2[:], r.t[:], AX_X, ALU.add))
                ch.link(ve.tensor_scalar(r.weight[:], r.slot[:], float(CAP), None, ALU.is_lt))
                ch.link(ve.tensor_scalar(place[:], r.slot[:], float(CAP - 1), None, ALU.min))
                ch.link(ve.scalar_tensor_tensor(place[:], r.m2[:], float(CAP), place[:], ALU.mult, ALU.add))
                ch.link(ve.tensor_copy(place_u[:], place[:]))
                ch.link(ve.tensor_tensor(r.slot[:], place[:], g.w("spare"), ALU.subtract))
                ch.link(ve.tensor_tensor(r.slot[:], r.slot[:], r.weight[:], ALU.mult))
                ch.link(ve.tensor_tensor(r.slot[:], r.slot[:], g.w("spare"), ALU.add))
                ch.link(ve.tensor_copy(r.slot_u[:], r.slot[:]))
                ch.link(ve.tensor_tensor(r.weight[:], r.weight[:], r.m[:], ALU.mult))

        dispatch(nc, g, "sd", r, r.slot_u)
        experts(nc, g, "se", 512, w1[:], w2[:], owner, ACT.Relu, b1=b1[:], b2=b2[:])
        combine(nc, g, "sc", place_u, r.weight)


def choice_stage(nc, g):
    with ExitStack() as ctx:
        g.rows = ctx.enter_context(nc.sbuf_tensor("ec_rows", [P, NT, D], F32))
        norm_stage(nc, g, "n5", keep=True)
        r = Router(nc, g, ctx, "ec")
        sb = r.sb
        w1, w2 = sb("w1", [P, NX * 256]), sb("w2", [P, NX * 256])
        softmax_block(nc, g, r, g.w("gate1"), None)
        thr = sb("thr", [P, NX])
        cand = sb("cand", [P, NX])
        part = sb("part", [P, NX])
        need = sb("need", [P, NX])
        gt = sb("gt", [P, NT, NX])
        eq = sb("eq", [P, NT, NX])
        tiles_i = sb("tiles_i", [P, NX], I32)
        ends = sb("ends", [P, NX])
        own = sb("own", [P, TILES + 1, NX])
        ownf = sb("ownf", [P, TILES + 1])
        owner = sb("owner", [P, TILES + 1], I32)
        bits = sb("bits", [P, BITS], I32)
        K = float(T // NX)
        win, parted, counted, chain, step, picked, ranked = (r.sem(n) for n in ("win", "parted", "counted", "chain2", "step", "picked", "ranked"))
        over = r.over_tiles
        by_expert = lambda a: a.rearrange("p n e -> p e n")
        with nc.Block() as block:

            @block.sync
            def _(sp):
                sp.dma_start(bits[:], g.bits_dram).then_inc(win, 16)
                for t, d in ((w1, g.moe1["w1"]), (w2, g.moe1["w2"])):
                    sp.dma_start(t[:], d).then_inc(win, 16)
                sp.wait_ge(win, 48)

            @block.tensor
            def _(pe):
                with pe.Fori(0, BITS + 1) as i:
                    pe.wait_ge(parted, i + 1)
                    pe.matmul(g.bank[3][:, 0:NX], g.w("allones"), part[:], start=True, stop=True).then_inc(counted, 1)
                for k in range(2):
                    pe.wait_ge(picked, k + 1)
                    count_flags(pe, g, (eq, r.oh)[k]).then_inc(ranked, 1)

            @block.vector
            def _(ve):
                ch = Chain(ve, chain)
                ch.link(ve.memset(thr[:], 0.0))
                ve.wait_ge(win, 48)
                with ve.Fori(0, BITS) as i:
                    ch.enter(i, 4)
                    bit = bits[:, bass.ds(i, 1)].broadcast_to([P, NX])
                    ch.link(ve.tensor_tensor(cand[:].bitcast(I32), thr[:].bitcast(I32), bit, ALU.bitwise_or))
                    ch.link(ve.tensor_tensor(r.t[:], r.p[:], over(cand[:]), ALU.is_ge))
                    ve.tensor_reduce(part[:], by_expert(r.t[:]), AX_X, ALU.add).then_inc(parted, 1)
                    ve.wait_ge(counted, i + 1)
                    ch.link(ve.scalar_tensor_tensor(cand[:], g.bank[3][:, 0:NX], K, cand[:], ALU.is_ge, ALU.mult))
                    ch.link(ve.tensor_tensor(thr[:], thr[:], cand[:], ALU.max))
                ch.leave(BITS)
                ch.link(ve.tensor_tensor(gt[:], r.p[:], over(thr[:]), ALU.is_gt))
                ve.tensor_tensor(eq[:], r.p[:], over(thr[:]), ALU.is_equal).then_inc(picked, 1)
                ve.tensor_reduce(part[:], by_expert(gt[:]), AX_X, ALU.add).then_inc(parted, 1)
                ve.wait_ge(counted, BITS + 1)
                ch.link(ve.tensor_scalar(need[:], g.bank[3][:, 0:NX], -1.0, K, ALU.mult, ALU.add))
                r.ranks(ve, ch, ranked, 1)
                ch.link(ve.tensor_tensor(r.pos[:], r.pos[:], over(need[:]), ALU.is_lt))
                ch.link(ve.tensor_tensor(eq[:], eq[:], r.pos[:], ALU.mult))
                ch.link(ve.tensor_tensor(gt[:], gt[:], eq[:], ALU.add))
                ch.link(ve.tensor_reduce(r.m[:], gt[:], AX_X, ALU.max))
                ch.link(ve.tensor_scalar(r.m[:], r.m[:], 0.0, None, ALU.is_equal))
                ch.link(ve.tensor_tensor(gt[:], gt[:], r.over_experts(r.m[:]), ALU.max))
                ch.link(ve.tensor_tensor(eq[:], r.p[:], gt[:], ALU.mult))
                ch.link(ve.scalar_tensor_tensor(eq[:], gt[:], -1.0, eq[:], ALU.add, ALU.add))
                ch.link(ve.tensor_reduce(r.weight[:], eq[:], AX_X, ALU.max))
                r.pick(ve, ch, eq[:], r.weight[:])
                ve.sem_inc(picked, 1)
                r.ranks(ve, ch, ranked, 2)
                ch.link(ve.tensor_tensor(r.t[:], r.oh[:], r.pos[:], ALU.mult))
                ch.link(ve.tensor_reduce(r.slot[:], r.t[:], AX_X, ALU.add))
                ch.link(ve.tensor_scalar(tiles_i[:], r.incl[:, :, NT - 1], float(P - 1), None, ALU.add))
                ch.link(ve.tensor_scalar(tiles_i[:], tiles_i[:], 7, None, ALU.arith_shift_right))
                ch.link(ve.tensor_copy(cand[:], tiles_i[:]))
                ch.link(ve.tensor_tensor_scan(ends[:], g.w("onerow")[:, 0:NX], cand[:], 0.0, ALU.mult, ALU.add))
                ch.link(ve.tensor_tensor(part[:], ends[:], cand[:], ALU.subtract))
                ch.link(ve.tensor_scalar(part[:], part[:], float(P), None, ALU.mult))
                ch.link(ve.tensor_tensor(r.t[:], r.oh[:], over(part[:]), ALU.mult))
                ch.link(ve.tensor_reduce(r.m2[:], r.t[:], AX_X, ALU.add))
                ch.link(ve.tensor_tensor(r.slot[:], r.slot[:], r.m2[:], ALU.add))
                ch.link(ve.tensor_copy(r.slot_u[:], r.slot[:]))
                ch.link(ve.tensor_tensor(own[:], ends[:].rearrange("p (o e) -> p o e", o=1).broadcast_to([P, TILES + 1, NX]),
                                         g.w("tileidx").rearrange("p (n o) -> p n o", o=1).broadcast_to([P, TILES + 1, NX]), ALU.is_le))
                ch.link(ve.tensor_reduce(ownf[:], own[:], AX_X, ALU.add))
                ch.link(ve.tensor_scalar(owner[:], ownf[:], float(NX - 1), None, ALU.min))

        dispatch(nc, g, "ed", r, r.slot_u)
        experts(nc, g, "ee", 256, w1[:], w2[:], owner, ACT.Gelu)
        combine(nc, g, "eo", r.slot_u, r.weight)


FILL = -99999.0


def single_cross_stage(nc, g):
    norm_stage(nc, g, "n4")
    with ExitStack() as ctx:
        sem = sem_maker(nc, ctx, "sa")
        sb = lambda name, shape, dt=F32: ctx.enter_context(nc.sbuf_tensor(f"sa_{name}", shape, dt))
        R = 2
        PPC = BPC // 2
        qT, kT, vT = sb("qT", [P, R, CH]), sb("kT", [P, R, CH]), sb("vT", [P, R, CH])
        v = sb("v", [P, R, PPC, D])
        mask = sb("mask", [P, NT, P], I32)
        on = sb("on", [P, R, PPC, P])
        low = sb("low", [P, R, PPC, P])
        sc = sb("sc", [P, R, PPC, P])
        pr = sb("pr", [P, R, PPC, P])
        pT = sb("pT", [P, R, PPC, P])
        nmx, rs, ri = sb("nmx", [P, R, PPC]), sb("rs", [P, R, PPC]), sb("ri", [P, R, PPC])
        mask_in, proj, qkv, vt, vcopy, mchain, mready, scored, vch, masked, exped, turned, tcopy, pv, added = (
            sem(n) for n in ("mask_in", "proj", "qkv", "vt", "vcopy", "mchain", "mready", "scored", "vch", "masked", "exped",
                             "turned", "tcopy", "pv", "added"))
        mready2 = sem("mready2")
        flat = lambda t, r: t[:, r].rearrange("p a k -> p (a k)")
        bank_p, bank_v, bank_s, bank_t, bank_o = g.bank[0:3], g.bank[3], g.bank[4:6], g.bank[6], g.bank[7]
        with nc.Block() as block:

            @block.sync
            def _(sp):
                for b in range(2):
                    src = g.mask1_dram.rearrange("(o n) k -> o n k", o=1).broadcast_to([S, NT, P])
                    sp.dma_start(mask[b * S:(b + 1) * S], src).then_inc(mask_in, 16)

            @block.gpsimd
            def _(pool):
                pool.wait_ge(mask_in, 32)
                ch = Chain(pool, mchain)
                with pool.Fori(0, NC // R) as pair:
                    ch.enter(pair, R * 4)
                    for r in range(R):
                        c = pair * R + r
                        pool.wait_ge(masked, pair * R + r + 1)
                        o, l = on[:, r], low[:, r]
                        over = lambda w: g.w(w).rearrange("p (o k) -> p o k", o=1).broadcast_to([P, PPC, P])
                        ch.link(pool.tensor_copy(o, mask[:, bass.ts(c, PPC), :]))
                        alone(pool)
                        ch.link(pool.tensor_scalar(o, o, 0.0, -1.0, ALU.is_equal, ALU.mult))
                        alone(pool)
                        ch.link(pool.tensor_scalar(o, o, 1.0, None, ALU.add))
                        alone(pool)
                        ch.link(pool.tensor_tensor(o, o, over("same"), ALU.mult))
                        alone(pool)
                        pool.tensor_scalar(l, o, -1.0, 1.0, ALU.mult, ALU.add).then_inc(mready2, 1)
                        pool.wait_ge(mready2, c + 1)
                        pool.tensor_tensor(l, l, over("lowrow"), ALU.mult).then_inc(mready, 1)
                    ch.leave(NC // R)

            @block.tensor
            def _(pe):
                with pe.Fori(0, NC // R) as pair:
                    for r in range(R):
                        c = pair * R + r
                        cs = bass.ts(c, CH)
                        pe.wait_ge(qkv, c * 3)
                        for k, (w, src) in enumerate((("Wq1", g.xT), ("Wk1", g.ctxT), ("Wv1", g.ctxT))):
                            pe.matmul(bank_p[k], g.w(w), src[:, cs], start=True, stop=True).then_inc(proj, 1)
                        pe.wait_ge(qkv, c * 3 + 2)
                        for p in range(PPC):
                            ps = slice(p * P, (p + 1) * P)
                            ins = pe.matmul(bank_s[r][:, ps], qT[:, r, ps], kT[:, r, ps], start=True, stop=True)
                        ins.then_inc(scored, 1)
                        pe.wait_ge(qkv, c * 3 + 3)
                        for p in range(PPC):
                            ins = pe.transpose(bank_v[:, p * P:(p + 1) * P], vT[:, r, p * P:(p + 1) * P], g.ident)
                        ins.then_inc(vt, 1)
                        pe.wait_ge(exped, c + 1)
                        for p in range(PPC):
                            ins = pe.transpose(bank_t[:, p * P:(p + 1) * P], pr[:, r, p, :], g.ident)
                        ins.then_inc(turned, 1)
                        pe.wait_ge(tcopy, c + 1)
                        pe.wait_ge(vcopy, c + 1)
                        pe.wait_ge(added, c)
                        for p in range(PPC):
                            ins = pe.matmul(bank_o[:, p * P:(p + 1) * P], pT[:, r, p, :], v[:, r, p, :], start=True, stop=True)
                        ins.then_inc(pv, 1)

            @block.scalar
            def _(act):
                with act.Fori(0, NC // R) as pair:
                    for r in range(R):
                        c = pair * R + r
                        for k, t in enumerate((qT, kT, vT)):
                            act.wait_ge(proj, c * 3 + (k + 1))
                            act.activation(t[:, r, :], bank_p[k], ACT.Copy).then_inc(qkv, 1)
                        act.wait_ge(vt, c + 1)
                        act.activation(flat(v, r), bank_v, ACT.Copy).then_inc(vcopy, 1)
                        act.wait_ge(masked, c + 3)
                        for p in range(PPC):
                            ins = act.activation(pr[:, r, p, :], sc[:, r, p, :], ACT.Exp, bias=nmx[:, r, p:p + 1],
                                                 accum_out=rs[:, r, p:p + 1])
                        ins.then_inc(exped, 1)

            @block.vector
            def _(ve):
                ve.sem_inc(masked, 2)
                ch = Chain(ve, vch)
                with ve.Fori(0, NC // R) as pair:
                    ch.enter(pair, R * 3)
                    for r in range(R):
                        c = pair * R + r
                        ve.wait_ge(scored, c + 1)
                        ve.wait_ge(mready, c + 1)
                        ch.link(ve.tensor_tensor(flat(sc, r), bank_s[r], flat(on, r), ALU.mult))
                        ch.link(ve.tensor_tensor(flat(sc, r), flat(sc, r), flat(low, r), ALU.add))
                        ve.tensor_reduce(nmx[:, r, :], sc[:, r], AX_X, ALU.max, negate=True).then_inc(masked, 1)
                        ve.wait_ge(turned, c + 1)
                        ve.tensor_copy(flat(pT, r), bank_t).then_inc(tcopy, 1)
                        ch.link(ve.reciprocal(ri[:, r, :], rs[:, r, :]))
                        ve.wait_ge(pv, c + 1)
                        for p in range(PPC):
                            x = g.X[:, bass.ds(c * PPC + p, 1), :].rearrange("p a d -> p (a d)")
                            ins = ve.scalar_tensor_tensor(x, bank_o[:, p * P:(p + 1) * P], ri[:, r, p:p + 1], x, ALU.mult, ALU.add)
                        ins.then_inc(added, 1)
                    ch.leave(NC // R)


def layout():
    H = E0 // P
    items = [("ident", P), ("norm_w", 1), ("inT", E0), ("skipT", E0), ("convrow", KC * E0), ("conv_b", H), ("wd1T", H * DD),
             ("wd2T", E0), ("wd2_b", H), ("wbcT", H * P), ("A_log", H * NS), ("W_D", H), ("outT", H * D), ("big", 32),
             ("Wq", D), ("bq", 1), ("Wk", D), ("bk", 1), ("Wv", D), ("bv", 1), ("Wo", D), ("bo", D), ("headrow", HG), ("ones", P)]
    for l in range(2):
        items += [(f"sW{l}", GATES * D), (f"sR{l}", GATES * D), (f"sb{l}", GATES), (f"sP{l}", D), (f"spb{l}", 1), (f"sga{l}", 1), (f"sbe{l}", 1)]
    items += [("garow", D), ("berow", D)]
    items += [("Wq1", D), ("Wk1", D), ("Wv1", D), ("same", P), ("lowrow", P)]
    items += [("gate0", NX), ("gateb0", NX), ("gate1", NX), ("eidx", NX), ("before", P), ("allones", P), ("onerow", NT), ("spare", NT),
              ("tileidx", TILES + 1)]
    at, out = 0, {}
    for n, w in items:
        out[n] = (at, w)
        at += w
    return out, at


def program(nc, x, packed, sel, ctxT, bias, mask8, pairsel, moe0, moe1, bits, mask1, out):
    lay, width = layout()
    g = Core()
    with ExitStack() as ctx:
        g.lasting = lambda name: ctx.enter_context(nc.semaphore(name))
        sb = lambda name, shape, dt=F32: ctx.enter_context(nc.sbuf_tensor(name, shape, dt))
        g.X = sb("X", [P, NT, D])
        g.xT = sb("xT", [P, T])
        g.wts = sb("wts", [P, width])
        g.w = lambda n: g.wts[:, lay[n][0]:lay[n][0] + lay[n][1]]
        g.ident = g.w("ident")
        g.neghalf = sb("neghalf", [P, NT])
        g.sel_dram, g.bias_dram, g.mask8_dram = sel, bias, mask8
        g.mask1_dram = mask1
        g.moe0, g.moe1, g.bits_dram = moe0, moe1, bits
        g.buf = nc.dram_tensor("places", ((TILES + 1) * P + T, D), F32, kind="Internal").ap()
        g.out = nc.dram_tensor("place_results", (TILES * P, D), F32, kind="Internal").ap()
        g.ctxT = sb("ctxT", [P, T])
        g.pairsel = sb("pairsel", [2, P], BF16)
        g.ps = ctx.enter_context(nc.psum_tensor("ps", [P, 8, CH], F32))
        g.bank = [g.ps[:, i, :] for i in range(8)]
        loaded = ctx.enter_context(nc.semaphore("loaded"))
        consts = ctx.enter_context(nc.semaphore("consts"))
        stored = ctx.enter_context(nc.semaphore("stored"))
        with nc.Block() as block:

            @block.sync
            def _(sp):
                sp.dma_start(g.X[:], x.rearrange("(a p) d -> p a d", p=P)).then_inc(loaded, 16)
                sp.dma_start(g.wts[:], packed).then_inc(loaded, 16)
                sp.dma_start(g.ctxT[:], ctxT).then_inc(loaded, 16)
                sp.dma_start(g.pairsel[:], pairsel).then_inc(loaded, 16)
                sp.wait_ge(loaded, 64)

            @block.vector
            def _(ve):
                ve.memset(g.neghalf[:], -0.5).then_inc(consts, 1)

        stages = [scan_stage, cross_stage, switch_stage, lstm_stage, single_cross_stage, choice_stage]
        for f in stages:
            f(nc, g)
        with nc.Block() as block:

            @block.sync
            def _(sp):
                sp.dma_start(out.rearrange("(a p) d -> p a d", p=P), g.X[:]).then_inc(stored, 16)
                sp.wait_ge(stored, 16)


def pack(inp):
    lay, width = layout()
    H = E0 // P
    arr = np.zeros((P, width), np.float32)

    def put(name, a):
        at, w = lay[name]
        a = np.asarray(a)
        arr[:a.shape[0], at:at + a.shape[1]] = a

    halves = lambda a: np.concatenate([a[h * P:(h + 1) * P] for h in range(H)], axis=1)
    I = lambda n: np.asarray(inp["L0_attn_" + n])
    put("ident", np.eye(P, dtype=np.float32))
    put("norm_w", I("norm_w")[:, None])
    put("inT", I("in_w").T)
    put("skipT", I("skip_w").T)
    put("convrow", np.broadcast_to(I("conv_w")[:, 0, :].T.reshape(1, KC * E0), (P, KC * E0)))
    put("conv_b", halves(I("conv_b")[:, None]))
    put("wd1T", halves(I("wd1").T))
    put("wd2T", I("wd2").T)
    put("wd2_b", halves(I("wd2_b")[:, None]))
    bc = np.concatenate([I("wb").T, I("wc").T], axis=1)
    put("wbcT", halves(np.concatenate([bc, bc, bc, bc], axis=1)))
    put("A_log", halves(I("A_log")))
    put("W_D", halves(I("W_D")[:, None]))
    put("outT", halves(I("out_w").T))
    put("big", np.full((P, 32), BIG, np.float32))
    I = lambda n: np.asarray(inp["L0_xattn_" + n])
    for n in ("Wq", "Wk", "Wv", "Wo"):
        put(n, I(n))
    put("bq", I("bq")[:, None])
    put("bk", I("bk")[:, None])
    put("bv", I("bv")[:, None])
    put("bo", I("bo")[None, :])
    put("headrow", (np.arange(P)[:, None] // DK % HG == np.arange(HG)[None, :]).astype(np.float32))
    put("ones", np.ones((1, P), np.float32))
    I = lambda n: np.asarray(inp["L1_attn_" + n])
    for l in range(2):
        put(f"sW{l}", I(f"W{l}").T)
        put(f"sR{l}", I(f"R{l}").T)
        put(f"sb{l}", I(f"b{l}").reshape(GATES, P).T)
        put(f"sP{l}", I(f"projW{l}").T)
        put(f"spb{l}", I(f"projb{l}")[:, None])
        put(f"sga{l}", I(f"gamma{l}")[:, None])
        put(f"sbe{l}", I(f"beta{l}")[:, None])
    for n in ("Wq", "Wk", "Wv"):
        put(n + "1", np.asarray(inp["L1_xattn_" + n]).T)
    same = np.arange(P)[:, None] // S == np.arange(P)[None, :] // S
    put("same", same.astype(np.float32))
    put("lowrow", np.where(same, np.float32(FILL), np.float32(-1.0e30)))
    put("gate0", np.asarray(inp["L0_ffn_gate_w"]).T)
    put("gateb0", np.broadcast_to(np.asarray(inp["L0_ffn_gate_b"])[None, :], (P, NX)))
    put("gate1", inp["L1_ffn_Wg"])
    put("eidx", np.broadcast_to(np.arange(NX, dtype=np.float32)[None, :], (P, NX)))
    put("before", np.triu(np.ones((P, P), np.float32), 1))
    put("allones", np.ones((P, P), np.float32))
    put("onerow", np.ones((P, NT), np.float32))
    put("spare", (np.arange(NT)[None, :] * P + np.arange(P)[:, None] + (TILES + 1) * P).astype(np.float32))
    put("tileidx", np.broadcast_to(np.arange(TILES + 1, dtype=np.float32)[None, :], (P, TILES + 1)))
    put("garow", np.broadcast_to(I("gamma1")[None, :], (P, D)))
    put("berow", np.broadcast_to(I("beta1")[None, :], (P, D)))
    return arr


def relative(rel_bias):
    rel = np.asarray(rel_bias)
    span = rel.shape[1] // 2
    at = np.arange(S)[:, None] - np.arange(S)[None, :] + span
    one = rel[:, at].transpose(1, 0, 2)
    return np.ascontiguousarray(np.concatenate([one, one], axis=0))


def selectors():
    s = np.zeros((P, 2 * NS, P), mybir.dt.np(BF16))
    for q in (0, 2, 3):
        for n in range(2 * NS):
            s[32 * q + n, n, :] = 1
    return s


def kernel(**inputs):
    import concourse.bacc as bacc
    from concourse.bass_utils import run_bass_kernel_spmd as run

    nc = bacc.Bacc("TRN2", target_bir_lowering=False, num_devices=1)
    arrays = {"x": np.ascontiguousarray(np.asarray(inputs["x"]).reshape(T, D)), "packed": pack(inputs), "sel": selectors()}
    arrays["ctxT"] = np.ascontiguousarray(np.asarray(inputs["ctx_1024"]).reshape(T, D).T)
    arrays["bias"] = relative(inputs["L0_xattn_rel_bias"])
    arrays["mask8"] = np.ascontiguousarray(np.asarray(inputs["mask_BxS2_bf0"]).view(np.uint8).reshape(NT, 2, S).transpose(1, 0, 2).reshape(2, T // 2)).view(np.int32)
    arrays["pairsel"] = np.repeat(np.eye(2), S, axis=1).astype(mybir.dt.np(BF16))
    arrays["mask1"] = np.ascontiguousarray(np.asarray(inputs["mask_BxS2_ik1"]).reshape(NT, 2 * S))
    I = lambda n: np.asarray(inputs[n])
    for l, F in ((0, 512), (1, 256)):
        w1, w2 = (I("L0_ffn_w1"), I("L0_ffn_w2")) if l == 0 else (I("L1_ffn_W1"), I("L1_ffn_W2"))
        arrays[f"w1_{l}"] = np.ascontiguousarray(w1.transpose(1, 0, 2).reshape(P, NX * F))
        arrays[f"w2_{l}"] = np.ascontiguousarray(w2.reshape(NX, F // P, P, D).transpose(2, 0, 1, 3).reshape(P, NX * F))
    arrays["b1_0"] = np.ascontiguousarray(np.broadcast_to(I("L0_ffn_b1").reshape(1, -1), (P, NX * 512)))
    arrays["b2_0"] = np.ascontiguousarray(np.broadcast_to(I("L0_ffn_b2").reshape(1, -1), (P, NX * D)))
    arrays["owner0"] = np.minimum(np.arange(TILES + 1) // (CAP // P), NX - 1).astype(np.int32)[None, :]
    arrays["bits"] = np.ascontiguousarray(np.broadcast_to((1 << np.arange(BITS - 1, -1, -1)).astype(np.int32)[None, :], (P, BITS)))
    ap = {n: nc.dram_tensor("in_" + n, a.shape, mybir.dt.from_np(a.dtype), kind="ExternalInput").ap() for n, a in arrays.items()}
    out = nc.dram_tensor("out_0_dram", (T, D), F32, kind="ExternalOutput").ap()
    moe0 = {"w1": ap["w1_0"], "w2": ap["w2_0"], "b1": ap["b1_0"], "b2": ap["b2_0"], "owner": ap["owner0"]}
    moe1 = {"w1": ap["w1_1"], "w2": ap["w2_1"]}
    program(nc, ap["x"], ap["packed"], ap["sel"], ap["ctxT"], ap["bias"], ap["mask8"], ap["pairsel"], moe0, moe1, ap["bits"], ap["mask1"], out)
    r = run(nc, [{"in_" + n: a for n, a in arrays.items()}], core_ids=[0])
    return r.results[0]["out_0_dram"].reshape(B, S, D)
```

```python
from contextlib import ExitStack

import numpy as np

import concourse.bass as bass
from concourse import mybir

ALU = mybir.AluOpType
ACT = mybir.ActivationFunctionType
F32 = mybir.dt.float32
BF16 = mybir.dt.bfloat16
I32 = mybir.dt.int32
U32 = mybir.dt.uint32
AX_X = mybir.AxisListType.X

P = 128
B, S, D = 64, 64, 128
T = B * S
NT = T // P
CH = 512
NC = T // CH
TPC = CH // P
BPC = CH // S
E0 = 256
NS = 16
DD = 64
KC = 4
EPS = 1e-5
BIG = 1.0e30



class Core:
    pass


class Chain:

    def __init__(self, eng, sem):
        self.eng, self.sem, self.n = eng, sem, 0
        self.i, self.per = None, 0

    def enter(self, i, per):
        self.i, self.per, self.base, self.n = i, per, self.n, 0

    def leave(self, times):
        assert self.n == self.per, (self.n, self.per)
        self.n, self.i = self.base + times * self.per, None

    def value(self):
        return self.n if self.i is None else self.i * self.per + (self.base + self.n)

    def inc(self, ins):
        ins.then_inc(self.sem, 1)
        self.n += 1

    def link(self, ins):
        self.inc(ins)
        self.eng.wait_ge(self.sem, self.value())


def alone(eng):
    eng.nop(nofuse=True)


def sem_maker(nc, ctx, tag):
    made = []

    def clear():
        for s in made:
            nc.sync.sem_clear(s)
        nc.all_engine_barrier()

    ctx.callback(clear)

    def make(name):
        made.append(ctx.enter_context(nc.semaphore(f"{tag}_{name}")))
        return made[-1]

    return make


def norm_stage(nc, g, tag, rms=False, gain=None, keep=False, place=None, fetch=None):
    with ExitStack() as ctx:
        sem = sem_maker(nc, ctx, tag)
        sb = lambda name, shape, dt=F32: ctx.enter_context(nc.sbuf_tensor(f"{tag}_{name}", shape, dt))
        stat, vchain, var_ready, rstd_ready = sem("stat"), sem("vchain"), sem("var_ready"), sem("rstd_ready")
        rows_ready, turned, evac, kept, centred = sem("rows_ready"), sem("turned"), sem("evac"), sem("kept"), sem("centred")
        square_ready, rr_ready = sem("square_ready"), sem("rr_ready")
        R = 4
        PARTS = 4
        PT = NT // PARTS
        st = sb("st", [P, NT, 6])
        a, b, mean, var, rstd, rr = (sb(n, [P, NT]) for n in ("a", "b", "mean", "var", "rstd", "rr"))
        xc = sb("xc", [P, R, TPC, D])
        xr = sb("xr", [P, R, TPC, D])
        rows = lambda c: g.rows[:, c * TPC:(c + 1) * TPC, :] if keep else xr[:, c % R]
        with nc.Block() as block:

            if fetch is not None:
                @block.sync
                def _(sp):
                    fetch(sp)

            @block.vector
            def _(ve):
                ch = Chain(ve, vchain)

                def moments(part):
                    h = slice(part * PT, (part + 1) * PT)
                    for t in range(part * PT, (part + 1) * PT):
                        ve.bn_stats(st[:, t, :], g.X[:, t, :]).then_inc(stat, 1)
                    ve.wait_ge(stat, (part + 1) * PT)
                    ch.inc(ve.tensor_tensor(b[:, h], st[:, h, 1], st[:, h, 4], ALU.subtract))
                    ch.inc(ve.tensor_tensor(a[:, h], st[:, h, 1], st[:, h, 4], ALU.add))
                    ch.link(ve.tensor_tensor(var[:, h], st[:, h, 2], st[:, h, 5], ALU.add))
                    ch.link(ve.scalar_tensor_tensor(b[:, h], b[:, h], 0.25, b[:, h], ALU.mult, ALU.mult))
                    ch.inc(ve.tensor_scalar(mean[:, h], a[:, h], 0.5, None, ALU.mult))
                    ch.link(ve.scalar_tensor_tensor(var[:, h], var[:, h], 1.0 / D, b[:, h], ALU.mult, ALU.add))
                    ve.tensor_scalar(a[:, h], var[:, h], EPS, None, ALU.add).then_inc(var_ready, 1)

                def square(part):
                    h = slice(part * PT, (part + 1) * PT)
                    ve.wait_ge(rstd_ready, part + 1)
                    ch.link(ve.tensor_tensor(b[:, h], rstd[:, h], rstd[:, h], ALU.mult))
                    ch.link(ve.tensor_tensor(b[:, h], b[:, h], var[:, h], ALU.mult))
                    ve.tensor_scalar(b[:, h], b[:, h], EPS, None, ALU.add).then_inc(square_ready, 1)

                def normalise(part):
                    for c in range(part * PT // TPC, (part + 1) * PT // TPC):
                        k = c % R
                        if c % (PT // TPC) == 0:
                            ve.wait_ge(rr_ready if rms else rstd_ready, part + 1)
                        if c >= R:
                            ve.wait_ge(turned, c - R + 1)
                            if rms:
                                ve.wait_ge(kept, c - R + 1)
                        for j in range(TPC):
                            t = c * TPC + j
                            ins = ve.tensor_scalar((xc[:, k] if rms else rows(c))[:, j, :], g.X[:, t, :], mean[:, t:t + 1], rstd[:, t:t + 1],
                                                   ALU.subtract, ALU.mult)
                        if not rms:
                            ins.then_inc(rows_ready, 1)
                        else:
                            ins.then_inc(centred, 1)
                            ve.wait_ge(centred, c + 1)
                            over = rr[:, c * TPC:(c + 1) * TPC].rearrange("p (a o) -> p a o", o=1).broadcast_to([P, TPC, D])
                            ve.tensor_tensor(rows(c), xc[:, k], over, ALU.mult).then_inc(rows_ready, 1)

                moments(0)
                for part in range(PARTS):
                    if part + 1 < PARTS:
                        moments(part + 1)
                    if rms:
                        square(part)
                        if part >= 1:
                            normalise(part - 1)
                    else:
                        normalise(part)
                if rms:
                    normalise(PARTS - 1)

            @block.gpsimd
            def _(pool):
                def root(part):
                    h = slice(part * PT, (part + 1) * PT)
                    pool.wait_ge(var_ready, part + 1)
                    pool.tensor_tensor(rstd[:, h], a[:, h], g.neghalf[:, h], ALU.pow).then_inc(rstd_ready, 1)

                def root_of_square(part):
                    h = slice(part * PT, (part + 1) * PT)
                    pool.wait_ge(square_ready, part + 1)
                    pool.tensor_tensor(rr[:, h], b[:, h], g.neghalf[:, h], ALU.pow).then_inc(rr_ready, 1)

                def add_residual(part):
                    for c in range(part * PT // TPC, (part + 1) * PT // TPC):
                        tiles = slice(c * TPC, (c + 1) * TPC)
                        pool.wait_ge(centred, c + 1)
                        pool.tensor_tensor(g.X[:, tiles, :], g.X[:, tiles, :], xc[:, c % R], ALU.add).then_inc(kept, 1)

                root(0)
                for part in range(PARTS):
                    if part + 1 < PARTS:
                        root(part + 1)
                    if rms:
                        root_of_square(part)
                        add_residual(part)

            @block.tensor
            def _(pe):
                for c in range(NC):
                    pe.wait_ge(rows_ready, c + 1)
                    if c >= R:
                        pe.wait_ge(evac, c - R + 1)
                    for j in range(TPC):
                        ins = pe.transpose(g.bank[c % R][:, j * P:(j + 1) * P], rows(c)[:, j, :], g.ident[:])
                    ins.then_inc(turned, 1)

            @block.scalar
            def _(act):
                for c in range(NC):
                    act.wait_ge(turned, c + 1)
                    out = place(c) if place else g.xT[:, c * CH:(c + 1) * CH]
                    src = g.bank[c % R] if place is None else g.bank[c % R].rearrange("p (b s) -> p b s", s=S)
                    act.activation(out, src, ACT.Identity, scale=gain if gain is not None else 1.0).then_inc(evac, 1)


def scan_stage(nc, g):
    H = E0 // P
    tag = "scan"
    norm_stage(nc, g, "n0", rms=True, gain=g.w("norm_w"), fetch=g.fetch_weights)
    with ExitStack() as ctx:
        sem = sem_maker(nc, ctx, tag)
        sb = lambda name, shape, dt=F32: ctx.enter_context(nc.sbuf_tensor(f"{tag}_{name}", shape, dt))
        xs = sb("xs", [P, H, T])
        delta = sb("delta", [P, H, T])
        parts = sb("parts", [P, T], BF16)
        sel = sb("sel", [P, 2 * NS, P], BF16)
        negA = sb("negA", [P, H * NS])
        sel_in = sem("sel_in")

        with ExitStack() as c2:
            sem2 = sem_maker(nc, c2, "proj")
            wk = c2.enter_context(nc.sbuf_tensor("proj_wk", [P, KC, E0], F32))
            scaled, conv, silu, vch = sem2("scaled"), sem2("conv"), sem2("silu"), sem2("vch")
            exped, negd = sem2("exped"), sem2("negd")
            with nc.Block() as block:

                @block.sync
                def _(sp):
                    sp.dma_start(sel[:], g.sel_dram).then_inc(sel_in, 16)

                @block.vector
                def _(ve):
                    for k in range(KC):
                        ve.tensor_tensor(wk[:, k, :], g.w("inT"), g.w("convrow")[:, k * E0:(k + 1) * E0], ALU.mult).then_inc(scaled, 1)
                    ve.wait_ge(exped, 1)
                    ve.tensor_scalar(negA[:], negA[:], -1.0, None, ALU.mult).then_inc(negd, 1)
                    ve.wait_ge(sel_in, 16)

                @block.tensor
                def _(pe):
                    pe.wait_ge(scaled, KC)
                    with pe.Fori(0, NC) as c:
                        for h in range(H):
                            pe.wait_ge(silu, c * H + (h + 1))
                            for k in range(KC):
                                out = g.bank[h][:].rearrange("p (b s) -> p b s", s=S)[:, :, k:S]
                                src = g.xT[:, bass.ts(c, CH)].rearrange("p (b s) -> p b s", s=S)[:, :, 0:S - k]
                                ins = pe.matmul(out, wk[:, KC - 1 - k, h * P:(h + 1) * P], src,
                                                start=(k == 0), stop=(k == KC - 1), skip_group_check=True)
                            ins.then_inc(conv, 1)

                @block.scalar
                def _(act):
                    act.activation(negA[:], g.w("A_log"), ACT.Exp).then_inc(exped, 1)
                    act.sem_inc(silu, H)
                    act.preload_act_table(ACT.Silu)
                    with act.Fori(0, NC) as c:
                        for h in range(H):
                            act.wait_ge(conv, c * H + (h + 1))
                            act.activation(xs[:, h, bass.ts(c, CH)], g.bank[h][:], ACT.Silu,
                                           bias=g.w("conv_b")[:, h:h + 1]).then_inc(silu, 1)

        with ExitStack() as c2:
            sem2 = sem_maker(nc, c2, "dl")
            t1 = c2.enter_context(nc.sbuf_tensor("dl_t1", [DD, 2, CH], F32))
            xb = c2.enter_context(nc.sbuf_tensor("dl_xb", [P, H, CH], F32))
            lg = c2.enter_context(nc.sbuf_tensor("dl_lg", [P, H, CH], F32))
            res = c2.enter_context(nc.sbuf_tensor("dl_res", [P, CH], F32))
            d1, d1c, d2, bc, clampd, ex, ln_, dl, vch = (sem2(n) for n in ("d1", "d1c", "d2", "bc", "clampd", "ex", "ln", "dl", "vch"))
            with nc.Block() as block:

                @block.tensor
                def _(pe):
                    with pe.Fori(0, NC) as c:
                        pe.wait_ge(d1c, c + 1)
                        for h in range(H):
                            ins = pe.matmul(g.bank[0][0:DD, :], g.w("wd1T")[:, h * DD:(h + 1) * DD], xs[:, h, bass.ts(c, CH)],
                                            start=(h == 0), stop=(h == H - 1))
                        ins.then_inc(d1, 1)
                        pe.wait_ge(vch, c * 6 + 6)
                        for h in range(H):
                            ins = pe.matmul(g.bank[3][:], g.w("wbcT")[:, h * P:(h + 1) * P], xs[:, h, bass.ts(c, CH)],
                                            start=(h == 0), stop=(h == H - 1))
                        ins.then_inc(bc, 1)
                        pe.wait_ge(d1c, c + 2)
                        pe.wait_ge(dl, c + 1)
                        for h in range(H):
                            ins = pe.matmul(g.bank[1 + h][:], g.w("wd2T")[0:DD, h * P:(h + 1) * P], t1[:, 0, :], start=True, stop=True)
                        ins.then_inc(d2, 1)

                @block.scalar
                def _(act):
                    act.sem_inc(d1c, 1)
                    act.preload_act_table_set("natural_log_exp_and_others")
                    with act.Fori(0, NC) as c:
                        act.wait_ge(d1, c + 1)
                        act.wait_ge(d2, c)
                        act.activation(t1[:, 0, :], g.bank[0][0:DD, :], ACT.Copy).then_inc(d1c, 1)
                        act.wait_ge(clampd, c + 1)
                        act.activation(xb[:], xb[:], ACT.Exp).then_inc(ex, 1)
                        act.wait_ge(ex, c + 1)
                        act.activation(lg[:], xb[:], ACT.Ln, bias=1.0).then_inc(ln_, 1)

                @block.vector
                def _(ve):
                    ve.sem_inc(vch, 6)
                    ve.sem_inc(dl, 1)
                    with ve.Fori(0, NC) as c:
                        ve.wait_ge(bc, c + 1)
                        cs = bass.ts(c, CH)
                        steps = (
                            lambda: ve.tensor_copy(parts[:, cs], g.bank[3][:]),
                            lambda: ve.tensor_tensor(res[:], g.bank[3][:], parts[:, cs], ALU.subtract),
                            lambda: ve.tensor_copy(parts[64:128, cs], res[64:128, :]),
                            lambda: ve.tensor_tensor(res[96:128, :], res[96:128, :], parts[96:128, cs], ALU.subtract),
                            lambda: ve.tensor_copy(parts[96:128, cs], res[96:128, :]),
                        )
                        for k, f in enumerate(steps):
                            alone(ve)
                            f().then_inc(vch, 1)
                            ve.wait_ge(vch, c * 6 + (7 + k))
                        ve.wait_ge(d2, c + 1)
                        for h in range(H):
                            ins = ve.tensor_scalar(xb[:, h, :], g.bank[1 + h][:], g.w("wd2_b")[:, h:h + 1], 40.0, ALU.add, ALU.min)
                            if h == 0:
                                ins.then_inc(vch, 1)
                        ins.then_inc(clampd, 1)
                        ve.wait_ge(ln_, c + 1)
                        for h in range(H):
                            ins = ve.scalar_tensor_tensor(delta[:, h, cs], g.bank[1 + h][:], g.w("wd2_b")[:, h:h + 1],
                                                          lg[:, h, :], ALU.add, ALU.max)
                        ins.then_inc(dl, 1)

        with ExitStack() as c2:
            sem2 = sem_maker(nc, c2, "rec")
            sb2 = lambda name, shape, dt=F32: c2.enter_context(nc.sbuf_tensor(f"rec_{name}", shape, dt))
            SR, LR = 2, 4
            dx = sb2("dx", [P, H, CH])
            dec = sb2("dec", [P, SR, H * CH])
            u = sb2("u", [P, SR, H * CH])
            hst = sb2("hst", [P, SR, H * CH])
            hc = sb2("hc", [P, LR, H * CH])
            cb = sb2("cb", [P, LR, CH])
            bank_b, bank_c, bank_y = g.bank[0:2], g.bank[2:6], g.bank[6:8]
            bready, cready, decay, ccopy, uready, hready, hcready, summed, dxr, reset, yout = (
                sem2(n) for n in ("bready", "cready", "decay", "ccopy", "uready", "hready", "hcready", "summed", "dxr", "reset", "yout"))
            three = lambda t: t.rearrange("p (h t) -> p h t", h=H)
            over_h = lambda t: t.rearrange("p (o t) -> p o t", o=1).broadcast_to([P, H, CH])
            with nc.Block() as block:

                @block.tensor
                def _(pe):
                    LEAD = 3
                    pe.sem_inc(summed, LR)

                    def broadcasts(c, n):
                        pe.wait_ge(uready, c * NS + (n + 1))
                        pe.matmul(bank_b[n % SR], sel[:, n, :], parts[:, bass.ts(c, CH)], start=True, stop=True).then_inc(bready, 1)
                        pe.wait_ge(ccopy, c * NS + (n + 1))
                        pe.matmul(bank_c[n % LR], sel[:, NS + n, :], parts[:, bass.ts(c, CH)], start=True, stop=True).then_inc(cready, 1)

                    def chunk(c, last):
                        for n in range(NS):
                            if n + LEAD < NS:
                                broadcasts(c, n + LEAD)
                            elif not last:
                                broadcasts(c + 1, n + LEAD - NS)
                            if n == 0:
                                pe.wait_ge(yout, c + 1)
                            pe.wait_ge(hcready, c * NS + (n + 1 + LR))
                            for h in range(H):
                                ins = pe.matmul(bank_y[h], g.ident, hc[:, n % LR, h * CH:(h + 1) * CH], start=(n == 0), stop=(n == NS - 1))
                            ins.then_inc(summed, 1)

                    for n in range(LEAD):
                        broadcasts(0, n)
                    with pe.Fori(0, NC - 1) as c:
                        chunk(c, False)
                    chunk(NC - 1, True)

                @block.scalar
                def _(act):
                    act.sem_inc(ccopy, LR)
                    act.preload_act_table(ACT.Exp)
                    with act.Fori(0, NC) as c:
                        act.wait_ge(reset, c + 1)
                        for n in range(NS):
                            act.wait_ge(hready, c * NS + (n + 1))
                            alone(act)
                            for h in range(H):
                                ins = act.activation(dec[:, n % SR, h * CH:(h + 1) * CH], delta[:, h, bass.ts(c, CH)],
                                                     ACT.Exp, scale=negA[:, h * NS + n:h * NS + n + 1])
                            ins.then_inc(decay, 1)
                            act.wait_ge(cready, c * NS + (n + 1))
                            act.wait_ge(hcready, c * NS + (n + 1))
                            act.activation(cb[:, n % LR, :], bank_c[n % LR], ACT.Copy).then_inc(ccopy, 1)

                @block.vector
                def _(ve):
                    ve.sem_inc(uready, SR)
                    ve.sem_inc(hready, SR)
                    ve.sem_inc(yout, 1)

                    def prepare(c):
                        ve.wait_ge(uready, c * NS + SR)
                        ve.tensor_tensor(dx[:], delta[:, :, bass.ts(c, CH)], xs[:, :, bass.ts(c, CH)], ALU.mult).then_inc(dxr, 1)
                        ve.wait_ge(dxr, c + 1)
                        alone(ve)
                        ve.tensor_copy(delta[:, :, bass.ts(c, CH)].rearrange("p h (b s) -> p h b s", s=S)[:, :, :, 0],
                                       g.w("big")[:, 0:H * BPC].rearrange("p (h b) -> p h b", h=H)).then_inc(reset, 1)

                    def form_u(c, n):
                        ve.wait_ge(bready, c * NS + (n + 1))
                        ve.wait_ge(hready, c * NS + (n + 1))
                        ve.tensor_tensor(three(u[:, n % SR, :]), dx[:], over_h(bank_b[n % SR]), ALU.mult).then_inc(uready, 1)

                    def scan(c, n, last=False):
                        if n + 1 < NS:
                            form_u(c, n + 1)
                        elif not last:
                            prepare(c + 1)
                            form_u(c + 1, 0)
                        ve.wait_ge(decay, c * NS + (n + 1))
                        ve.wait_ge(uready, c * NS + (n + 1 + SR))
                        ve.wait_ge(hcready, c * NS + (n + 1 + LR - SR))
                        ve.tensor_tensor_scan(hst[:, n % SR, :], dec[:, n % SR, :], u[:, n % SR, :], 0.0,
                                              ALU.mult, ALU.add).then_inc(hready, 1)

                    def read_out(c):
                        ve.wait_ge(summed, c * NS + (NS + LR))
                        for h in range(H):
                            ins = ve.scalar_tensor_tensor(xs[:, h, bass.ts(c, CH)], xs[:, h, bass.ts(c, CH)],
                                                          g.w("W_D")[:, h:h + 1], bank_y[h], ALU.mult, ALU.add)
                        ins.then_inc(yout, 1)

                    AHEAD = 2
                    prepare(0)
                    form_u(0, 0)
                    for n in range(AHEAD):
                        scan(0, n)
                    with ve.Fori(0, NC - 1) as c:
                        for n in range(AHEAD, NS):
                            scan(c, n)
                        for n in range(AHEAD):
                            scan(c + 1, n)
                        read_out(c)
                    for n in range(AHEAD, NS):
                        scan(NC - 1, n, last=True)
                    read_out(NC - 1)

                @block.gpsimd
                def _(pool):
                    pool.sem_inc(hcready, LR)
                    with pool.Fori(0, NC) as c:
                        for n in range(NS):
                            pool.wait_ge(hready, c * NS + (n + 1 + SR))
                            pool.wait_ge(ccopy, c * NS + (n + 1 + LR))
                            pool.wait_ge(summed, c * NS + (n + 1))
                            pool.tensor_tensor(three(hc[:, n % LR, :]), three(hst[:, n % SR, :]), over_h(cb[:, n % LR, :]), ALU.mult).then_inc(hcready, 1)

        with ExitStack() as c2:
            sem2 = sem_maker(nc, c2, "go")
            gate = c2.enter_context(nc.sbuf_tensor("go_gate", [P, H, CH], F32))
            yg = c2.enter_context(nc.sbuf_tensor("go_yg", [P, H, CH], F32))
            skip, gated, mult, proj, added = (sem2(n) for n in ("skip", "gated", "mult", "proj", "added"))
            with nc.Block() as block:

                @block.tensor
                def _(pe):
                    with pe.Fori(0, NC) as c:
                        pe.wait_ge(gated, c * H)
                        for h in range(H):
                            pe.matmul(g.bank[h][:], g.w("skipT")[:, h * P:(h + 1) * P], g.xT[:, bass.ts(c, CH)],
                                      start=True, stop=True).then_inc(skip, 1)
                        pe.wait_ge(mult, c + 1)
                        pe.wait_ge(added, c)
                        for j in range(TPC):
                            for h in range(H):
                                ins = pe.matmul(g.bank[2][:, j * P:(j + 1) * P], yg[:, h, j * P:(j + 1) * P],
                                                g.w("outT")[:, h * D:(h + 1) * D], start=(h == 0), stop=(h == H - 1))
                        ins.then_inc(proj, 1)

                @block.scalar
                def _(act):
                    act.preload_act_table(ACT.Silu)
                    with act.Fori(0, NC) as c:
                        act.wait_ge(mult, c)
                        for h in range(H):
                            act.wait_ge(skip, c * H + (h + 1))
                            act.activation(gate[:, h, :], g.bank[h][:], ACT.Silu).then_inc(gated, 1)

                @block.vector
                def _(ve):
                    with ve.Fori(0, NC) as c:
                        ve.wait_ge(gated, c * H + H)
                        ve.wait_ge(added, c)
                        ve.tensor_tensor(yg[:], xs[:, :, bass.ts(c, CH)], gate[:], ALU.mult).then_inc(mult, 1)
                        ve.wait_ge(proj, c + 1)
                        xc = g.X[:, bass.ts(c, TPC), :].rearrange("p a d -> p (a d)")
                        ve.tensor_tensor(xc, xc, g.bank[2][:], ALU.add).then_inc(added, 1)


NH, DK = 16, 8
HG = 4
NG = NH // HG
VW = 2 * (DK + 1)


def cross_stage(nc, g):
    def fetch(sp):
        sp.dma_start(g.ctxT[:], g.ctxT_dram).then_inc(g.ctxT_in, 16)
        sp.wait_ge(g.ctxT_in, 16)
        sp.wait_ge(g.late_in, 32)

    norm_stage(nc, g, "n1", fetch=fetch)
    with ExitStack() as ctx:
        sem = sem_maker(nc, ctx, "ca")
        sb = lambda name, shape, dt=F32: ctx.enter_context(nc.sbuf_tensor(f"ca_{name}", shape, dt))
        R = 2
        qg = sb("qg", [P, R, NG, CH])
        kd = sb("kd", [P, R, BPC, HG, S])
        vT = sb("vT", [P, R, BPC, 2, S])
        vd = sb("vd", [P, R, BPC, NH // 2, VW])
        bias = sb("bias", [P, NH, S])
        mask8 = sb("mask8", [2, T // 8], I32)
        maskneg = sb("maskneg", [2, NT, S], BF16)
        kbias = sb("kbias", [P, HG])
        qbias = sb("qbias", [P, 1])
        sc = sb("sc", [P, 2, NH, S])
        pr = sb("pr", [P, 2, NH * S])
        mx = sb("mx", [P, 2, NH])
        pT = sb("pT", [P, 2, NH // 2, P])
        ri = sb("ri", [P, 2, NH])
        o = sb("o", [P, 2, D])
        oT = sb("oT", [P, 2, D])
        bias_in, init, kb = sem("bias_in"), sem("init"), sem("kb")
        with nc.Block() as block:

            @block.sync
            def _(sp):
                sp.dma_start(bias[:], g.bias_dram).then_inc(bias_in, 16)
                sp.dma_start(mask8[:], g.mask8_dram).then_inc(bias_in, 16)
                sp.wait_ge(bias_in, 32)

            @block.gpsimd
            def _(pool):
                pool.memset(qg[:], 0.0).then_inc(init, 1)
                pool.memset(vd[:], 0.0).then_inc(init, 1)
                pool.wait_ge(init, 2)
                for h2 in range(2):
                    col = h2 * (DK + 1) + DK
                    pool.memset(vd[h2 * S:(h2 + 1) * S, :, :, :, col:col + 1].rearrange("p r b j o -> p (r b j) o"), 1.0).then_inc(init, 1)

            @block.vector
            def _(ve):
                ve.tensor_scalar(qbias[:], g.w("bq"), DK ** -0.5, None, ALU.mult).then_inc(kb, 1)
                ve.tensor_scalar(kbias[:], g.w("headrow"), g.w("bk"), None, ALU.mult).then_inc(kb, 1)
                ve.wait_ge(bias_in, 32)
                ve.tensor_scalar(maskneg[:], mask8[:].bitcast(mybir.dt.uint8).rearrange("a (n k) -> a n k", k=S), -1.0e30, None, ALU.mult).then_inc(kb, 1)

        proj, qkv, vt, vcopy = sem("proj"), sem("qkv"), sem("vt"), sem("vcopy")
        scored, biased, maxed, shifted, exped, turned, tcopy, pv, rinv, normed, oturned, ocopy, outp, added = (
            sem(n) for n in ("scored", "biased", "maxed", "shifted", "exped", "turned", "tcopy", "pv", "rinv", "normed",
                             "oturned", "ocopy", "outp", "added"))
        PPC = BPC // 2
        bank_s = [g.ps[:, 1:3, :], g.ps[:, 3:5, :]]
        bank_t = g.ps[:, 5:7, :]
        bank_o = g.bank[7]
        T_AT, F_AT = 2 * P, 3 * P
        bank_p = g.bank[0]
        LEAD = 2

        def run(eng, slot):
            slot(0, 0, 0, True, False)
            with eng.Fori(0, NC // R - 1) as i:
                for k in range(1, R * PPC + 1):
                    slot(i * R + k // PPC, k // PPC % R, k % PPC, False, False)
            for k in range(1, R * PPC):
                slot(NC - R + k // PPC, k // PPC % R, k % PPC, False, k // PPC == R - 1)

        with nc.Block() as block:

            @block.tensor
            def _(pe):
                def project(c, k):
                    w, src = (("Wq", g.xT), ("Wk", g.ctxT), ("Wv", g.ctxT))[k]
                    if k == 0:
                        pe.wait_ge(vcopy, c * 2 + 1)
                    else:
                        pe.wait_ge(qkv, c * 3 + k)
                    pe.matmul(bank_p, g.w(w), src[:, bass.ts(c, CH)], start=True, stop=True).then_inc(proj, 1)

                def turn_v(c, r, q):
                    if q == 0:
                        pe.wait_ge(qkv, c * 3 + 3)
                    else:
                        pe.wait_ge(vcopy, c * 2 + 2)
                    for b in range(4):
                        ins = pe.transpose(bank_p[:, b * P:(b + 1) * P], vT[:, r, q * 4 + b].rearrange("p o k -> p (o k)"), g.ident)
                    ins.then_inc(vt, 1)

                def scores(c, r, p, b):
                    n = c * PPC + p
                    sbk = bank_s[p % 2]
                    if b == 0:
                        if p == 0:
                            pe.wait_ge(qkv, c * 3 + 2)
                        pe.wait_ge(biased, n + 1)
                        for k in range(2):
                            m = maskneg[:, bass.ds(n, 1), :].broadcast_to([2, NH // 2, S])
                            pe.matmul(sbk[:, k, :], g.pairsel[:], m, start=True, stop=False, skip_group_check=True)
                    for gr in range(NG):
                        ins = pe.matmul(sbk[b * S:(b + 1) * S, gr // 2, gr % 2 * 256:gr % 2 * 256 + 256],
                                        qg[:, r, gr, (2 * p + b) * S:(2 * p + b + 1) * S], kd[:, r, 2 * p + b, :, :],
                                        start=False, stop=True, skip_group_check=True)
                    if b == 1:
                        ins.then_inc(scored, 1)

                def turn_probs(c, p):
                    n = c * PPC + p
                    pe.wait_ge(exped, n + 1)
                    pe.wait_ge(tcopy, n + 1)
                    for j in range(NH // 2):
                        ins = pe.transpose(bank_t[:, j // 4, j % 4 * P:(j % 4 + 1) * P], pr[:, p % 2, j * P:(j + 1) * P], g.ident)
                    ins.then_inc(turned, 1)

                def values(c, r, p):
                    n = c * PPC + p
                    pe.wait_ge(tcopy, n + 2)
                    pe.wait_ge(added, n + 1)
                    if p == 0:
                        pe.wait_ge(vcopy, c * 2 + 3)
                    for b in range(2):
                        for j in range(NH // 2):
                            ins = pe.matmul(bank_o[b * S:(b + 1) * S, j * VW:(j + 1) * VW],
                                            pT[:, p % 2, j, b * S:(b + 1) * S], vd[:, r, 2 * p + b, j, :], start=True, stop=True)
                    ins.then_inc(pv, 1)

                def turn_out(n, q):
                    pe.wait_ge(normed, n + 1)
                    pe.transpose(bank_o[:, T_AT:T_AT + P], o[:, q, :], g.ident).then_inc(oturned, 1)

                def output(n, q):
                    pe.wait_ge(ocopy, n + 1)
                    pe.matmul(bank_o[:, F_AT:F_AT + D], oT[:, q, :], g.w("Wo"), start=True, stop=False)
                    pe.matmul(bank_o[:, F_AT:F_AT + D], g.w("ones")[0:1, :], g.w("bo")[0:1, :], start=False, stop=True).then_inc(outp, 1)

                def slot(c, r, p, first, last):
                    before, q = c * PPC + (p - 1), (p - 1) % 2
                    more = not last or p + LEAD < PPC
                    ahead = (c, r, p + LEAD) if p + LEAD < PPC else (c + 1, 1 - r, p + LEAD - PPC)
                    turn_probs(c, p)
                    if more:
                        scores(*ahead, 0)
                    if not first:
                        turn_out(before, q)
                    if not last:
                        if p < 3:
                            project(c + 1, p)
                        else:
                            turn_v(c + 1, 1 - r, 0)
                    if not first:
                        output(before, q)
                    if more:
                        scores(*ahead, 1)
                    values(c, r, p)
                    if not last and p == 3:
                        turn_v(c + 1, 1 - r, 1)

                for k in range(3):
                    project(0, k)
                for q in range(2):
                    turn_v(0, 0, q)
                for p in range(LEAD):
                    scores(0, 0, p, 0)
                    scores(0, 0, p, 1)
                run(pe, slot)
                turn_out(NC * PPC - 1, 1)
                output(NC * PPC - 1, 1)

            @block.scalar
            def _(act):
                act.sem_inc(vcopy, 1)
                act.sem_inc(tcopy, 1)
                act.preload_act_table(ACT.Exp)

                def take_q(c, r):
                    act.wait_ge(proj, c * 3 + 1)
                    for gr in range(NG):
                        rows = slice(32 * gr, 32 * gr + 32)
                        ins = act.activation(qg[rows, r, gr, :], bank_p[rows, :], ACT.Identity, bias=qbias[rows, :], scale=DK ** -0.5)
                    ins.then_inc(qkv, 1)

                def take_k(c, r):
                    act.wait_ge(proj, c * 3 + 2)
                    for h in range(HG):
                        ins = act.activation(kd[:, r, :, h, :], bank_p.rearrange("p (b k) -> p b k", k=S), ACT.Identity,
                                             bias=kbias[:, h:h + 1], scale=g.w("headrow")[:, h:h + 1])
                    ins.then_inc(qkv, 1)

                def take_v(c, r):
                    act.wait_ge(proj, c * 3 + 3)
                    act.activation(vT[:, r], bank_p.rearrange("p (b o k) -> p b o k", o=1, k=S).broadcast_to([P, BPC, 2, S]),
                                   ACT.Identity, bias=g.w("bv")).then_inc(qkv, 1)

                def spread_v(c, r, q):
                    act.wait_ge(vt, c * 2 + (q + 1))
                    for h2 in range(2):
                        half = slice(h2 * S, (h2 + 1) * S)
                        src = bank_p[half, :].rearrange("p (b j t d) -> p b j t d", b=4, t=2, d=DK)[:, :, :, h2, :]
                        for b in range(4):
                            ins = act.activation(vd[half, r, q * 4 + b, :, h2 * (DK + 1):h2 * (DK + 1) + DK], src[:, b], ACT.Copy)
                    ins.then_inc(vcopy, 1)

                def probs(n, q):
                    act.wait_ge(shifted, n + 1)
                    act.activation(pr[:, q, :], sc[:, q, :, :].rearrange("p h k -> p (h k)"), ACT.Exp).then_inc(exped, 1)

                def probs_copy(n, q):
                    act.wait_ge(turned, n + 1)
                    act.activation(pT[:, q, :, :].rearrange("p j q -> p (j q)"), bank_t.rearrange("p a b -> p (a b)"), ACT.Copy).then_inc(tcopy, 1)

                def output_copy(n, q):
                    act.wait_ge(oturned, n + 1)
                    act.activation(oT[:, q, :], bank_o[:, T_AT:T_AT + P], ACT.Copy).then_inc(ocopy, 1)

                def slot(c, r, p, first, last):
                    probs_copy(c * PPC + p, p % 2)
                    if not last or p + 1 < PPC:
                        probs(c * PPC + (p + 1), (p + 1) % 2)
                    if not first:
                        output_copy(c * PPC + (p - 1), (p - 1) % 2)
                    if not last:
                        if p < 3:
                            (take_q, take_k, take_v)[p](c + 1, 1 - r)
                        else:
                            for q in range(2):
                                spread_v(c + 1, 1 - r, q)

                for take in (take_q, take_k, take_v):
                    take(0, 0)
                for q in range(2):
                    spread_v(0, 0, q)
                probs(0, 0)
                run(act, slot)
                output_copy(NC * PPC - 1, 1)

            @block.vector
            def _(ve):
                ve.sem_inc(biased, 2)
                ve.sem_inc(added, 1)

                def softmax(n, q):
                    ve.wait_ge(scored, n + 1)
                    ve.tensor_tensor(sc[:, q].rearrange("p h k -> p (h k)"), bank_s[q].rearrange("p a b -> p (a b)"),
                                     bias[:].rearrange("p h k -> p (h k)"), ALU.add).then_inc(biased, 1)
                    ve.wait_ge(biased, n + 3)
                    ve.tensor_reduce(mx[:, q, :], sc[:, q], AX_X, ALU.max).then_inc(maxed, 1)
                    ve.wait_ge(maxed, n + 1)
                    ve.tensor_tensor(sc[:, q], sc[:, q], mx[:, q, :].rearrange("p (h o) -> p h o", o=1).broadcast_to([P, NH, S]),
                                     ALU.subtract).then_inc(shifted, 1)

                def finish(n, q):
                    ve.wait_ge(pv, n + 1)
                    res = bank_o[:, :NH // 2 * VW].rearrange("p (h w) -> p h w", w=DK + 1)
                    ve.reciprocal(ri[:, q, :], res[:, :, DK]).then_inc(rinv, 1)
                    ve.wait_ge(rinv, n + 1)
                    ve.tensor_tensor(o[:, q, :].rearrange("p (h d) -> p h d", d=DK), res[:, :, 0:DK],
                                     ri[:, q, :].rearrange("p (h o) -> p h o", o=1).broadcast_to([P, NH, DK]), ALU.mult).then_inc(normed, 1)

                def add(n):
                    ve.wait_ge(outp, n + 1)
                    x = g.X[:, bass.ds(n, 1), :].rearrange("p a d -> p (a d)")
                    ve.tensor_tensor(x, x, bank_o[:, F_AT:F_AT + D], ALU.add).then_inc(added, 1)

                def slot(c, r, p, first, last):
                    if not first:
                        add(c * PPC + (p - 1))
                    if not last or p + LEAD < PPC:
                        softmax(c * PPC + (p + LEAD), p % 2)
                    finish(c * PPC + p, p % 2)

                for n in range(LEAD):
                    softmax(n, n)
                run(ve, slot)
                ve.wait_ge(outp, NC * PPC)
                x = g.X[:, NT - 1, :]
                ve.tensor_tensor(x, x, bank_o[:, F_AT:F_AT + D], ALU.add).then_inc(added, 1)


GATES = 4
SPC = CH // B
SB = SPC // 2


def waves(nc, g, tag, hs, x1):
    LAYERS = 2
    with ExitStack() as ctx:
        sem = sem_maker(nc, ctx, tag)
        sb = lambda name, shape, dt=F32: ctx.enter_context(nc.sbuf_tensor(f"{tag}_{name}", shape, dt))
        fm = sb("fm", [P, LAYERS, B])
        m = sb("m", [P, 2, LAYERS, B])
        pre = sb("pre", [P, 2, LAYERS, B])
        ga = sb("ga", [P, 2, LAYERS, B])
        tz, eo = sb("tz", [P, LAYERS, B]), sb("eo", [P, LAYERS, B])
        norm, snorm = sb("norm", [P, LAYERS, B]), sb("snorm", [P, LAYERS, B])
        cell, scc, gt = (sb(n, [P, LAYERS, B]) for n in ("cell", "scc", "gt"))
        den, inv = sb("den", [P, LAYERS, B]), sb("inv", [P, LAYERS, B])
        bparts = sb("bparts", [P, LAYERS, GATES * P], BF16)
        bres = sb("bres", [P, LAYERS, GATES * P])
        ones = sb("ones", [P, SB * B], BF16)
        gl, z = sb("gl", [P, CH]), sb("z", [P, CH])
        zn = sb("zn", [P, TPC, D])
        st = sb("st", [P, TPC, 6])
        a, b, mean, var, rstd = (sb(n, [P, TPC]) for n in ("a", "b", "mean", "var", "rstd"))
        hready = sem("hready0"), sem("hready1")
        inverted = sem("inverted")
        gates_if, gates_zo, dve, gexp, zexp, init, predone = (
            sem(n) for n in ("gates_if", "gates_zo", "dve", "gexp", "zexp", "init", "predone"))
        cstep, cready, bvec = sem("cstep"), sem("cready"), sem("bvec")
        proj, gelu, zready, turned, stat, mixv, var_ready, rstd_ready, nready, back, done = (
            sem(n) for n in ("proj", "gelu", "zready", "turned", "stat", "mixv", "var_ready", "rstd_ready", "nready", "back", "done"))
        stat_a, mean_ready = sem("stat_a"), sem("mean_ready")
        PER = 6
        PERM = 4

        def bank_of(blk, pair, layer):
            return g.bank[4 * blk + 2 * pair + layer]

        def gate(j, k, lo, hi):
            first = 4 * (j // SB) + 2 * (k // 2)
            col = (k % 2 * SB + j % SB) * B
            return g.ps[:, first + lo:first + hi, col:col + B]

        bank_p, bank_z, bank_b = g.bank[4], g.bank[5], g.bank[6]

        def inversions(c, j, lo, hi):
            return j if lo == hi - 1 and lo == 0 else c * (2 * SPC) + ((hi - lo) * j - SPC)

        def run(eng, wave):
            wave(0, 0, 1, True)
            with eng.Fori(0, NC - 2) as i:
                wave(i + 1, 0, 2, True)
            wave(NC - 1, 0, 2, False)
            wave(NC, 1, 2, False)

        with nc.Block() as block:

            @block.gpsimd
            def _(pool):
                pool.memset(hs[:, 0, 0:B], 0.0).then_inc(init, 1)
                pool.memset(hs[:, 1, CH:CH + B], 0.0).then_inc(init, 1)
                pool.memset(m[:, 1], 0.0).then_inc(init, 1)
                pool.memset(norm[:], 0.0).then_inc(init, 1)
                pool.memset(cell[:], 0.0).then_inc(init, 1)
                pool.memset(ones[:], 1.0).then_inc(init, 1)
                pool.wait_ge(init, 6)

                def wave(c, lo, hi, ahead):
                    L = slice(lo, hi)
                    for j in range(SPC):
                        s = c * SPC + j
                        pool.wait_ge(gexp, s + 1)
                        pool.tensor_tensor(scc[:, L], cell[:, L], ga[:, 0, L], ALU.mult).then_inc(cstep, 1)
                        pool.wait_ge(zexp, 2 * s + 1)
                        pool.tensor_tensor(gt[:, L], ga[:, 1, L], tz[:, L], ALU.mult).then_inc(cstep, 1)
                        pool.wait_ge(cstep, 2 * s + 2)
                        pool.tensor_tensor(cell[:, L], scc[:, L], gt[:, L], ALU.add).then_inc(cready, 1)
                    if lo == 0:
                        pool.wait_ge(var_ready, c + 1)
                        pool.tensor_tensor(rstd[:], a[:], g.neghalf[:, 0:TPC], ALU.pow).then_inc(rstd_ready, 1)

                run(pool, wave)

            @block.tensor
            def _(pe):
                def from_input(c, blk, layer, k):
                    x = g.xT if layer == 0 else x1
                    out = bank_of(blk, k // 2, layer)[:, k % 2 * SB * B:(k % 2 + 1) * SB * B]
                    at = c * CH + (blk * SB * B - layer * CH)
                    pe.matmul(out, g.w(f"sW{layer}")[:, k * P:(k + 1) * P], x[:, bass.ds(at, SB * B)],
                              start=(k % 2 == 0), stop=False, skip_group_check=True)
                    pe.matmul(out, bparts[:, layer, k * P:(k + 1) * P], ones[:], start=False, stop=False, skip_group_check=True)

                def h_before(c, j, layer):
                    pe.wait_ge(hready[layer], c * SPC + (j + 1 - layer * SPC))

                def wave(c, lo, hi, ahead):
                    if hi == 2:
                        for k in range(GATES):
                            from_input(c, 0, 1, k)
                    for j in range(SPC):
                        for pair, layer in ((p, l) for p in range(2) for l in range(lo, hi)):
                            if pair == 0:
                                h_before(c, j, layer)
                            for k in (2 * pair, 2 * pair + 1):
                                ins = pe.matmul(gate(j, k, layer, layer + 1), g.w(f"sR{layer}")[:, k * P:(k + 1) * P],
                                                hs[:, layer, bass.ds(c * CH + j * B, B)],
                                                start=False, stop=(k % 2 == 1), skip_group_check=True)
                                if k % 2 == 1 and layer == hi - 1:
                                    ins.then_inc((gates_if, gates_zo)[k // 2], 1)
                        if j < SB:
                            for layer in range(lo, hi):
                                from_input(c, 1, layer, j)
                        elif ahead:
                            from_input(c + 1, 0, 0, j - SB)
                    if lo == 0:
                        pe.wait_ge(hready[0], c * SPC + (SPC + 1))
                        if hi == 2:
                            pe.wait_ge(hready[1], c * SPC + 1)
                        pe.matmul(bank_p, g.w("sP0"), hs[:, 0, bass.ds(c * CH + B, CH)], start=True, stop=True).then_inc(proj, 1)
                        pe.wait_ge(zready, c + 1)
                        for j in range(TPC):
                            ins = pe.transpose(bank_z[:, j * P:(j + 1) * P], z[:, j * P:(j + 1) * P], g.ident)
                        ins.then_inc(turned, 1)
                        pe.wait_ge(nready, (c + 1) * TPC)
                        for j in range(TPC):
                            ins = pe.transpose(bank_b[:, j * P:(j + 1) * P], zn[:, j, :], g.ident)
                        ins.then_inc(back, 1)
                        pe.wait_ge(done, c + 1)

                pe.wait_ge(init, 6)
                pe.wait_ge(bvec, 6)
                for k in range(GATES):
                    from_input(0, 0, 0, k)
                run(pe, wave)

            @block.scalar
            def _(act):
                def wave(c, lo, hi, ahead):
                    act.preload_act_table(ACT.Exp)
                    for j in range(SPC):
                        s = c * SPC + j
                        act.wait_ge(predone, s + 1)
                        act.activation(ga[:, 0:2, lo:hi], pre[:, :, lo:hi], ACT.Exp).then_inc(gexp, 1)
                        act.wait_ge(gates_zo, s + 1)
                        act.activation(tz[:, lo:hi], gate(j, 2, lo, hi), ACT.Tanh).then_inc(zexp, 1)
                        act.activation(eo[:, lo:hi], gate(j, 3, lo, hi), ACT.Exp, scale=-1.0).then_inc(zexp, 1)
                    if lo == 0:
                        act.preload_act_table(ACT.Gelu)
                        act.wait_ge(proj, c + 1)
                        act.activation(gl[:], bank_p, ACT.Gelu, bias=g.w("spb0")).then_inc(gelu, 1)
                        act.wait_ge(back, c + 1)
                        act.activation(x1[:, bass.ts(c, CH)], bank_b, ACT.Identity, bias=g.w("sbe0"), scale=g.w("sga0")).then_inc(done, 1)

                run(act, wave)

            @block.vector
            def _(ve):
                whole = g.wts[:, g.lay["sbrow0"][0]:g.lay["sbrow0"][0] + LAYERS * GATES * P].rearrange("p (l k) -> p l k", l=LAYERS)
                for k, f in enumerate((
                        lambda: ve.tensor_copy(bparts[:], whole),
                        lambda: ve.tensor_tensor(bres[:], whole, bparts[:], ALU.subtract),
                        lambda: ve.tensor_copy(bparts[32:64], bres[32:64]),
                        lambda: ve.tensor_copy(bparts[64:128], bres[64:128]),
                        lambda: ve.tensor_tensor(bres[64:128], bres[64:128], bparts[64:128], ALU.subtract),
                        lambda: ve.tensor_copy(bparts[64:128], bres[64:128]))):
                    f().then_inc(bvec, 1)
                    ve.wait_ge(bvec, k + 1)
                for h in hready:
                    ve.sem_inc(h, 1)
                ve.wait_ge(init, 6)

                def step(c, j, lo, hi):
                    s = c * SPC + j
                    q = j % 2
                    L = slice(lo, hi)
                    n = [0]

                    def inc(ins):
                        ins.then_inc(dve, 1)
                        n[0] += 1

                    def link(ins):
                        inc(ins)
                        ve.wait_ge(dve, c * SPC * PER + (j * PER + n[0]))

                    new, old = m[:, q, L], m[:, 1 - q, L]
                    ve.wait_ge(gates_if, s + 1)
                    link(ve.tensor_tensor(fm[:, L], gate(j, 1, lo, hi), old, ALU.add))
                    link(ve.tensor_tensor(new, gate(j, 0, lo, hi), fm[:, L], ALU.max))
                    inc(ve.tensor_tensor(pre[:, 0, L], fm[:, L], new, ALU.subtract))
                    ve.tensor_tensor(pre[:, 1, L], gate(j, 0, lo, hi), new, ALU.subtract).then_inc(predone, 1)
                    ve.wait_ge(gexp, s + 1)
                    link(ve.tensor_tensor(snorm[:, L], norm[:, L], ga[:, 0, L], ALU.mult))
                    link(ve.tensor_tensor(norm[:, L], snorm[:, L], ga[:, 1, L], ALU.add))
                    ve.wait_ge(zexp, 2 * s + 2)
                    link(ve.scalar_tensor_tensor(den[:, L], eo[:, L], 1.0, norm[:, L], ALU.add, ALU.mult))
                    assert n[0] == PER
                    for k, layer in enumerate(range(lo, hi)):
                        ve.reciprocal(inv[:, layer], den[:, layer]).then_inc(inverted, 1)
                        ve.wait_ge(inverted, inversions(c, j, lo, hi) + (k + 1))
                        if k == 0:
                            ve.wait_ge(cready, s + 1)
                        ve.tensor_tensor(hs[:, layer, bass.ds(c * CH + (j + 1) * B, B)], cell[:, layer], inv[:, layer], ALU.mult).then_inc(hready[layer], 1)

                def mix(c):
                    n = [0]

                    def inc(ins):
                        ins.then_inc(mixv, 1)
                        n[0] += 1

                    def link(ins):
                        inc(ins)
                        ve.wait_ge(mixv, c * PERM + n[0])

                    ve.wait_ge(gelu, c + 1)
                    ve.tensor_tensor(z[:], gl[:], g.xT[:, bass.ts(c, CH)], ALU.add).then_inc(zready, 1)
                    ve.wait_ge(turned, c + 1)
                    for j in range(TPC):
                        ve.bn_stats(st[:, j, :], bank_z[:, j * P:(j + 1) * P]).then_inc(stat, 1)
                    ve.wait_ge(stat, (c + 1) * TPC)
                    inc(ve.tensor_tensor(b[:], st[:, :, 1], st[:, :, 4], ALU.subtract))
                    link(ve.tensor_tensor(var[:], st[:, :, 2], st[:, :, 5], ALU.add))
                    ve.tensor_tensor(a[:], st[:, :, 1], st[:, :, 4], ALU.add).then_inc(stat_a, 1)
                    link(ve.scalar_tensor_tensor(b[:], b[:], 0.25, b[:], ALU.mult, ALU.mult))
                    link(ve.scalar_tensor_tensor(var[:], var[:], 1.0 / D, b[:], ALU.mult, ALU.add))
                    ve.wait_ge(stat_a, c + 1)
                    ve.tensor_scalar(mean[:], a[:], 0.5, None, ALU.mult).then_inc(mean_ready, 1)
                    ve.wait_ge(mean_ready, c + 1)
                    ve.tensor_scalar(a[:], var[:], EPS, None, ALU.add).then_inc(var_ready, 1)
                    ve.wait_ge(rstd_ready, c + 1)
                    for j in range(TPC):
                        ve.tensor_scalar(zn[:, j, :], bank_z[:, j * P:(j + 1) * P], mean[:, j:j + 1],
                                         rstd[:, j:j + 1], ALU.subtract, ALU.mult).then_inc(nready, 1)

                def wave(c, lo, hi, ahead):
                    for j in range(SPC):
                        step(c, j, lo, hi)
                    if lo == 0:
                        mix(c)

                run(ve, wave)


def final_norm(nc, g, tag, xin, hs):
    with ExitStack() as ctx:
        sem = sem_maker(nc, ctx, tag)
        sb = lambda name, shape, dt=F32: ctx.enter_context(nc.sbuf_tensor(f"{tag}_{name}", shape, dt))
        R = 4
        gl = sb("gl", [P, 2, CH])
        z = sb("z", [P, R, CH])
        zn = sb("zn", [P, R, TPC, D])
        zs = sb("zs", [P, R, TPC, D])
        st = sb("st", [P, R, TPC, 6])
        a, b, mean, var, rstd = (sb(n, [P, R, TPC]) for n in ("a", "b", "mean", "var", "rstd"))
        proj, gelu, zready, turned, stat, vch, var_ready, rstd_ready, nready, gained, shifted, added = (
            sem(n) for n in ("proj", "gelu", "zready", "turned", "stat", "vch", "var_ready", "rstd_ready", "nready", "gained", "shifted", "added"))

        def view(t, c):
            return t.rearrange("p (s b) -> p b s", b=B)[:, bass.ts(c, BPC), :]
        three = lambda t: t.rearrange("p (a k) -> p a k", k=S)
        bank_p, bank_z = g.bank[0:2], g.bank[2:6]
        with nc.Block() as block:

            @block.tensor
            def _(pe):
                def turn(c, r):
                    pe.wait_ge(zready, c + 3)
                    pe.wait_ge(nready, c + 1)
                    for j in range(TPC):
                        ins = pe.transpose(bank_z[r][:, j * P:(j + 1) * P], z[:, r, j * P:(j + 1) * P], g.ident)
                    ins.then_inc(turned, 1)

                with pe.Fori(0, NC // R) as group:
                    for r in range(R):
                        c = group * R + r
                        pe.wait_ge(gelu, c + 1)
                        pe.matmul(three(bank_p[r % 2]), g.w("sP1"), view(hs, c), start=True, stop=True).then_inc(proj, 1)
                        if r >= 1:
                            turn(group * R + (r - 1), r - 1)
                    turn(group * R + (R - 1), R - 1)

            @block.scalar
            def _(act):
                act.preload_act_table(ACT.Gelu)
                act.sem_inc(gelu, 2)
                with act.Fori(0, NC // R) as group:
                    for r in range(R):
                        c = group * R + r
                        act.wait_ge(proj, c + 1)
                        act.wait_ge(zready, c + 1)
                        act.activation(gl[:, r % 2, :], bank_p[r % 2], ACT.Gelu, bias=g.w("spb1")).then_inc(gelu, 1)

            @block.gpsimd
            def _(pool):
                row = lambda n: g.w(n).rearrange("p (o d) -> p o d", o=1).broadcast_to([P, TPC, D])

                def root(c, r):
                    pool.wait_ge(var_ready, c + 1)
                    pool.tensor_tensor(rstd[:, r, :], a[:, r, :], g.neghalf[:, 0:TPC], ALU.pow).then_inc(rstd_ready, 1)

                def gain(c, r):
                    pool.wait_ge(nready, c + (R + 1))
                    pool.tensor_tensor(zs[:, r], zn[:, r], row("garow"), ALU.mult).then_inc(gained, 1)
                    pool.wait_ge(gained, c + 1)
                    pool.tensor_tensor(zs[:, r], zs[:, r], row("berow"), ALU.add).then_inc(shifted, 1)

                with pool.Fori(0, NC // R) as group:
                    for r in range(R):
                        root(group * R + r, r)
                        if r >= 1:
                            gain(group * R + (r - 1), r - 1)
                    gain(group * R + (R - 1), R - 1)

            @block.vector
            def _(ve):
                PER = 6
                ve.sem_inc(zready, 2)
                ve.sem_inc(nready, R)

                def sum_up(c, r):
                    ve.wait_ge(gelu, c + 3)
                    ve.tensor_tensor(three(z[:, r, :]), three(gl[:, r % 2, :]), view(xin, c), ALU.add).then_inc(zready, 1)

                def moments(c, r):
                    n = [0]

                    def inc(ins):
                        ins.then_inc(vch, 1)
                        n[0] += 1

                    def link(ins):
                        inc(ins)
                        ve.wait_ge(vch, c * PER + n[0])

                    ve.wait_ge(turned, c + 1)
                    for j in range(TPC):
                        ve.bn_stats(st[:, r, j, :], bank_z[r][:, j * P:(j + 1) * P]).then_inc(stat, 1)
                    ve.wait_ge(stat, c * TPC + TPC)
                    ve_a, ve_b, ve_m, ve_v = a[:, r, :], b[:, r, :], mean[:, r, :], var[:, r, :]
                    inc(ve.tensor_tensor(ve_a, st[:, r, :, 1], st[:, r, :, 4], ALU.add))
                    inc(ve.tensor_tensor(ve_b, st[:, r, :, 1], st[:, r, :, 4], ALU.subtract))
                    link(ve.tensor_tensor(ve_v, st[:, r, :, 2], st[:, r, :, 5], ALU.add))
                    link(ve.scalar_tensor_tensor(ve_b, ve_b, 0.25, ve_b, ALU.mult, ALU.mult))
                    inc(ve.tensor_scalar(ve_m, ve_a, 0.5, None, ALU.mult))
                    link(ve.scalar_tensor_tensor(ve_v, ve_v, 1.0 / D, ve_b, ALU.mult, ALU.add))
                    assert n[0] == PER
                    ve.tensor_scalar(ve_a, ve_v, EPS, None, ALU.add).then_inc(var_ready, 1)

                def normalise(c, r):
                    ve.wait_ge(rstd_ready, c + 1)
                    for j in range(TPC):
                        ins = ve.tensor_scalar(zn[:, r, j, :], bank_z[r][:, j * P:(j + 1) * P], mean[:, r, j:j + 1],
                                               rstd[:, r, j:j + 1], ALU.subtract, ALU.mult)
                    ins.then_inc(nready, 1)

                def add(c, r):
                    ve.wait_ge(shifted, c + 1)
                    xc = g.X[:, bass.ts(c, TPC), :]
                    ve.tensor_tensor(xc, xc, zs[:, r], ALU.add).then_inc(added, 1)

                with ve.Fori(0, NC // R) as group:
                    for r in range(R + 3):
                        for lag, step in enumerate((sum_up, moments, normalise, add)):
                            if 0 <= r - lag < R:
                                step(group * R + (r - lag), r - lag)


def lstm_stage(nc, g):
    by_step = lambda c: g.xT[:, :].rearrange("p (s b) -> p b s", b=B)[:, bass.ts(c, BPC), :]
    norm_stage(nc, g, "n3", place=by_step)
    with ExitStack() as ctx:
        hs = ctx.enter_context(nc.sbuf_tensor("lstm_h", [P, 2, T + CH + B], F32))
        x1 = ctx.enter_context(nc.sbuf_tensor("lstm_x1", [P, T], F32))
        waves(nc, g, "rw", hs, x1)
        final_norm(nc, g, "m1", x1[:, :], hs[:, 1, CH + B:])


NX = 8
CAP = T * 5 // (4 * NX)
TILES = T // P + NX
PAD_TILES = TILES + 2
RING = 4
WAYS = 4
BITS = 30


class Router:

    def __init__(self, nc, g, ctx, tag):
        self.nc, self.g, self.tag = nc, g, tag
        self.sem = sem_maker(nc, ctx, tag)
        self.sb = lambda name, shape, dt=F32: ctx.enter_context(nc.sbuf_tensor(f"{tag}_{name}", shape, dt))
        self.p = self.sb("p", [P, NT, NX])
        self.oh = self.sb("oh", [P, NT, NX])
        self.t = self.sb("t", [P, NT, NX])
        self.pos = self.sb("pos", [P, NT, NX])
        self.incl = self.sb("incl", [P, NX, NT])
        self.m = self.sb("m", [P, NT])
        self.m2 = self.sb("m2", [P, NT])
        self.slot = self.sb("slot", [P, NT])
        self.slot_u = self.sb("slot_u", [P, NT], U32)
        self.weight = self.sb("weight", [P, NT])

    def over_experts(self, a):
        return a.rearrange("p (n o) -> p n o", o=1).broadcast_to([P, NT, NX])

    def over_tiles(self, a):
        return a.rearrange("p (o e) -> p o e", o=1).broadcast_to([P, NT, NX])

    def pick(self, ve, ch, score, best):
        over, r = self.over_experts, self
        ch.link(ve.tensor_tensor(r.t[:], score, over(best), ALU.is_ge))
        ch.link(ve.scalar_tensor_tensor(r.t[:], r.t[:], -float(NX), r.over_tiles(r.g.w("eidx")), ALU.mult, ALU.add))
        ch.link(ve.tensor_reduce(r.m2[:], r.t[:], AX_X, ALU.min))
        ch.link(ve.tensor_tensor(r.oh[:], r.t[:], over(r.m2[:]), ALU.is_equal))

    def ranks(self, ve, ch, counted, times):
        r, g = self, self.g
        ve.wait_ge(counted, times)
        cnt = g.bank[1][:, 0:NT * NX].rearrange("p (n e) -> p e n", e=NX)
        for e in range(NX):
            ch.inc(ve.tensor_tensor_scan(r.incl[:, e, :], g.w("onerow"), cnt[:, e, :], 0.0, ALU.mult, ALU.add))
        ve.wait_ge(ch.sem, ch.value())
        incl = r.incl[:].rearrange("p e n -> p n e")
        flat = lambda k: g.bank[k][:, 0:NT * NX].rearrange("p (n e) -> p n e", e=NX)
        ch.link(ve.tensor_tensor(r.pos[:], incl, flat(1), ALU.subtract))
        ch.link(ve.tensor_tensor(r.pos[:], r.pos[:], flat(0), ALU.add))


def count_flags(pe, g, flags):
    f = flags[:].rearrange("p n e -> p (n e)")
    pe.matmul(g.bank[0][:, 0:NT * NX], g.w("before"), f, start=True, stop=True)
    return pe.matmul(g.bank[1][:, 0:NT * NX], g.w("allones"), f, start=True, stop=True)


def softmax_block(nc, g, r, gate, bias):
    logits, chain, sub, exped = (r.sem(n) for n in ("logits", "chain", "sub", "exped"))
    with nc.Block() as block:

        @block.tensor
        def _(pe):
            for n in range(NT):
                ins = pe.matmul(g.bank[2][:, n * NX:(n + 1) * NX], g.xT[:, n * P:(n + 1) * P], gate, start=True, stop=True)
            ins.then_inc(logits, 1)

        @block.scalar
        def _(act):
            act.wait_ge(sub, 1)
            act.activation(r.p[:], r.p[:], ACT.Exp).then_inc(exped, 1)

        @block.vector
        def _(ve):
            ch = Chain(ve, chain)
            lg = g.bank[2][:, 0:NT * NX].rearrange("p (n e) -> p n e", e=NX)
            ve.wait_ge(logits, 1)
            if bias is not None:
                ch.link(ve.tensor_tensor(r.p[:], lg, r.over_tiles(bias), ALU.add))
            else:
                ch.link(ve.tensor_copy(r.p[:], lg))
            ch.link(ve.tensor_reduce(r.m[:], r.p[:], AX_X, ALU.max))
            ve.tensor_tensor(r.p[:], r.p[:], r.over_experts(r.m[:]), ALU.subtract).then_inc(sub, 1)
            ve.wait_ge(exped, 1)
            ch.link(ve.tensor_reduce(r.m[:], r.p[:], AX_X, ALU.add))
            ch.link(ve.reciprocal(r.m[:], r.m[:]))
            ch.link(ve.tensor_tensor(r.p[:], r.p[:], r.over_experts(r.m[:]), ALU.mult))
            ch.link(ve.tensor_reduce(r.m[:], r.p[:], AX_X, ALU.max))


def clear_places(sp, g):
    view = g.buf[0:PAD_TILES * P, :].rearrange("(a p) d -> p a d", p=P)
    for a in range(0, PAD_TILES, TPC):
        w = min(TPC, PAD_TILES - a)
        sp.dma_start(view[:, a:a + w, :], g.zero[:, 0:w * D].rearrange("p (a d) -> p a d", d=D)).then_inc(g.cleared, 16)
        g.clears += 16
    sp.wait_ge(g.cleared, g.clears)


def dispatch(nc, g, tag, r, slots, win, loads):
    with ExitStack() as ctx:
        sem = sem_maker(nc, ctx, tag)
        scattered = g.lasting(f"{tag}_scattered")
        with nc.Block() as block:

            @block.sync
            def _(sp):
                sp.wait_ge(win, 16 * loads)

            @block.gpsimd
            def _(pool):
                for n in range(NT):
                    pool.indirect_dma_start(g.buf, bass.IndirectOffsetOnAxis(ap=slots[:, n:n + 1], axis=0), g.rows[:, n, :], None).then_inc(scattered, 16)
                pool.wait_ge(scattered, 16 * NT)


def experts(nc, g, tag, F, w1, w2, owner, func, b1=None, b2=None):
    FB = F // P
    with ExitStack() as ctx:
        sem = sem_maker(nc, ctx, tag)
        sb = lambda name, shape, dt=F32: ctx.enter_context(nc.sbuf_tensor(f"{tag}_{name}", shape, dt))
        xr = sb("xr", [P, RING, D])
        xT = sb("xT", [P, 2, P])
        h = sb("h", [P, 2, F])
        hT = sb("hT", [P, 2, FB, P])
        y = sb("y", [P, RING, D])
        row_in = [sem(f"row_in{k}") for k in range(RING)]
        out_done = [sem(f"out_done{k}") for k in range(RING)]
        turned, xcopy, mm1, hready, hturned, hcopy, mm2, yready = (
            sem(n) for n in ("turned", "xcopy", "mm1", "hready", "hturned", "hcopy", "mm2", "yready"))
        bank_x, bank_h, bank_t, bank_y = g.bank[0:2], g.bank[2:4], g.bank[4:6], g.bank[6:8]
        with nc.Block() as block:

            @block.sync
            def _(sp):
                def load(k, r):
                    sp.dma_start(xr[:, r, :], g.buf[bass.ts(k, P), :]).then_inc(row_in[r], 16)

                for k in range(RING):
                    load(k, k)
                for r in range(RING):
                    sp.sem_inc(out_done[r], 16)

                def store(k, r):
                    sp.wait_ge(yready, k + 3)
                    sp.dma_start(g.out[bass.ts(k, P), :], y[:, r, :]).then_inc(out_done[r], 16)

                with sp.Fori(0, TILES // RING - 1) as i:
                    for r in range(RING):
                        sp.wait_ge(turned, i * RING + (r + 1))
                        load(i * RING + (RING + r), r)
                        store(i * RING + r, r)
                for r in range(RING):
                    if TILES + r < PAD_TILES:
                        sp.wait_ge(turned, TILES - RING + r + 1)
                        load(TILES + r, r)
                    store(TILES - RING + r, r)
                for r in range(RING):
                    sp.wait_ge(out_done[r], 16 * (TILES // RING) + 16)

            @block.tensor
            def _(pe):
                def turn(k, r, uses):
                    pe.wait_ge(row_in[r], uses * 16)
                    pe.wait_ge(xcopy, k + 1)
                    pe.transpose(bank_x[r % 2][:, 0:P], xr[:, r, :], g.ident).then_inc(turned, 1)

                def first(k, r):
                    e = pe.value_load(owner[0:1, bass.ds(k, 1)], min_val=0, max_val=NX - 1)
                    pe.wait_ge(xcopy, k + 3)
                    pe.wait_ge(hready, k + 1)
                    pe.matmul(bank_h[r % 2][:, 0:F], xT[:, r % 2, :], w1[:, bass.ts(e, F)], start=True, stop=True).then_inc(mm1, 1)

                def turn_hidden(k, r):
                    pe.wait_ge(hready, k + 3)
                    pe.wait_ge(hcopy, k + 1)
                    for f in range(FB):
                        ins = pe.transpose(bank_t[r % 2][:, f * P:(f + 1) * P], h[:, r % 2, f * P:(f + 1) * P], g.ident)
                    ins.then_inc(hturned, 1)

                def second(k, r):
                    e = pe.value_load(owner[0:1, bass.ds(k, 1)], min_val=0, max_val=NX - 1)
                    pe.wait_ge(hcopy, k + 3)
                    pe.wait_ge(yready, k + 1)
                    for f in range(FB):
                        ins = pe.matmul(bank_y[r % 2][:, 0:D], hT[:, r % 2, f, :], w2[:, bass.ds(e * (FB * D) + f * D, D)],
                                        start=(f == 0), stop=(f == FB - 1))
                    ins.then_inc(mm2, 1)

                turn(0, 0, 1)
                turn(1, 1, 1)
                first(0, 0)
                with pe.Fori(0, TILES // RING) as i:
                    for r in range(RING):
                        k = i * RING + r
                        turn_hidden(k, r)
                        turn(k + 2, (r + 2) % RING, i + (1 if r + 2 < RING else 2))
                        first(k + 1, (r + 1) % RING)
                        second(k, r)

            @block.scalar
            def _(act):
                act.sem_inc(xcopy, 2)
                act.sem_inc(hcopy, 2)

                act.preload_act_table(func)

                def take_x(k, r):
                    act.wait_ge(turned, k + 1)
                    act.activation(xT[:, r % 2, :], bank_x[r % 2][:, 0:P], ACT.Copy).then_inc(xcopy, 1)

                def hidden(k, r):
                    act.wait_ge(mm1, k + 1)
                    act.activation(h[:, r % 2, :], bank_h[r % 2][:, 0:F], func).then_inc(hready, 1)

                def hidden_turned(k, r):
                    act.wait_ge(hturned, k + 1)
                    act.activation(hT[:, r % 2].rearrange("p f t -> p (f t)"), bank_t[r % 2][:, 0:F], func).then_inc(hcopy, 1)

                if b1 is None:
                    act.sem_inc(hready, 2)
                take_x(0, 0)
                take_x(1, 1)
                if b1 is None:
                    hidden(0, 0)
                with act.Fori(0, TILES // RING) as i:
                    for r in range(RING):
                        k = i * RING + r
                        if b1 is not None:
                            hidden_turned(k, r)
                        take_x(k + 2, (r + 2) % RING)
                        if b1 is None:
                            hidden(k + 1, (r + 1) % RING)

            @block.vector
            def _(ve):
                ve.sem_inc(yready, 2)
                if b1 is not None:
                    ve.sem_inc(hready, 2)

                def first(k, r):
                    e = ve.value_load(owner[0:1, bass.ds(k, 1)], min_val=0, max_val=NX - 1)
                    ve.wait_ge(mm1, k + 1)
                    ve.tensor_tensor(h[:, r % 2, :], bank_h[r % 2][:, 0:F], b1[:, bass.ts(e, F)], ALU.add).then_inc(hready, 1)

                def second(k, r, uses):
                    if b1 is None:
                        ve.wait_ge(hturned, k + 1)
                        ve.tensor_copy(hT[:, r % 2].rearrange("p f t -> p (f t)"), bank_t[r % 2][:, 0:F]).then_inc(hcopy, 1)
                    if b2 is not None:
                        e = ve.value_load(owner[0:1, bass.ds(k, 1)], min_val=0, max_val=NX - 1)
                    ve.wait_ge(out_done[r], uses * 16 + 16)
                    ve.wait_ge(mm2, k + 1)
                    if b2 is not None:
                        ve.tensor_tensor(y[:, r, :], bank_y[r % 2][:, 0:D], b2[:, bass.ts(e, D)], ALU.add).then_inc(yready, 1)
                    else:
                        ve.tensor_copy(y[:, r, :], bank_y[r % 2][:, 0:D]).then_inc(yready, 1)

                if b1 is not None:
                    first(0, 0)
                with ve.Fori(0, TILES // RING) as i:
                    for r in range(RING):
                        k = i * RING + r
                        if b1 is not None:
                            first(k + 1, (r + 1) % RING)
                        second(k, r, i)


def combine(nc, g, tag, places, weight):
    G = 8
    with ExitStack() as ctx:
        sem = sem_maker(nc, ctx, tag)
        row = ctx.enter_context(nc.sbuf_tensor(f"{tag}_row", [P, G, D], F32))
        got = [g.lasting(f"{tag}_got{k}") for k in range(G)]
        added = sem("added")
        with nc.Block() as block:

            @block.gpsimd
            def _(pool):
                for n in range(NT):
                    if n >= G:
                        pool.wait_ge(added, n - G + 1)
                    pool.indirect_dma_start(row[:, n % G, :], None, g.out, bass.IndirectOffsetOnAxis(ap=places[:, n:n + 1], axis=0)).then_inc(got[n % G], 16)

            @block.vector
            def _(ve):
                for n in range(NT):
                    ve.wait_ge(got[n % G], 16 * (n // G + 1))
                    ve.scalar_tensor_tensor(g.X[:, n, :], row[:, n % G, :], weight[:, n:n + 1], g.X[:, n, :],
                                            ALU.mult, ALU.add).then_inc(added, 1)


def switch_stage(nc, g):
    with ExitStack() as ctx:
        g.rows = ctx.enter_context(nc.sbuf_tensor("sw_rows", [P, NT, D], F32))
        r = Router(nc, g, ctx, "sw")
        sb = r.sb
        w1, w2, b1, b2 = sb("w1", [P, NX * 512]), sb("w2", [P, NX * 512]), sb("b1", [P, NX * 512]), sb("b2", [P, NX * D])
        place = sb("place", [P, NT])
        place_u = sb("place_u", [P, NT], U32)
        owner = sb("owner", [1, PAD_TILES], I32)
        win, picked, counted, chain = (r.sem(n) for n in ("win", "picked", "counted", "chain2"))

        def fetch(sp):
            clear_places(sp, g)
            for t, d in ((owner, g.moe0["owner"]), (w1, g.moe0["w1"]), (w2, g.moe0["w2"]), (b1, g.moe0["b1"]), (b2, g.moe0["b2"])):
                sp.dma_start(t[:], d).then_inc(win, 16)

        norm_stage(nc, g, "n2", keep=True, fetch=fetch)
        softmax_block(nc, g, r, g.w("gate0"), g.w("gateb0"))
        with nc.Block() as block:

            @block.tensor
            def _(pe):
                pe.wait_ge(picked, 1)
                count_flags(pe, g, r.oh).then_inc(counted, 1)

            @block.vector
            def _(ve):
                ch = Chain(ve, chain)
                r.pick(ve, ch, r.p[:], r.m[:])
                ve.sem_inc(picked, 1)
                r.ranks(ve, ch, counted, 1)
                ch.link(ve.tensor_tensor(r.t[:], r.oh[:], r.pos[:], ALU.mult))
                ch.link(ve.tensor_reduce(r.slot[:], r.t[:], AX_X, ALU.add))
                ch.link(ve.tensor_tensor(r.t[:], r.oh[:], r.over_tiles(g.w("eidx")), ALU.mult))
                ch.link(ve.tensor_reduce(r.m2[:], r.t[:], AX_X, ALU.add))
                ch.link(ve.tensor_scalar(r.weight[:], r.slot[:], float(CAP), None, ALU.is_lt))
                ch.link(ve.tensor_scalar(place[:], r.slot[:], float(CAP - 1), None, ALU.min))
                ch.link(ve.scalar_tensor_tensor(place[:], r.m2[:], float(CAP), place[:], ALU.mult, ALU.add))
                ch.link(ve.tensor_copy(place_u[:], place[:]))
                ch.link(ve.tensor_tensor(r.slot[:], place[:], g.w("spare"), ALU.subtract))
                ch.link(ve.tensor_tensor(r.slot[:], r.slot[:], r.weight[:], ALU.mult))
                ch.link(ve.tensor_tensor(r.slot[:], r.slot[:], g.w("spare"), ALU.add))
                ch.link(ve.tensor_copy(r.slot_u[:], r.slot[:]))
                ch.link(ve.tensor_tensor(r.weight[:], r.weight[:], r.m[:], ALU.mult))

        dispatch(nc, g, "sd", r, r.slot_u, win, 5)
        experts(nc, g, "se", 512, w1[:], w2[:], owner, ACT.Relu, b1=b1[:], b2=b2[:])
        combine(nc, g, "sc", place_u, r.weight)


def choice_stage(nc, g):
    with ExitStack() as ctx:
        g.rows = ctx.enter_context(nc.sbuf_tensor("ec_rows", [P, NT, D], F32))
        r = Router(nc, g, ctx, "ec")
        sb = r.sb
        w1, w2 = sb("w1", [P, NX * 256]), sb("w2", [P, NX * 256])
        thr = sb("thr", [P, NX])
        trial = sb("trial", [P, WAYS, NX])
        reach = sb("reach", [P, WAYS - 1, NX, NT])
        reached = sb("reached", [P, WAYS - 1, NX])
        cand = sb("cand", [P, NX])
        part = sb("part", [P, NX])
        need = sb("need", [P, NX])
        gt = sb("gt", [P, NT, NX])
        eq = sb("eq", [P, NT, NX])
        tiles_i = sb("tiles_i", [P, NX], I32)
        ends = sb("ends", [P, NX])
        own = sb("own", [P, PAD_TILES, NX])
        ownf = sb("ownf", [P, PAD_TILES])
        owner = sb("owner", [P, PAD_TILES], I32)
        bits = sb("bits", [P, BITS // 2, WAYS], I32)
        K = float(T // NX)
        bits_in = r.sem("bits_in")
        win, parted, counted, chain, step, picked, ranked = (r.sem(n) for n in ("win", "parted", "counted", "chain2", "step", "picked", "ranked"))
        over = r.over_tiles
        by_expert = lambda a: a.rearrange("p n e -> p e n")

        def fetch(sp):
            sp.dma_start(bits[:], g.bits_dram.rearrange("p (i w) -> p i w", w=WAYS)).then_inc(bits_in, 16)
            sp.wait_ge(bits_in, 16)
            clear_places(sp, g)
            for t, d in ((w1, g.moe1["w1"]), (w2, g.moe1["w2"])):
                sp.dma_start(t[:], d).then_inc(win, 16)

        norm_stage(nc, g, "n5", keep=True, fetch=fetch)
        softmax_block(nc, g, r, g.w("gate1"), None)
        with nc.Block() as block:

            @block.tensor
            def _(pe):
                with pe.Fori(0, BITS // 2) as i:
                    pe.wait_ge(parted, i + 1)
                    pe.matmul(g.bank[3][:, 0:(WAYS - 1) * NX], g.w("allones"), reached[:].rearrange("p w e -> p (w e)"),
                              start=True, stop=True).then_inc(counted, 1)
                pe.wait_ge(parted, BITS // 2 + 1)
                pe.matmul(g.bank[3][:, 0:NX], g.w("allones"), part[:], start=True, stop=True).then_inc(counted, 1)
                for k in range(2):
                    pe.wait_ge(picked, k + 1)
                    count_flags(pe, g, (eq, r.oh)[k]).then_inc(ranked, 1)

            @block.vector
            def _(ve):
                ch = Chain(ve, chain)
                ch.link(ve.memset(thr[:], 0.0))
                by_trial = lambda a: a.rearrange("p (w e) -> p w e", e=NX)
                with ve.Fori(0, BITS // 2) as i:
                    ch.enter(i, WAYS)
                    ways = bits[:, bass.ds(i, 1), :].rearrange("p o w -> p w o").broadcast_to([P, WAYS, NX])
                    ch.link(ve.tensor_tensor(trial[:].bitcast(I32), thr[:].bitcast(I32).rearrange("p (o e) -> p o e", o=1).broadcast_to([P, WAYS, NX]),
                                             ways, ALU.bitwise_or))
                    for w in range(1, WAYS):
                        ins = ve.tensor_tensor(reach[:, w - 1].rearrange("p e n -> p n e"), r.p[:], over(trial[:, w, :]), ALU.is_ge)
                    ch.link(ins)
                    ve.tensor_reduce(reached[:], reach[:], AX_X, ALU.add).then_inc(parted, 1)
                    ve.wait_ge(counted, i + 1)
                    ch.link(ve.scalar_tensor_tensor(trial[:, 1:], by_trial(g.bank[3][:, 0:(WAYS - 1) * NX]), K, trial[:, 1:], ALU.is_ge, ALU.mult))
                    ch.link(ve.tensor_reduce(thr[:], trial[:].rearrange("p w e -> p e w"), AX_X, ALU.max))
                ch.leave(BITS // 2)
                ch.link(ve.tensor_tensor(gt[:], r.p[:], over(thr[:]), ALU.is_gt))
                ve.tensor_tensor(eq[:], r.p[:], over(thr[:]), ALU.is_equal).then_inc(picked, 1)
                ve.tensor_reduce(part[:], by_expert(gt[:]), AX_X, ALU.add).then_inc(parted, 1)
                ve.wait_ge(counted, BITS // 2 + 1)
                ch.link(ve.tensor_scalar(need[:], g.bank[3][:, 0:NX], -1.0, K, ALU.mult, ALU.add))
                r.ranks(ve, ch, ranked, 1)
                ch.link(ve.tensor_tensor(r.pos[:], r.pos[:], over(need[:]), ALU.is_lt))
                ch.link(ve.tensor_tensor(eq[:], eq[:], r.pos[:], ALU.mult))
                ch.link(ve.tensor_tensor(gt[:], gt[:], eq[:], ALU.add))
                ch.link(ve.tensor_reduce(r.m[:], gt[:], AX_X, ALU.max))
                ch.link(ve.tensor_scalar(r.m[:], r.m[:], 0.0, None, ALU.is_equal))
                ch.link(ve.tensor_tensor(gt[:], gt[:], r.over_experts(r.m[:]), ALU.max))
                ch.link(ve.tensor_tensor(eq[:], r.p[:], gt[:], ALU.mult))
                ch.link(ve.scalar_tensor_tensor(eq[:], gt[:], -1.0, eq[:], ALU.add, ALU.add))
                ch.link(ve.tensor_reduce(r.weight[:], eq[:], AX_X, ALU.max))
                r.pick(ve, ch, eq[:], r.weight[:])
                ve.sem_inc(picked, 1)
                r.ranks(ve, ch, ranked, 2)
                ch.link(ve.tensor_tensor(r.t[:], r.oh[:], r.pos[:], ALU.mult))
                ch.link(ve.tensor_reduce(r.slot[:], r.t[:], AX_X, ALU.add))
                ch.link(ve.tensor_scalar(tiles_i[:], r.incl[:, :, NT - 1], float(P - 1), None, ALU.add))
                ch.link(ve.tensor_scalar(tiles_i[:], tiles_i[:], 7, None, ALU.arith_shift_right))
                ch.link(ve.tensor_copy(cand[:], tiles_i[:]))
                ch.link(ve.tensor_tensor_scan(ends[:], g.w("onerow")[:, 0:NX], cand[:], 0.0, ALU.mult, ALU.add))
                ch.link(ve.tensor_tensor(part[:], ends[:], cand[:], ALU.subtract))
                ch.link(ve.tensor_scalar(part[:], part[:], float(P), None, ALU.mult))
                ch.link(ve.tensor_tensor(r.t[:], r.oh[:], over(part[:]), ALU.mult))
                ch.link(ve.tensor_reduce(r.m2[:], r.t[:], AX_X, ALU.add))
                ch.link(ve.tensor_tensor(r.slot[:], r.slot[:], r.m2[:], ALU.add))
                ch.link(ve.tensor_copy(r.slot_u[:], r.slot[:]))
                ch.link(ve.tensor_tensor(own[:], ends[:].rearrange("p (o e) -> p o e", o=1).broadcast_to([P, PAD_TILES, NX]),
                                         g.w("tileidx").rearrange("p (n o) -> p n o", o=1).broadcast_to([P, PAD_TILES, NX]), ALU.is_le))
                ch.link(ve.tensor_reduce(ownf[:], own[:], AX_X, ALU.add))
                ch.link(ve.tensor_scalar(owner[:], ownf[:], float(NX - 1), None, ALU.min))

        dispatch(nc, g, "ed", r, r.slot_u, win, 2)
        experts(nc, g, "ee", 256, w1[:], w2[:], owner, ACT.Gelu)
        combine(nc, g, "eo", r.slot_u, r.weight)


FILL = -99999.0


def single_cross_stage(nc, g):
    with ExitStack() as ctx:
        sem = sem_maker(nc, ctx, "sa")
        sb = lambda name, shape, dt=F32: ctx.enter_context(nc.sbuf_tensor(f"sa_{name}", shape, dt))
        R = 2
        PPC = BPC // 2
        mask = sb("mask", [P, NT, P], I32)
        mask_in = sem("mask_in")

        def fetch(sp):
            for b in range(2):
                src = g.mask1_dram.rearrange("(o n) k -> o n k", o=1).broadcast_to([S, NT, P])
                sp.dma_start(mask[b * S:(b + 1) * S], src).then_inc(mask_in, 16)
            sp.wait_ge(mask_in, 32)

        norm_stage(nc, g, "n4", fetch=fetch)
        qT, kT, vT = sb("qT", [P, R, CH]), sb("kT", [P, R, CH]), sb("vT", [P, R, CH])
        v = sb("v", [P, R, PPC, D])
        on = sb("on", [P, R, PPC, P])
        low = sb("low", [P, R, PPC, P])
        sc = sb("sc", [P, R, PPC, P])
        pr = sb("pr", [P, R, PPC, P])
        pT = sb("pT", [P, R, PPC, P])
        nmx, rs, ri = sb("nmx", [P, R, PPC]), sb("rs", [P, R, PPC]), sb("ri", [P, R, PPC])
        proj, qkv, vt, vcopy, scored, vch, masked, exped, turned, tcopy, pv, added = (
            sem(n) for n in ("proj", "qkv", "vt", "vcopy", "scored", "vch", "masked", "exped", "turned", "tcopy", "pv", "added"))
        flat = lambda t, r: t[:, r].rearrange("p a k -> p (a k)")
        bank_p, bank_v, bank_s, bank_t, bank_o = g.bank[0:3], g.bank[3], g.bank[4:6], g.bank[6], g.bank[7]

        def run(eng, step):
            with eng.Fori(0, NC // R - 1) as i:
                for r in range(R):
                    step(i * R + r, r, False)
            for r in range(R):
                step(NC - R + r, r, r == R - 1)

        with nc.Block() as block:

            @block.tensor
            def _(pe):
                def project(c):
                    for k, (w, src) in enumerate((("Wq1", g.xT), ("Wk1", g.ctxT), ("Wv1", g.ctxT))):
                        pe.matmul(bank_p[k], g.w(w), src[:, bass.ts(c, CH)], start=True, stop=True).then_inc(proj, 1)

                def scores(c, r):
                    pe.wait_ge(qkv, c * 3 + 2)
                    for p in range(PPC):
                        ps = slice(p * P, (p + 1) * P)
                        ins = pe.matmul(bank_s[r][:, ps], qT[:, r, ps], kT[:, r, ps], start=True, stop=True)
                    ins.then_inc(scored, 1)

                def turn_v(c, r):
                    pe.wait_ge(qkv, c * 3 + 3)
                    pe.wait_ge(vcopy, c + 1)
                    for p in range(PPC):
                        ins = pe.transpose(bank_v[:, p * P:(p + 1) * P], vT[:, r, p * P:(p + 1) * P], g.ident)
                    ins.then_inc(vt, 1)

                def step(c, r, last):
                    if not last:
                        pe.wait_ge(qkv, c * 3 + 3)
                        project(c + 1)
                    pe.wait_ge(exped, c + 1)
                    for p in range(PPC):
                        ins = pe.transpose(bank_t[:, p * P:(p + 1) * P], pr[:, r, p, :], g.ident)
                    ins.then_inc(turned, 1)
                    if not last:
                        scores(c + 1, 1 - r)
                        turn_v(c + 1, 1 - r)
                    pe.wait_ge(tcopy, c + 1)
                    pe.wait_ge(vcopy, c + 2)
                    pe.wait_ge(added, c + 1)
                    for p in range(PPC):
                        ins = pe.matmul(bank_o[:, p * P:(p + 1) * P], pT[:, r, p, :], v[:, r, p, :], start=True, stop=True)
                    ins.then_inc(pv, 1)

                project(0)
                scores(0, 0)
                turn_v(0, 0)
                run(pe, step)

            @block.scalar
            def _(act):
                act.sem_inc(vcopy, 1)
                act.preload_act_table(ACT.Exp)

                def take(c, r):
                    for k, t in enumerate((qT, kT, vT)):
                        act.wait_ge(proj, c * 3 + (k + 1))
                        act.activation(t[:, r, :], bank_p[k], ACT.Copy).then_inc(qkv, 1)
                    act.wait_ge(vt, c + 1)
                    act.activation(flat(v, r), bank_v, ACT.Copy).then_inc(vcopy, 1)
                    act.wait_ge(masked, c + 1)
                    for p in range(PPC):
                        ins = act.activation(pr[:, r, p, :], sc[:, r, p, :], ACT.Exp, bias=nmx[:, r, p:p + 1],
                                             accum_out=rs[:, r, p:p + 1])
                    ins.then_inc(exped, 1)

                def step(c, r, last):
                    if not last:
                        take(c + 1, 1 - r)

                take(0, 0)
                run(act, step)

            @block.vector
            def _(ve):
                PER = 5
                ve.sem_inc(added, 1)

                def link(c, k, ins):
                    ins.then_inc(vch, 1)
                    ve.wait_ge(vch, c * PER + k)

                def mask_scores(c, r):
                    row = lambda w: g.w(w).rearrange("p (o k) -> p o k", o=1).broadcast_to([P, PPC, P])
                    link(c, 1, ve.scalar_tensor_tensor(on[:, r], mask[:, bass.ts(c, PPC), :], 0.0, row("same"), ALU.not_equal, ALU.mult))
                    link(c, 2, ve.scalar_tensor_tensor(low[:, r], on[:, r], 1.0, row("neglow"), ALU.subtract, ALU.mult))
                    ve.wait_ge(scored, c + 1)
                    link(c, 3, ve.tensor_tensor(flat(sc, r), bank_s[r], flat(on, r), ALU.mult))
                    link(c, 4, ve.tensor_tensor(flat(sc, r), flat(sc, r), flat(low, r), ALU.add))
                    ve.tensor_reduce(nmx[:, r, :], sc[:, r], AX_X, ALU.max, negate=True).then_inc(masked, 1)

                def step(c, r, last):
                    ve.wait_ge(turned, c + 1)
                    ve.tensor_copy(flat(pT, r), bank_t).then_inc(tcopy, 1)
                    ve.reciprocal(ri[:, r, :], rs[:, r, :]).then_inc(vch, 1)
                    if not last:
                        mask_scores(c + 1, 1 - r)
                    else:
                        ve.wait_ge(vch, NC * PER)
                    ve.wait_ge(pv, c + 1)
                    for p in range(PPC):
                        x = g.X[:, bass.ds(c * PPC + p, 1), :].rearrange("p a d -> p (a d)")
                        ins = ve.scalar_tensor_tensor(x, bank_o[:, p * P:(p + 1) * P], ri[:, r, p:p + 1], x, ALU.mult, ALU.add)
                    ins.then_inc(added, 1)

                mask_scores(0, 0)
                run(ve, step)


def layout():
    H = E0 // P
    items = [("ident", P), ("norm_w", 1), ("inT", E0), ("skipT", E0), ("convrow", KC * E0), ("conv_b", H), ("wd1T", H * DD),
             ("wd2T", E0), ("wd2_b", H), ("wbcT", H * P), ("A_log", H * NS), ("W_D", H), ("outT", H * D), ("big", 32),
             ("Wq", D), ("bq", 1), ("Wk", D), ("bk", 1), ("Wv", D), ("bv", 1), ("Wo", D), ("bo", D), ("headrow", HG), ("ones", P)]
    for l in range(2):
        items += [(f"sW{l}", GATES * D), (f"sR{l}", GATES * D), (f"sP{l}", D), (f"spb{l}", 1), (f"sga{l}", 1), (f"sbe{l}", 1)]
    items += [("sbrow0", GATES * D), ("sbrow1", GATES * D), ("garow", D), ("berow", D)]
    items += [("Wq1", D), ("Wk1", D), ("Wv1", D), ("same", P), ("neglow", P)]
    items += [("gate0", NX), ("gateb0", NX), ("gate1", NX), ("eidx", NX), ("before", P), ("allones", P), ("onerow", NT), ("spare", NT),
              ("tileidx", PAD_TILES)]
    at, out = 0, {}
    for n, w in items:
        out[n] = (at, w)
        at += w
    return out, at


def program(nc, x, packed, sel, ctxT, bias, mask8, pairsel, moe0, moe1, bits, mask1, out):
    lay, width = layout()
    g = Core()
    g.lay = lay
    with ExitStack() as ctx:
        g.lasting = lambda name: ctx.enter_context(nc.semaphore(name))
        sb = lambda name, shape, dt=F32: ctx.enter_context(nc.sbuf_tensor(name, shape, dt))
        g.X = sb("X", [P, NT, D])
        g.xT = sb("xT", [P, T])
        g.wts = sb("wts", [P, width])
        g.w = lambda n: g.wts[:, lay[n][0]:lay[n][0] + lay[n][1]]
        g.ident = g.w("ident")
        g.zero = sb("zero", [P, CH])
        g.cleared, g.clears = ctx.enter_context(nc.semaphore("cleared")), 0
        g.neghalf = sb("neghalf", [P, NT])
        first, early = lay["inT"][0], lay["Wq"][0]
        g.early_in, g.late_in = ctx.enter_context(nc.semaphore("early_in")), ctx.enter_context(nc.semaphore("late_in"))

        def fetch_weights(sp):
            sp.dma_start(g.wts[:, first:early], packed[:, first:early]).then_inc(g.early_in, 16)
            sp.dma_start(g.wts[:, early:], packed[:, early:]).then_inc(g.late_in, 16)
            sp.dma_start(g.pairsel[:], pairsel).then_inc(g.late_in, 16)
            sp.wait_ge(g.early_in, 16)

        g.fetch_weights = fetch_weights
        g.ctxT, g.ctxT_dram, g.ctxT_in = None, ctxT, ctx.enter_context(nc.semaphore("ctxT_in"))
        g.sel_dram, g.bias_dram, g.mask8_dram = sel, bias, mask8
        g.mask1_dram = mask1
        g.moe0, g.moe1, g.bits_dram = moe0, moe1, bits
        g.buf = nc.dram_tensor("places", (PAD_TILES * P + T, D), F32, kind="Internal").ap()
        g.out = nc.dram_tensor("place_results", (TILES * P, D), F32, kind="Internal").ap()
        g.pairsel = sb("pairsel", [2, P], BF16)
        g.ps = ctx.enter_context(nc.psum_tensor("ps", [P, 8, CH], F32))
        g.bank = [g.ps[:, i, :] for i in range(8)]
        loaded = ctx.enter_context(nc.semaphore("loaded"))
        consts = ctx.enter_context(nc.semaphore("consts"))
        stored = ctx.enter_context(nc.semaphore("stored"))
        with nc.Block() as block:

            @block.sync
            def _(sp):
                sp.dma_start(g.X[:], x.rearrange("(a p) d -> p a d", p=P)).then_inc(loaded, 16)
                sp.dma_start(g.wts[:, 0:first], packed[:, 0:first]).then_inc(loaded, 16)
                sp.wait_ge(loaded, 32)

            @block.vector
            def _(ve):
                ve.memset(g.neghalf[:], -0.5).then_inc(consts, 1)
                ve.memset(g.zero[:], 0.0).then_inc(consts, 1)

        stages = [scan_stage, cross_stage, switch_stage, lstm_stage, single_cross_stage, choice_stage]
        for f in stages:
            if g.ctxT is None and f is not scan_stage:
                g.ctxT = sb("ctxT", [P, T])
            f(nc, g)
        with nc.Block() as block:

            @block.sync
            def _(sp):
                sp.dma_start(out.rearrange("(a p) d -> p a d", p=P), g.X[:]).then_inc(stored, 16)
                sp.wait_ge(stored, 16)


def pack(inp):
    lay, width = layout()
    H = E0 // P
    arr = np.zeros((P, width), np.float32)

    def put(name, a):
        at, w = lay[name]
        a = np.asarray(a)
        arr[:a.shape[0], at:at + a.shape[1]] = a

    halves = lambda a: np.concatenate([a[h * P:(h + 1) * P] for h in range(H)], axis=1)
    rows3 = lambda a: np.where(np.isin(np.arange(P), (0, 32, 64))[:, None], a, np.float32(0.0))
    I = lambda n: np.asarray(inp["L0_attn_" + n])
    put("ident", np.eye(P, dtype=np.float32))
    put("norm_w", I("norm_w")[:, None])
    put("inT", I("in_w").T)
    put("skipT", I("skip_w").T)
    put("convrow", np.broadcast_to(I("conv_w")[:, 0, :].T.reshape(1, KC * E0), (P, KC * E0)))
    put("conv_b", halves(I("conv_b")[:, None]))
    put("wd1T", halves(I("wd1").T))
    put("wd2T", I("wd2").T)
    put("wd2_b", halves(I("wd2_b")[:, None]))
    bc = np.concatenate([I("wb").T, I("wc").T], axis=1)
    put("wbcT", halves(np.concatenate([bc, bc, bc, bc], axis=1)))
    put("A_log", halves(I("A_log")))
    put("W_D", halves(I("W_D")[:, None]))
    put("outT", halves(I("out_w").T))
    put("big", np.full((P, 32), BIG, np.float32))
    I = lambda n: np.asarray(inp["L0_xattn_" + n])
    for n in ("Wq", "Wk", "Wv", "Wo"):
        put(n, I(n))
    put("bq", I("bq")[:, None])
    put("bk", I("bk")[:, None])
    put("bv", I("bv")[:, None])
    put("bo", I("bo")[None, :])
    put("headrow", (np.arange(P)[:, None] // DK % HG == np.arange(HG)[None, :]).astype(np.float32))
    put("ones", np.ones((1, P), np.float32))
    I = lambda n: np.asarray(inp["L1_attn_" + n])
    for l in range(2):
        put(f"sW{l}", I(f"W{l}").T)
        put(f"sR{l}", I(f"R{l}").T)
        put(f"sbrow{l}", rows3(I(f"b{l}").reshape(1, GATES * P)))
        put(f"sP{l}", I(f"projW{l}").T)
        put(f"spb{l}", I(f"projb{l}")[:, None])
        put(f"sga{l}", I(f"gamma{l}")[:, None])
        put(f"sbe{l}", I(f"beta{l}")[:, None])
    for n in ("Wq", "Wk", "Wv"):
        put(n + "1", np.asarray(inp["L1_xattn_" + n]).T)
    same = np.arange(P)[:, None] // S == np.arange(P)[None, :] // S
    put("same", same.astype(np.float32))
    put("neglow", np.where(same, np.float32(-FILL), np.float32(1.0e30)))
    put("gate0", np.asarray(inp["L0_ffn_gate_w"]).T)
    put("gateb0", np.broadcast_to(np.asarray(inp["L0_ffn_gate_b"])[None, :], (P, NX)))
    put("gate1", inp["L1_ffn_Wg"])
    put("eidx", np.broadcast_to(np.arange(NX, dtype=np.float32)[None, :], (P, NX)))
    put("before", np.triu(np.ones((P, P), np.float32), 1))
    put("allones", np.ones((P, P), np.float32))
    put("onerow", np.ones((P, NT), np.float32))
    put("spare", (np.arange(NT)[None, :] * P + np.arange(P)[:, None] + PAD_TILES * P).astype(np.float32))
    put("tileidx", np.broadcast_to(np.arange(PAD_TILES, dtype=np.float32)[None, :], (P, PAD_TILES)))
    put("garow", np.broadcast_to(I("gamma1")[None, :], (P, D)))
    put("berow", np.broadcast_to(I("beta1")[None, :], (P, D)))
    return arr


def relative(rel_bias):
    rel = np.asarray(rel_bias)
    span = rel.shape[1] // 2
    at = np.arange(S)[:, None] - np.arange(S)[None, :] + span
    one = rel[:, at].transpose(1, 0, 2)
    return np.ascontiguousarray(np.concatenate([one, one], axis=0))


def selectors():
    s = np.zeros((P, 2 * NS, P), mybir.dt.np(BF16))
    for q in (0, 2, 3):
        for n in range(2 * NS):
            s[32 * q + n, n, :] = 1
    return s


def kernel(**inputs):
    import concourse.bacc as bacc
    from concourse.bass_utils import run_bass_kernel_spmd as run

    nc = bacc.Bacc("TRN2", target_bir_lowering=False, num_devices=1)
    arrays = {"x": np.ascontiguousarray(np.asarray(inputs["x"]).reshape(T, D)), "packed": pack(inputs), "sel": selectors()}
    arrays["ctxT"] = np.ascontiguousarray(np.asarray(inputs["ctx_1024"]).reshape(T, D).T)
    arrays["bias"] = relative(inputs["L0_xattn_rel_bias"])
    arrays["mask8"] = np.ascontiguousarray(np.asarray(inputs["mask_BxS2_bf0"]).view(np.uint8).reshape(NT, 2, S).transpose(1, 0, 2).reshape(2, T // 2)).view(np.int32)
    arrays["pairsel"] = np.repeat(np.eye(2), S, axis=1).astype(mybir.dt.np(BF16))
    arrays["mask1"] = np.ascontiguousarray(np.asarray(inputs["mask_BxS2_ik1"]).reshape(NT, 2 * S))
    I = lambda n: np.asarray(inputs[n])
    for l, F in ((0, 512), (1, 256)):
        w1, w2 = (I("L0_ffn_w1"), I("L0_ffn_w2")) if l == 0 else (I("L1_ffn_W1"), I("L1_ffn_W2"))
        arrays[f"w1_{l}"] = np.ascontiguousarray(w1.transpose(1, 0, 2).reshape(P, NX * F))
        arrays[f"w2_{l}"] = np.ascontiguousarray(w2.reshape(NX, F // P, P, D).transpose(2, 0, 1, 3).reshape(P, NX * F))
    arrays["b1_0"] = np.ascontiguousarray(np.broadcast_to(I("L0_ffn_b1").reshape(1, -1), (P, NX * 512)))
    arrays["b2_0"] = np.ascontiguousarray(np.broadcast_to(I("L0_ffn_b2").reshape(1, -1), (P, NX * D)))
    arrays["owner0"] = np.minimum(np.arange(PAD_TILES) // (CAP // P), NX - 1).astype(np.int32)[None, :]
    high = np.arange(BITS - 1, 0, -2)
    ways = np.stack([0 * high, 1 << (high - 1), 1 << high, (1 << high) | (1 << (high - 1))], axis=1)
    arrays["bits"] = np.ascontiguousarray(np.broadcast_to(ways.reshape(1, -1), (P, BITS // 2 * WAYS))).astype(np.int32)
    ap = {n: nc.dram_tensor("in_" + n, a.shape, mybir.dt.from_np(a.dtype), kind="ExternalInput").ap() for n, a in arrays.items()}
    out = nc.dram_tensor("out_0_dram", (T, D), F32, kind="ExternalOutput").ap()
    moe0 = {"w1": ap["w1_0"], "w2": ap["w2_0"], "b1": ap["b1_0"], "b2": ap["b2_0"], "owner": ap["owner0"]}
    moe1 = {"w1": ap["w1_1"], "w2": ap["w2_1"]}
    program(nc, ap["x"], ap["packed"], ap["sel"], ap["ctxT"], ap["bias"], ap["mask8"], ap["pairsel"], moe0, moe1, ap["bits"], ap["mask1"], out)
    r = run(nc, [{"in_" + n: a for n, a in arrays.items()}], core_ids=[0])
    return r.results[0]["out_0_dram"].reshape(B, S, D)
```

```python
from contextlib import ExitStack

import numpy as np

import concourse.bass as bass
from concourse import mybir

ALU = mybir.AluOpType
ACT = mybir.ActivationFunctionType
F32 = mybir.dt.float32
BF16 = mybir.dt.bfloat16
I32 = mybir.dt.int32
U32 = mybir.dt.uint32
AX_X = mybir.AxisListType.X

P = 128
B, S, D = 64, 64, 128
T = B * S
NT = T // P
CH = 512
NC = T // CH
TPC = CH // P
BPC = CH // S
E0 = 256
NS = 16
DD = 64
KC = 4
EPS = 1e-5
BIG = 1.0e30



class Core:
    pass


class Chain:

    def __init__(self, eng, sem):
        self.eng, self.sem, self.n = eng, sem, 0
        self.i, self.per = None, 0

    def enter(self, i, per):
        self.i, self.per, self.base, self.n = i, per, self.n, 0

    def leave(self, times):
        assert self.n == self.per, (self.n, self.per)
        self.n, self.i = self.base + times * self.per, None

    def value(self):
        return self.n if self.i is None else self.i * self.per + (self.base + self.n)

    def inc(self, ins):
        ins.then_inc(self.sem, 1)
        self.n += 1

    def link(self, ins):
        self.inc(ins)
        self.eng.wait_ge(self.sem, self.value())


def alone(eng):
    eng.nop(nofuse=True)


def sem_maker(nc, ctx, tag):
    made = []

    def clear():
        for s in made:
            nc.sync.sem_clear(s)
        nc.all_engine_barrier()

    ctx.callback(clear)

    def make(name):
        made.append(ctx.enter_context(nc.semaphore(f"{tag}_{name}")))
        return made[-1]

    return make


def norm_stage(nc, g, tag, rms=False, gain=None, keep=False, place=None, fetch=None, prior=None):
    with ExitStack() as ctx:
        sem = sem_maker(nc, ctx, tag)
        sb = lambda name, shape, dt=F32: ctx.enter_context(nc.sbuf_tensor(f"{tag}_{name}", shape, dt))
        stat, vchain, var_ready, rstd_ready = sem("stat"), sem("vchain"), sem("var_ready"), sem("rstd_ready")
        rows_ready, turned, evac, kept, centred = sem("rows_ready"), sem("turned"), sem("evac"), sem("kept"), sem("centred")
        square_ready, rr_ready = sem("square_ready"), sem("rr_ready")
        R = 4
        PARTS = 4
        PT = NT // PARTS
        st = sb("st", [P, NT, 6])
        a, b, mean, var, rstd, rr = (sb(n, [P, NT]) for n in ("a", "b", "mean", "var", "rstd", "rr"))
        xc = sb("xc", [P, R, TPC, D])
        xr = sb("xr", [P, R, TPC, D])
        rows = lambda c: g.rows[:, c * TPC:(c + 1) * TPC, :] if keep else xr[:, c % R]
        with nc.Block() as block:

            if fetch is not None:
                @block.sync
                def _(sp):
                    fetch(sp)

            @block.vector
            def _(ve):
                ch = Chain(ve, vchain)

                def moments(part):
                    h = slice(part * PT, (part + 1) * PT)
                    if prior is not None:
                        prior.add(ve, range(part * PT, (part + 1) * PT))
                        ve.wait_ge(prior.added, (part + 1) * PT)
                    for t in range(part * PT, (part + 1) * PT):
                        ve.bn_stats(st[:, t, :], g.X[:, t, :]).then_inc(stat, 1)
                    ve.wait_ge(stat, (part + 1) * PT)
                    ch.inc(ve.tensor_tensor(b[:, h], st[:, h, 1], st[:, h, 4], ALU.subtract))
                    ch.inc(ve.tensor_tensor(a[:, h], st[:, h, 1], st[:, h, 4], ALU.add))
                    ch.link(ve.tensor_tensor(var[:, h], st[:, h, 2], st[:, h, 5], ALU.add))
                    ch.link(ve.scalar_tensor_tensor(b[:, h], b[:, h], 0.25, b[:, h], ALU.mult, ALU.mult))
                    ch.inc(ve.tensor_scalar(mean[:, h], a[:, h], 0.5, None, ALU.mult))
                    ch.link(ve.scalar_tensor_tensor(var[:, h], var[:, h], 1.0 / D, b[:, h], ALU.mult, ALU.add))
                    ve.tensor_scalar(a[:, h], var[:, h], EPS, None, ALU.add).then_inc(var_ready, 1)

                def square(part):
                    h = slice(part * PT, (part + 1) * PT)
                    ve.wait_ge(rstd_ready, part + 1)
                    ch.link(ve.tensor_tensor(b[:, h], rstd[:, h], rstd[:, h], ALU.mult))
                    ch.link(ve.tensor_tensor(b[:, h], b[:, h], var[:, h], ALU.mult))
                    ve.tensor_scalar(b[:, h], b[:, h], EPS, None, ALU.add).then_inc(square_ready, 1)

                def normalise(part):
                    for c in range(part * PT // TPC, (part + 1) * PT // TPC):
                        k = c % R
                        if c % (PT // TPC) == 0:
                            ve.wait_ge(rr_ready if rms else rstd_ready, part + 1)
                        if c >= R:
                            ve.wait_ge(turned, c - R + 1)
                            if rms:
                                ve.wait_ge(kept, c - R + 1)
                        for j in range(TPC):
                            t = c * TPC + j
                            ins = ve.tensor_scalar((xc[:, k] if rms else rows(c))[:, j, :], g.X[:, t, :], mean[:, t:t + 1], rstd[:, t:t + 1],
                                                   ALU.subtract, ALU.mult)
                        if not rms:
                            ins.then_inc(rows_ready, 1)
                        else:
                            ins.then_inc(centred, 1)
                            ve.wait_ge(centred, c + 1)
                            over = rr[:, c * TPC:(c + 1) * TPC].rearrange("p (a o) -> p a o", o=1).broadcast_to([P, TPC, D])
                            ve.tensor_tensor(rows(c), xc[:, k], over, ALU.mult).then_inc(rows_ready, 1)

                moments(0)
                for part in range(PARTS):
                    if part + 1 < PARTS:
                        moments(part + 1)
                    if rms:
                        square(part)
                        if part >= 1:
                            normalise(part - 1)
                    else:
                        normalise(part)
                if rms:
                    normalise(PARTS - 1)

            @block.gpsimd
            def _(pool):
                def root(part):
                    h = slice(part * PT, (part + 1) * PT)
                    pool.wait_ge(var_ready, part + 1)
                    pool.tensor_tensor(rstd[:, h], a[:, h], g.neghalf[:, h], ALU.pow).then_inc(rstd_ready, 1)

                def root_of_square(part):
                    h = slice(part * PT, (part + 1) * PT)
                    pool.wait_ge(square_ready, part + 1)
                    pool.tensor_tensor(rr[:, h], b[:, h], g.neghalf[:, h], ALU.pow).then_inc(rr_ready, 1)

                def add_residual(part):
                    for c in range(part * PT // TPC, (part + 1) * PT // TPC):
                        tiles = slice(c * TPC, (c + 1) * TPC)
                        pool.wait_ge(centred, c + 1)
                        pool.tensor_tensor(g.X[:, tiles, :], g.X[:, tiles, :], xc[:, c % R], ALU.add).then_inc(kept, 1)

                def gather(part):
                    if prior is not None and part < PARTS:
                        prior.gather(pool, range(part * PT, (part + 1) * PT))

                gather(0)
                gather(1)
                root(0)
                for part in range(PARTS):
                    gather(part + 2)
                    if part + 1 < PARTS:
                        root(part + 1)
                    if rms:
                        root_of_square(part)
                        add_residual(part)

            @block.tensor
            def _(pe):
                for c in range(NC):
                    pe.wait_ge(rows_ready, c + 1)
                    if c >= R:
                        pe.wait_ge(evac, c - R + 1)
                    for j in range(TPC):
                        ins = pe.transpose(g.bank[c % R][:, j * P:(j + 1) * P], rows(c)[:, j, :], g.ident[:])
                    ins.then_inc(turned, 1)

            @block.scalar
            def _(act):
                for c in range(NC):
                    act.wait_ge(turned, c + 1)
                    out = place(c) if place else g.xT[:, c * CH:(c + 1) * CH]
                    src = g.bank[c % R] if place is None else g.bank[c % R].rearrange("p (b s) -> p b s", s=S)
                    act.activation(out, src, ACT.Identity, scale=gain if gain is not None else 1.0).then_inc(evac, 1)


def scan_stage(nc, g):
    H = E0 // P
    tag = "scan"
    norm_stage(nc, g, "n0", rms=True, gain=g.w("norm_w"), fetch=g.fetch_weights)
    with ExitStack() as ctx:
        sem = sem_maker(nc, ctx, tag)
        sb = lambda name, shape, dt=F32: ctx.enter_context(nc.sbuf_tensor(f"{tag}_{name}", shape, dt))
        xs = sb("xs", [P, H, T])
        delta = sb("delta", [P, H, T])
        parts = sb("parts", [P, T], BF16)
        sel = sb("sel", [P, 2 * NS, P], BF16)
        negA = sb("negA", [P, H * NS])
        sel_in = sem("sel_in")

        def paired(eng, step):
            with eng.Fori(0, NC // 2 - 1) as i:
                for r in range(2):
                    step(i * 2 + r, r, False)
            for r in range(2):
                step(NC - 2 + r, r, r == 1)

        with ExitStack() as c2:
            sem2 = sem_maker(nc, c2, "proj")
            acc = c2.enter_context(nc.sbuf_tensor("proj_acc", [P, 2, H, CH], F32))
            proj, tap, conv, silu, exped, negd = (sem2(n) for n in ("proj", "tap", "conv", "silu", "exped", "negd"))
            chain = sem2("chain")
            by_batch = lambda t: t.rearrange("p (b s) -> p b s", s=S)
            with nc.Block() as block:

                @block.sync
                def _(sp):
                    sp.dma_start(sel[:], g.sel_dram).then_inc(sel_in, 16)

                @block.tensor
                def _(pe):
                    with pe.Fori(0, NC // 2) as i:
                        for r in range(2):
                            c = i * 2 + r
                            pe.wait_ge(conv, c * H + H)
                            for h in range(H):
                                pe.matmul(g.bank[2 * r + h], g.w("inT")[:, h * P:(h + 1) * P], g.xT[:, bass.ts(c, CH)],
                                          start=True, stop=True).then_inc(proj, 1)

                @block.scalar
                def _(act):
                    act.activation(negA[:], g.w("A_log"), ACT.Exp).then_inc(exped, 1)
                    act.sem_inc(silu, 2)
                    act.preload_act_table(ACT.Silu)

                    def last_tap(c, r):
                        act.wait_ge(silu, c + 1)
                        for h in range(H):
                            act.wait_ge(proj, c * H + (h + 1))
                            act.activation(acc[:, r, h, :], g.bank[2 * r + h], ACT.Identity, bias=g.w("conv_b")[:, h:h + 1],
                                           scale=g.w("convc")[:, h * KC + KC - 1:h * KC + KC]).then_inc(tap, 1)

                    def step(c, r, last):
                        if not last:
                            last_tap(c + 1, 1 - r)
                        act.wait_ge(conv, c * H + 3 * H)
                        act.activation(xs[:, :, bass.ts(c, CH)], acc[:, r], ACT.Silu).then_inc(silu, 1)

                    last_tap(0, 0)
                    paired(act, step)

                @block.vector
                def _(ve):
                    ve.sem_inc(conv, 2 * H)
                    ve.wait_ge(exped, 1)
                    ve.tensor_scalar(negA[:], negA[:], -1.0, None, ALU.mult).then_inc(negd, 1)

                    def step(c, r, last):
                        for k in range(1, KC):
                            for h in range(H):
                                if k == 1:
                                    ve.wait_ge(tap, c * H + (h + 1))
                                else:
                                    ve.wait_ge(chain, c * (2 * H) + ((k - 2) * H + h + 1))
                                out = by_batch(acc[:, r, h, :])[:, :, k:S]
                                src = by_batch(g.bank[2 * r + h])[:, :, 0:S - k]
                                at = h * KC + KC - 1 - k
                                ins = ve.scalar_tensor_tensor(out, src, g.w("convc")[:, at:at + 1], out, ALU.mult, ALU.add)
                                ins.then_inc(chain if k < KC - 1 else conv, 1)

                    paired(ve, step)
                    ve.wait_ge(sel_in, 16)

        with ExitStack() as c2:
            sem2 = sem_maker(nc, c2, "dl")
            t1 = c2.enter_context(nc.sbuf_tensor("dl_t1", [DD, 2, CH], F32))
            xb = c2.enter_context(nc.sbuf_tensor("dl_xb", [P, 2, H, CH], F32))
            lg = c2.enter_context(nc.sbuf_tensor("dl_lg", [P, 2, H, CH], F32))
            res = c2.enter_context(nc.sbuf_tensor("dl_res", [P, 2, CH], F32))
            d1, d1c, d2, bc, clampd, ex, ln_, dl, split = (sem2(n) for n in ("d1", "d1c", "d2", "bc", "clampd", "ex", "ln", "dl", "split"))
            bank_1, bank_bc, bank_2 = g.bank[0:2], g.bank[2:4], (g.bank[4:6], g.bank[6:8])
            SPLITS = 3
            high, rest = sem2("high"), sem2("rest")
            with nc.Block() as block:

                @block.tensor
                def _(pe):
                    pe.sem_inc(d2, 2)

                    def narrow(c, r):
                        pe.wait_ge(d1c, c + 1)
                        for h in range(H):
                            ins = pe.matmul(bank_1[r][0:DD, :], g.w("wd1T")[:, h * DD:(h + 1) * DD], xs[:, h, bass.ts(c, CH)],
                                            start=(h == 0), stop=(h == H - 1))
                        ins.then_inc(d1, 1)

                    def step(c, r, last):
                        pe.wait_ge(d1c, c + 3)
                        pe.wait_ge(dl, c + 1)
                        for h in range(H):
                            ins = pe.matmul(bank_2[r][h], g.w("wd2T")[0:DD, h * P:(h + 1) * P], t1[:, r, :], start=True, stop=True)
                        ins.then_inc(d2, 1)
                        pe.wait_ge(rest, c + 1)
                        for h in range(H):
                            ins = pe.matmul(bank_bc[r], g.w("wbcT")[:, h * P:(h + 1) * P], xs[:, h, bass.ts(c, CH)],
                                            start=(h == 0), stop=(h == H - 1))
                        ins.then_inc(bc, 1)
                        if not last:
                            narrow(c + 1, 1 - r)

                    narrow(0, 0)
                    paired(pe, step)

                @block.scalar
                def _(act):
                    act.sem_inc(d1c, 2)
                    act.preload_act_table_set("natural_log_exp_and_others")

                    def take(c, r):
                        act.wait_ge(d1, c + 1)
                        act.wait_ge(d2, c + 1)
                        act.activation(t1[:, r, :], bank_1[r][0:DD, :], ACT.Copy).then_inc(d1c, 1)

                    def step(c, r, last):
                        if not last:
                            take(c + 1, 1 - r)
                        act.wait_ge(clampd, c + 1)
                        act.activation(xb[:, r], xb[:, r], ACT.Exp).then_inc(ex, 1)
                        act.wait_ge(ex, c + 1)
                        act.activation(lg[:, r], xb[:, r], ACT.Ln, bias=1.0).then_inc(ln_, 1)

                    take(0, 0)
                    paired(act, step)

                @block.vector
                def _(ve):
                    ve.sem_inc(rest, 2)
                    ve.sem_inc(dl, 2)

                    def step(c, r, last):
                        cs = bass.ts(c, CH)
                        ve.wait_ge(d2, c + 3)
                        for h in range(H):
                            ins = ve.tensor_scalar(xb[:, r, h, :], bank_2[r][h], g.w("wd2_b")[:, h:h + 1], 40.0, ALU.add, ALU.min)
                        ins.then_inc(clampd, 1)
                        ve.wait_ge(bc, c + 1)
                        alone(ve)
                        ve.tensor_copy(parts[:, cs], bank_bc[r]).then_inc(high, 1)
                        ve.wait_ge(high, c + 1)
                        ve.wait_ge(split, c * SPLITS + SPLITS)
                        ve.tensor_tensor(res[:, r], bank_bc[r], parts[:, cs], ALU.subtract).then_inc(rest, 1)
                        ve.wait_ge(ln_, c + 1)
                        for h in range(H):
                            ins = ve.scalar_tensor_tensor(delta[:, h, cs], bank_2[r][h], g.w("wd2_b")[:, h:h + 1],
                                                          lg[:, r, h, :], ALU.add, ALU.max)
                        ins.then_inc(dl, 1)

                    paired(ve, step)

                @block.gpsimd
                def _(pool):
                    pool.sem_inc(split, 2 * SPLITS)

                    def step(c, r, last):
                        cs = bass.ts(c, CH)
                        pool.wait_ge(rest, c + 3)
                        for k, f in enumerate((
                                lambda: pool.tensor_copy(parts[64:128, cs], res[64:128, r]),
                                lambda: pool.tensor_tensor(res[96:128, r], res[96:128, r], parts[96:128, cs], ALU.subtract),
                                lambda: pool.tensor_copy(parts[96:128, cs], res[96:128, r]))):
                            alone(pool)
                            f().then_inc(split, 1)
                            pool.wait_ge(split, c * SPLITS + (2 * SPLITS + 1 + k))

                    paired(pool, step)

        with ExitStack() as c2:
            sem2 = sem_maker(nc, c2, "rec")
            sb2 = lambda name, shape, dt=F32: c2.enter_context(nc.sbuf_tensor(f"rec_{name}", shape, dt))
            SR, LR = 2, 4
            dx = sb2("dx", [P, H, CH])
            dec = sb2("dec", [P, SR, H * CH])
            u = sb2("u", [P, LR, H * CH])
            hst = sb2("hst", [P, SR, H * CH])
            hc = sb2("hc", [P, LR, H * CH])
            cb = sb2("cb", [P, LR, CH])
            bank_b, bank_c, bank_y = g.bank[0:2], g.bank[2:6], g.bank[6:8]
            bready, cready, decay, ccopy, uready, hready, hcready, summed, dxr, reset, yout = (
                sem2(n) for n in ("bready", "cready", "decay", "ccopy", "uready", "hready", "hcready", "summed", "dxr", "reset", "yout"))
            three = lambda t: t.rearrange("p (h t) -> p h t", h=H)
            over_h = lambda t: t.rearrange("p (o t) -> p o t", o=1).broadcast_to([P, H, CH])
            with nc.Block() as block:

                @block.tensor
                def _(pe):
                    LEAD = 3
                    pe.sem_inc(summed, LR)

                    def broadcasts(c, n):
                        pe.wait_ge(uready, c * NS + (n + 1))
                        pe.matmul(bank_b[n % SR], sel[:, n, :], parts[:, bass.ts(c, CH)], start=True, stop=True).then_inc(bready, 1)
                        pe.wait_ge(ccopy, c * NS + (n + 1))
                        pe.matmul(bank_c[n % LR], sel[:, NS + n, :], parts[:, bass.ts(c, CH)], start=True, stop=True).then_inc(cready, 1)

                    def chunk(c, last):
                        for n in range(NS):
                            if n + LEAD < NS:
                                broadcasts(c, n + LEAD)
                            elif not last:
                                broadcasts(c + 1, n + LEAD - NS)
                            if n == 0:
                                pe.wait_ge(yout, c + 1)
                            pe.wait_ge(hcready, c * NS + (n + 1 + LR))
                            for h in range(H):
                                ins = pe.matmul(bank_y[h], g.ident, hc[:, n % LR, h * CH:(h + 1) * CH], start=(n == 0), stop=(n == NS - 1))
                            ins.then_inc(summed, 1)

                    for n in range(LEAD):
                        broadcasts(0, n)
                    with pe.Fori(0, NC - 1) as c:
                        chunk(c, False)
                    chunk(NC - 1, True)

                @block.scalar
                def _(act):
                    act.sem_inc(ccopy, LR)
                    act.preload_act_table(ACT.Exp)
                    with act.Fori(0, NC) as c:
                        act.wait_ge(reset, c + 1)
                        for n in range(NS):
                            act.wait_ge(hready, c * NS + (n + 1 + LR - SR))
                            alone(act)
                            for h in range(H):
                                ins = act.activation(dec[:, n % SR, h * CH:(h + 1) * CH], delta[:, h, bass.ts(c, CH)],
                                                     ACT.Exp, scale=negA[:, h * NS + n:h * NS + n + 1])
                            ins.then_inc(decay, 1)
                            act.wait_ge(cready, c * NS + (n + 1))
                            act.wait_ge(hcready, c * NS + (n + 1))
                            act.activation(cb[:, n % LR, :], bank_c[n % LR], ACT.Copy).then_inc(ccopy, 1)

                @block.vector
                def _(ve):
                    ve.sem_inc(uready, SR)
                    ve.sem_inc(hready, LR)
                    ve.sem_inc(yout, 1)

                    def prepare(c):
                        ve.wait_ge(uready, c * NS + SR)
                        ve.tensor_tensor(dx[:], delta[:, :, bass.ts(c, CH)], xs[:, :, bass.ts(c, CH)], ALU.mult).then_inc(dxr, 1)
                        ve.wait_ge(dxr, c + 1)
                        alone(ve)
                        ve.tensor_copy(delta[:, :, bass.ts(c, CH)].rearrange("p h (b s) -> p h b s", s=S)[:, :, :, 0],
                                       g.w("big")[:, 0:H * BPC].rearrange("p (h b) -> p h b", h=H)).then_inc(reset, 1)

                    def form_u(c, n):
                        ve.wait_ge(bready, c * NS + (n + 1))
                        ve.wait_ge(hready, c * NS + (n + 1))
                        ve.tensor_tensor(three(u[:, n % LR, :]), dx[:], over_h(bank_b[n % SR]), ALU.mult).then_inc(uready, 1)

                    def scan(c, n, last=False):
                        if n + 1 < NS:
                            form_u(c, n + 1)
                        elif not last:
                            prepare(c + 1)
                            form_u(c + 1, 0)
                        ve.wait_ge(decay, c * NS + (n + 1))
                        ve.wait_ge(uready, c * NS + (n + 1 + SR))
                        ve.wait_ge(hcready, c * NS + (n + 1 + LR - SR))
                        ve.tensor_tensor_scan(hst[:, n % SR, :], dec[:, n % SR, :], u[:, n % LR, :], 0.0,
                                              ALU.mult, ALU.add).then_inc(hready, 1)

                    def read_out(c):
                        ve.wait_ge(summed, c * NS + (NS + LR))
                        for h in range(H):
                            ins = ve.scalar_tensor_tensor(xs[:, h, bass.ts(c, CH)], xs[:, h, bass.ts(c, CH)],
                                                          g.w("W_D")[:, h:h + 1], bank_y[h], ALU.mult, ALU.add)
                        ins.then_inc(yout, 1)

                    AHEAD = 2
                    prepare(0)
                    form_u(0, 0)
                    for n in range(AHEAD):
                        scan(0, n)
                    with ve.Fori(0, NC - 1) as c:
                        for n in range(AHEAD, NS):
                            scan(c, n)
                        for n in range(AHEAD):
                            scan(c + 1, n)
                        read_out(c)
                    for n in range(AHEAD, NS):
                        scan(NC - 1, n, last=True)
                    read_out(NC - 1)

                @block.gpsimd
                def _(pool):
                    pool.sem_inc(hcready, LR)
                    with pool.Fori(0, NC) as c:
                        for n in range(NS):
                            pool.wait_ge(hready, c * NS + (n + 1 + LR))
                            pool.wait_ge(ccopy, c * NS + (n + 1 + LR))
                            pool.wait_ge(summed, c * NS + (n + 1))
                            pool.tensor_tensor(three(hc[:, n % LR, :]), three(hst[:, n % SR, :]), over_h(cb[:, n % LR, :]), ALU.mult).then_inc(hcready, 1)

        with ExitStack() as c2:
            sem2 = sem_maker(nc, c2, "go")
            gate = c2.enter_context(nc.sbuf_tensor("go_gate", [P, 2, H, CH], F32))
            yg = c2.enter_context(nc.sbuf_tensor("go_yg", [P, 2, H, CH], F32))
            skip, gated, mult, proj, added = (sem2(n) for n in ("skip", "gated", "mult", "proj", "added"))
            bank_s, bank_o = (g.bank[0:2], g.bank[2:4]), g.bank[4:6]
            with nc.Block() as block:

                @block.tensor
                def _(pe):
                    def skips(c, r):
                        pe.wait_ge(gated, c * H + H)
                        for h in range(H):
                            pe.matmul(bank_s[r][h], g.w("skipT")[:, h * P:(h + 1) * P], g.xT[:, bass.ts(c, CH)],
                                      start=True, stop=True).then_inc(skip, 1)

                    def step(c, r, last):
                        if not last:
                            skips(c + 1, 1 - r)
                        pe.wait_ge(mult, c + 3)
                        pe.wait_ge(added, c + 1)
                        for j in range(TPC):
                            for h in range(H):
                                ins = pe.matmul(bank_o[r][:, j * P:(j + 1) * P], yg[:, r, h, j * P:(j + 1) * P],
                                                g.w("outT")[:, h * D:(h + 1) * D], start=(h == 0), stop=(h == H - 1))
                        ins.then_inc(proj, 1)

                    skips(0, 0)
                    paired(pe, step)

                @block.scalar
                def _(act):
                    act.preload_act_table(ACT.Silu)
                    act.sem_inc(gated, 2 * H)
                    with act.Fori(0, NC // 2) as i:
                        for r in range(2):
                            c = i * 2 + r
                            act.wait_ge(mult, c + 1)
                            for h in range(H):
                                act.wait_ge(skip, c * H + (h + 1))
                                act.activation(gate[:, r, h, :], bank_s[r][h], ACT.Silu).then_inc(gated, 1)

                @block.vector
                def _(ve):
                    ve.sem_inc(mult, 2)
                    ve.sem_inc(added, 2)

                    def gate_y(c, r):
                        ve.wait_ge(gated, c * H + 3 * H)
                        ve.tensor_tensor(yg[:, r], xs[:, :, bass.ts(c, CH)], gate[:, r], ALU.mult).then_inc(mult, 1)

                    def step(c, r, last):
                        if not last:
                            gate_y(c + 1, 1 - r)
                        ve.wait_ge(proj, c + 1)
                        xc = g.X[:, bass.ts(c, TPC), :].rearrange("p a d -> p (a d)")
                        ve.tensor_tensor(xc, xc, bank_o[r], ALU.add).then_inc(added, 1)

                    gate_y(0, 0)
                    paired(ve, step)


NH, DK = 16, 8
HG = NH // 2
NG = NH // HG
VW = 2 * (DK + 1)


def cross_stage(nc, g):
    def fetch(sp):
        sp.dma_start(g.ctxT[:], g.ctxT_dram).then_inc(g.ctxT_in, 16)
        sp.wait_ge(g.ctxT_in, 16)
        sp.wait_ge(g.late_in, 32)

    norm_stage(nc, g, "n1", fetch=fetch)
    with ExitStack() as ctx:
        sem = sem_maker(nc, ctx, "ca")
        sb = lambda name, shape, dt=F32: ctx.enter_context(nc.sbuf_tensor(f"ca_{name}", shape, dt))
        R = 2
        qg = sb("qg", [P, R, NG, CH])
        ks = sb("ks", [P, NG, CH])
        kd = sb("kd", [P, R, NG, BPC // 2, HG, S])
        vT = sb("vT", [P, R, BPC, 2, S])
        vd = sb("vd", [P, R, BPC, NH // 2, VW])
        bias = sb("bias", [P, NH, S])
        mask8 = sb("mask8", [2, T // 8], I32)
        maskneg = sb("maskneg", [2, NT, S], BF16)
        qbias = sb("qbias", [P, NG])
        sc = sb("sc", [P, 2, NH, S])
        pr = sb("pr", [P, 2, NH * S])
        mx = sb("mx", [P, 2, NH])
        pT = sb("pT", [P, 2, NH // 2, P])
        ri = sb("ri", [P, 2, NH])
        o = sb("o", [P, 2, D])
        oT = sb("oT", [P, 2, D])
        bias_in, init, kb = sem("bias_in"), sem("init"), sem("kb")
        with nc.Block() as block:

            @block.sync
            def _(sp):
                sp.dma_start(bias[:], g.bias_dram).then_inc(bias_in, 16)
                sp.dma_start(mask8[:], g.mask8_dram).then_inc(bias_in, 16)
                sp.wait_ge(bias_in, 32)

            @block.gpsimd
            def _(pool):
                pool.memset(qg[:], 0.0).then_inc(init, 1)
                pool.memset(vd[:], 0.0).then_inc(init, 1)
                pool.wait_ge(init, 2)
                for h2 in range(2):
                    col = h2 * (DK + 1) + DK
                    pool.memset(vd[h2 * S:(h2 + 1) * S, :, :, :, col:col + 1].rearrange("p r b j o -> p (r b j) o"), 1.0).then_inc(init, 1)

            @block.vector
            def _(ve):
                ve.tensor_scalar(qbias[:], g.w("bq"), DK ** -0.5, None, ALU.mult).then_inc(kb, 1)
                ve.wait_ge(bias_in, 32)
                ve.tensor_scalar(maskneg[:], mask8[:].bitcast(mybir.dt.uint8).rearrange("a (n k) -> a n k", k=S), -1.0e30, None, ALU.mult).then_inc(kb, 1)

        proj, qkv, vt, vcopy = sem("proj"), sem("qkv"), sem("vt"), sem("vcopy")
        spread = sem("spread0"), sem("spread1")
        PPC = BPC // 2
        PROJ = ("K0", "K1", "Q0", "Q1", "V")
        NPR = len(PROJ)

        def diagonal(eng, c, r, group, part):
            if part == 0:
                eng.wait_ge(qkv, c * NPR + (group + 1))
            pairs = slice(part * PPC // 2, (part + 1) * PPC // 2)
            for b in range(2):
                rows = slice(b * S, (b + 1) * S)
                k = ks[rows, group, :].rearrange("p (n o b s) -> p n o b s", o=1, b=2, s=S)[:, pairs, :, b, :].broadcast_to([S, PPC // 2, HG, S])
                m = g.w("headrow")[rows, :].rearrange("p (o h t) -> p o h t", o=1, t=1).broadcast_to([S, PPC // 2, HG, S])
                ins = eng.tensor_tensor(kd[rows, r, group, pairs], k, m, ALU.mult)
            ins.then_inc(spread[group], 1)

        scored, biased, maxed, shifted, exped, turned, tcopy, pv, rinv, normed, oturned, ocopy, outp, added = (
            sem(n) for n in ("scored", "biased", "maxed", "shifted", "exped", "turned", "tcopy", "pv", "rinv", "normed",
                             "oturned", "ocopy", "outp", "added"))
        bank_s = [g.ps[:, 1:3, :], g.ps[:, 3:5, :]]
        bank_t = g.ps[:, 5:7, :]
        bank_o = g.bank[7]
        T_AT, F_AT = 2 * P, 3 * P
        bank_p = g.bank[0]
        LEAD = 2

        def run(eng, slot):
            slot(0, 0, 0, True, False)
            with eng.Fori(0, NC // R - 1) as i:
                for k in range(1, R * PPC + 1):
                    slot(i * R + k // PPC, k // PPC % R, k % PPC, False, False)
            for k in range(1, R * PPC):
                slot(NC - R + k // PPC, k // PPC % R, k % PPC, False, k // PPC == R - 1)

        with nc.Block() as block:

            @block.gpsimd
            def _(pool):
                for group in range(NG):
                    pool.sem_inc(spread[group], 2)
                with pool.Fori(0, NC // R) as i:
                    for r in range(R):
                        for part in range(2):
                            for group in range(NG):
                                diagonal(pool, i * R + r, r, group, part)

            @block.tensor
            def _(pe):
                def project(c, k):
                    name = PROJ[k]
                    if k == 0:
                        pe.wait_ge(vcopy, c * 2 + 1)
                    else:
                        pe.wait_ge(qkv, c * NPR + k)
                    src = g.xT if name[0] == "Q" else g.ctxT
                    pe.matmul(bank_p, g.w("W" + name), src[:, bass.ts(c, CH)], start=True, stop=True).then_inc(proj, 1)

                def turn_v(c, r, q):
                    if q == 0:
                        pe.wait_ge(qkv, c * NPR + NPR)
                    else:
                        pe.wait_ge(vcopy, c * 2 + 2)
                    for b in range(4):
                        ins = pe.transpose(bank_p[:, b * P:(b + 1) * P], vT[:, r, q * 4 + b].rearrange("p o k -> p (o k)"), g.ident)
                    ins.then_inc(vt, 1)

                def scores(c, r, p, group):
                    n = c * PPC + p
                    bank = bank_s[p % 2][:, group, :]
                    if p == 0:
                        pe.wait_ge(qkv, c * NPR + (3 + group))
                    if p % 2 == 0:
                        pe.wait_ge(spread[group], 2 * c + (p // 2 + 3))
                        alone(pe)
                    if group == 0:
                        pe.wait_ge(biased, n + 1)
                    m = maskneg[:, bass.ds(n, 1), :].broadcast_to([2, HG, S])
                    pe.matmul(bank, g.pairsel[:], m, start=True, stop=False, skip_group_check=True)
                    ins = pe.matmul(bank, qg[:, r, group, p * P:(p + 1) * P], kd[:, r, group, p, :, :],
                                    start=False, stop=True, skip_group_check=True)
                    if group == NG - 1:
                        ins.then_inc(scored, 1)

                def turn_probs(c, p):
                    n = c * PPC + p
                    pe.wait_ge(exped, n + 1)
                    pe.wait_ge(tcopy, n + 1)
                    for j in range(NH // 2):
                        ins = pe.transpose(bank_t[:, j // 4, j % 4 * P:(j % 4 + 1) * P], pr[:, p % 2, j * P:(j + 1) * P], g.ident)
                    ins.then_inc(turned, 1)

                def values(c, r, p):
                    n = c * PPC + p
                    pe.wait_ge(tcopy, n + 2)
                    pe.wait_ge(added, n + 1)
                    if p == 0:
                        pe.wait_ge(vcopy, c * 2 + 3)
                    for b in range(2):
                        for j in range(NH // 2):
                            ins = pe.matmul(bank_o[b * S:(b + 1) * S, j * VW:(j + 1) * VW],
                                            pT[:, p % 2, j, b * S:(b + 1) * S], vd[:, r, 2 * p + b, j, :], start=True, stop=True)
                    ins.then_inc(pv, 1)

                def turn_out(n, q):
                    pe.wait_ge(normed, n + 1)
                    pe.transpose(bank_o[:, T_AT:T_AT + P], o[:, q, :], g.ident).then_inc(oturned, 1)

                def output(n, q):
                    pe.wait_ge(ocopy, n + 1)
                    pe.matmul(bank_o[:, F_AT:F_AT + D], oT[:, q, :], g.w("Wo"), start=True, stop=False)
                    pe.matmul(bank_o[:, F_AT:F_AT + D], g.w("ones")[0:1, :], g.w("bo")[0:1, :], start=False, stop=True).then_inc(outp, 1)

                def slot(c, r, p, first, last):
                    before, q = c * PPC + (p - 1), (p - 1) % 2
                    more = not last or p + LEAD < PPC
                    ahead = (c, r, p + LEAD) if p + LEAD < PPC else (c + 1, 1 - r, p + LEAD - PPC)
                    turn_probs(c, p)
                    if more:
                        scores(*ahead, 0)
                    if not first:
                        turn_out(before, q)
                    if not last:
                        if p < 3:
                            project(c + 1, 2 * p)
                        else:
                            turn_v(c + 1, 1 - r, 0)
                    if not first:
                        output(before, q)
                    if more:
                        scores(*ahead, 1)
                    values(c, r, p)
                    if not last:
                        if p < 2:
                            project(c + 1, 2 * p + 1)
                        elif p == 3:
                            turn_v(c + 1, 1 - r, 1)

                for k in range(NPR):
                    project(0, k)
                for q in range(2):
                    turn_v(0, 0, q)
                for p in range(LEAD):
                    scores(0, 0, p, 0)
                    scores(0, 0, p, 1)
                run(pe, slot)
                turn_out(NC * PPC - 1, 1)
                output(NC * PPC - 1, 1)

            @block.scalar
            def _(act):
                act.sem_inc(vcopy, 1)
                act.sem_inc(tcopy, 1)
                act.preload_act_table(ACT.Exp)

                def take_k(c, r, group):
                    act.wait_ge(proj, c * NPR + (group + 1))
                    act.wait_ge(spread[group], 2 * c + 2)
                    act.activation(ks[:, group, :], bank_p, ACT.Identity, bias=g.w(f"bK{group}")).then_inc(qkv, 1)

                def take_q(c, r, group):
                    act.wait_ge(proj, c * NPR + (3 + group))
                    for b in range(2):
                        rows = slice(b * S, (b + 1) * S)
                        pick = lambda t: t.rearrange("p (n b s) -> p n b s", b=2, s=S)[:, :, b, :]
                        ins = act.activation(pick(qg[rows, r, group, :]), pick(bank_p[rows, :]), ACT.Identity,
                                             bias=qbias[rows, group:group + 1], scale=DK ** -0.5)
                    ins.then_inc(qkv, 1)

                def take_v(c, r):
                    act.wait_ge(proj, c * NPR + NPR)
                    act.activation(vT[:, r], bank_p.rearrange("p (b o k) -> p b o k", o=1, k=S).broadcast_to([P, BPC, 2, S]),
                                   ACT.Identity, bias=g.w("bv")).then_inc(qkv, 1)

                def spread_v(c, r, q):
                    act.wait_ge(vt, c * 2 + (q + 1))
                    for h2 in range(2):
                        half = slice(h2 * S, (h2 + 1) * S)
                        src = bank_p[half, :].rearrange("p (b j t d) -> p b j t d", b=4, t=2, d=DK)[:, :, :, h2, :]
                        for b in range(4):
                            ins = act.activation(vd[half, r, q * 4 + b, :, h2 * (DK + 1):h2 * (DK + 1) + DK], src[:, b], ACT.Copy)
                    ins.then_inc(vcopy, 1)

                def probs(n, q):
                    act.wait_ge(shifted, n + 1)
                    act.activation(pr[:, q, :], sc[:, q, :, :].rearrange("p h k -> p (h k)"), ACT.Exp).then_inc(exped, 1)

                def probs_copy(n, q):
                    act.wait_ge(turned, n + 1)
                    act.activation(pT[:, q, :, :].rearrange("p j q -> p (j q)"), bank_t.rearrange("p a b -> p (a b)"), ACT.Copy).then_inc(tcopy, 1)

                def output_copy(n, q):
                    act.wait_ge(oturned, n + 1)
                    act.activation(oT[:, q, :], bank_o[:, T_AT:T_AT + P], ACT.Copy).then_inc(ocopy, 1)

                def slot(c, r, p, first, last):
                    probs_copy(c * PPC + p, p % 2)
                    if not first:
                        output_copy(c * PPC + (p - 1), (p - 1) % 2)
                    if not last or p + 1 < PPC:
                        probs(c * PPC + (p + 1), (p + 1) % 2)
                    if not last:
                        if p < 2:
                            for group in range(NG):
                                (take_k, take_q)[p](c + 1, 1 - r, group)
                        elif p == 2:
                            take_v(c + 1, 1 - r)
                        else:
                            for q in range(2):
                                spread_v(c + 1, 1 - r, q)

                for take in (take_k, take_q):
                    for group in range(NG):
                        take(0, 0, group)
                take_v(0, 0)
                for q in range(2):
                    spread_v(0, 0, q)
                probs(0, 0)
                run(act, slot)
                output_copy(NC * PPC - 1, 1)

            @block.vector
            def _(ve):
                ve.sem_inc(biased, 2)
                ve.sem_inc(added, 1)

                def take_scores(n, q):
                    ve.wait_ge(scored, n + 1)
                    ve.tensor_tensor(sc[:, q].rearrange("p h k -> p (h k)"), bank_s[q].rearrange("p a b -> p (a b)"),
                                     bias[:].rearrange("p h k -> p (h k)"), ALU.add).then_inc(biased, 1)

                def shift(n, q):
                    ve.wait_ge(biased, n + 3)
                    ve.tensor_reduce(mx[:, q, :], sc[:, q], AX_X, ALU.max).then_inc(maxed, 1)
                    ve.wait_ge(maxed, n + 1)
                    ve.tensor_tensor(sc[:, q], sc[:, q], mx[:, q, :].rearrange("p (h o) -> p h o", o=1).broadcast_to([P, NH, S]),
                                     ALU.subtract).then_inc(shifted, 1)

                def finish(n, q):
                    ve.wait_ge(pv, n + 1)
                    res = bank_o[:, :NH // 2 * VW].rearrange("p (h w) -> p h w", w=DK + 1)
                    ve.reciprocal(ri[:, q, :], res[:, :, DK]).then_inc(rinv, 1)
                    ve.wait_ge(rinv, n + 1)
                    ve.tensor_tensor(o[:, q, :].rearrange("p (h d) -> p h d", d=DK), res[:, :, 0:DK],
                                     ri[:, q, :].rearrange("p (h o) -> p h o", o=1).broadcast_to([P, NH, DK]), ALU.mult).then_inc(normed, 1)

                def add(n):
                    ve.wait_ge(outp, n + 1)
                    x = g.X[:, bass.ds(n, 1), :].rearrange("p a d -> p (a d)")
                    ve.tensor_tensor(x, x, bank_o[:, F_AT:F_AT + D], ALU.add).then_inc(added, 1)

                def slot(c, r, p, first, last):
                    if not first:
                        add(c * PPC + (p - 1))
                    more = not last or p + LEAD < PPC
                    if more:
                        take_scores(c * PPC + (p + LEAD), p % 2)
                    finish(c * PPC + p, p % 2)
                    if more:
                        shift(c * PPC + (p + LEAD), p % 2)

                for n in range(LEAD):
                    take_scores(n, n)
                    shift(n, n)
                run(ve, slot)
                ve.wait_ge(outp, NC * PPC)
                x = g.X[:, NT - 1, :]
                ve.tensor_tensor(x, x, bank_o[:, F_AT:F_AT + D], ALU.add).then_inc(added, 1)


GATES = 4
SPC = CH // B
SB = SPC // 2


def waves(nc, g, tag, hs, x1):
    LAYERS = 2
    with ExitStack() as ctx:
        sem = sem_maker(nc, ctx, tag)
        sb = lambda name, shape, dt=F32: ctx.enter_context(nc.sbuf_tensor(f"{tag}_{name}", shape, dt))
        fm = sb("fm", [P, LAYERS, B])
        m = sb("m", [P, 2, LAYERS, B])
        pre = sb("pre", [P, 2, LAYERS, B])
        ga = sb("ga", [P, 2, LAYERS, B])
        tz, eo = sb("tz", [P, LAYERS, B]), sb("eo", [P, LAYERS, B])
        norm, snorm = sb("norm", [P, LAYERS, B]), sb("snorm", [P, LAYERS, B])
        cell, scc, gt = (sb(n, [P, LAYERS, B]) for n in ("cell", "scc", "gt"))
        den, inv = sb("den", [P, LAYERS, B]), sb("inv", [P, LAYERS, B])
        bparts = sb("bparts", [P, LAYERS, GATES * P], BF16)
        bres = sb("bres", [P, LAYERS, GATES * P])
        ones = sb("ones", [P, SB * B], BF16)
        gl, z = sb("gl", [P, CH]), sb("z", [P, CH])
        zn = sb("zn", [P, TPC, D])
        st = sb("st", [P, TPC, 6])
        a, b, mean, var, rstd = (sb(n, [P, TPC]) for n in ("a", "b", "mean", "var", "rstd"))
        hready = sem("hready0"), sem("hready1")
        inverted = sem("inverted")
        gates_if, gates_zo, dve, gexp, zexp, init, predone = (
            sem(n) for n in ("gates_if", "gates_zo", "dve", "gexp", "zexp", "init", "predone"))
        cstep, cready, bvec = sem("cstep"), sem("cready"), sem("bvec")
        proj, gelu, zready, turned, stat, mixv, var_ready, rstd_ready, nready, back, done = (
            sem(n) for n in ("proj", "gelu", "zready", "turned", "stat", "mixv", "var_ready", "rstd_ready", "nready", "back", "done"))
        stat_a, mean_ready = sem("stat_a"), sem("mean_ready")
        PER = 5
        PERM = 4

        def bank_of(blk, pair, layer):
            return g.bank[4 * blk + 2 * pair + layer]

        def gate(j, k, lo, hi):
            first = 4 * (j // SB) + 2 * (k // 2)
            col = (k % 2 * SB + j % SB) * B
            return g.ps[:, first + lo:first + hi, col:col + B]

        bank_p, bank_z, bank_b = bank_of(0, 0, 1), g.bank[5], g.bank[6]
        HALF = CH // 2

        def inversions(c, j, lo, hi):
            return j if lo == hi - 1 and lo == 0 else c * (2 * SPC) + ((hi - lo) * j - SPC)

        def run(eng, wave):
            wave(0, 0, 1, True)
            with eng.Fori(0, NC - 2) as i:
                wave(i + 1, 0, 2, True)
            wave(NC - 1, 0, 2, False)
            wave(NC, 1, 2, False)

        with nc.Block() as block:

            @block.gpsimd
            def _(pool):
                pool.memset(hs[:, 0, 0:B], 0.0).then_inc(init, 1)
                pool.memset(hs[:, 1, CH:CH + B], 0.0).then_inc(init, 1)
                pool.memset(m[:, 1], 0.0).then_inc(init, 1)
                pool.memset(norm[:], 0.0).then_inc(init, 1)
                pool.memset(cell[:], 0.0).then_inc(init, 1)
                pool.memset(ones[:], 1.0).then_inc(init, 1)
                pool.wait_ge(init, 6)

                def wave(c, lo, hi, ahead):
                    L = slice(lo, hi)
                    for j in range(SPC):
                        s = c * SPC + j
                        pool.wait_ge(gexp, 2 * s + 1)
                        pool.tensor_tensor(scc[:, L], cell[:, L], ga[:, 0, L], ALU.mult).then_inc(cstep, 1)
                        pool.wait_ge(gexp, 2 * s + 2)
                        pool.wait_ge(zexp, 2 * s + 1)
                        pool.tensor_tensor(gt[:, L], ga[:, 1, L], tz[:, L], ALU.mult).then_inc(cstep, 1)
                        pool.wait_ge(cstep, 2 * s + 2)
                        pool.tensor_tensor(cell[:, L], scc[:, L], gt[:, L], ALU.add).then_inc(cready, 1)
                    if lo == 0:
                        pool.wait_ge(var_ready, c + 1)
                        pool.tensor_tensor(rstd[:], a[:], g.neghalf[:, 0:TPC], ALU.pow).then_inc(rstd_ready, 1)

                run(pool, wave)

            @block.tensor
            def _(pe):
                def from_input(c, blk, layer, k):
                    x = g.xT if layer == 0 else x1
                    out = bank_of(blk, k // 2, layer)[:, k % 2 * SB * B:(k % 2 + 1) * SB * B]
                    at = c * CH + (blk * SB * B - layer * CH)
                    pe.matmul(out, g.w(f"sW{layer}")[:, k * P:(k + 1) * P], x[:, bass.ds(at, SB * B)],
                              start=(k % 2 == 0), stop=False, skip_group_check=True)
                    pe.matmul(out, bparts[:, layer, k * P:(k + 1) * P], ones[:], start=False, stop=False, skip_group_check=True)

                def h_before(c, j, layer):
                    pe.wait_ge(hready[layer], c * SPC + (j + 1 - layer * SPC))

                def wave(c, lo, hi, ahead):
                    for j in range(SPC):
                        for pair, layer in ((p, l) for p in range(2) for l in range(lo, hi)):
                            if j == 0 and hi == 2 and layer == lo:
                                for k in (2 * pair, 2 * pair + 1):
                                    from_input(c, 0, 1, k)
                            if pair == 0:
                                h_before(c, j, layer)
                            for k in (2 * pair, 2 * pair + 1):
                                ins = pe.matmul(gate(j, k, layer, layer + 1), g.w(f"sR{layer}")[:, k * P:(k + 1) * P],
                                                hs[:, layer, bass.ds(c * CH + j * B, B)],
                                                start=False, stop=(k % 2 == 1), skip_group_check=True)
                                if k % 2 == 1 and layer == hi - 1:
                                    ins.then_inc((gates_if, gates_zo)[k // 2], 1)
                        if j < SB:
                            if j == 0 and hi == 2:
                                pe.wait_ge(done, 2 * c)
                            for layer in range(lo, hi):
                                from_input(c, 1, layer, j)
                        elif ahead:
                            from_input(c + 1, 0, 0, j - SB)
                        if lo == 0 and j in (SB, SPC - 1):
                            for_steps(c, *((0, SB) if j == SB else (SB, SPC - 1)))
                    if lo == 0:
                        pe.wait_ge(hready[0], c * SPC + (SPC + 1))
                        for_steps(c, SPC - 1, SPC).then_inc(proj, 1)
                        for j in range(TPC):
                            if j % 2 == 0:
                                pe.wait_ge(zready, 2 * c + (j // 2 + 1))
                            pe.transpose(bank_z[:, j * P:(j + 1) * P], z[:, j * P:(j + 1) * P], g.ident).then_inc(turned, 1)
                        for j in range(TPC):
                            pe.wait_ge(nready, c * TPC + (j + 1))
                            pe.transpose(bank_b[:, j * P:(j + 1) * P], zn[:, j, :], g.ident).then_inc(back, 1)
                        pe.wait_ge(done, 2 * c + 1)

                def for_steps(c, a, b):
                    return pe.matmul(bank_p[:, a * B:b * B], g.w("sP0"), hs[:, 0, bass.ds(c * CH + (a + 1) * B, (b - a) * B)], start=True, stop=True)

                pe.wait_ge(init, 6)
                pe.wait_ge(bvec, 6)
                for k in range(GATES):
                    from_input(0, 0, 0, k)
                run(pe, wave)

            @block.scalar
            def _(act):
                def wave(c, lo, hi, ahead):
                    act.preload_act_table(ACT.Exp)
                    for j in range(SPC):
                        s = c * SPC + j
                        for k in range(2):
                            act.wait_ge(predone, 2 * s + k + 1)
                            act.activation(ga[:, k, lo:hi], pre[:, k, lo:hi], ACT.Exp).then_inc(gexp, 1)
                        act.wait_ge(gates_zo, s + 1)
                        act.activation(tz[:, lo:hi], gate(j, 2, lo, hi), ACT.Tanh).then_inc(zexp, 1)
                        act.activation(eo[:, lo:hi], gate(j, 3, lo, hi), ACT.Exp, scale=-1.0).then_inc(zexp, 1)
                    if lo == 0:
                        act.preload_act_table(ACT.Gelu)
                        act.wait_ge(proj, c + 1)
                        for k in range(2):
                            cols = slice(k * HALF, (k + 1) * HALF)
                            act.activation(gl[:, cols], bank_p[:, cols], ACT.Gelu, bias=g.w("spb0")).then_inc(gelu, 1)
                        act.wait_ge(back, c * TPC + TPC)
                        for k in range(2):
                            act.activation(x1[:, bass.ds(c * CH + k * HALF, HALF)], bank_b[:, k * HALF:(k + 1) * HALF], ACT.Identity,
                                           bias=g.w("sbe0"), scale=g.w("sga0")).then_inc(done, 1)

                run(act, wave)

            @block.vector
            def _(ve):
                whole = g.wts[:, g.lay["sbrow0"][0]:g.lay["sbrow0"][0] + LAYERS * GATES * P].rearrange("p (l k) -> p l k", l=LAYERS)
                for k, f in enumerate((
                        lambda: ve.tensor_copy(bparts[:], whole),
                        lambda: ve.tensor_tensor(bres[:], whole, bparts[:], ALU.subtract),
                        lambda: ve.tensor_copy(bparts[32:64], bres[32:64]),
                        lambda: ve.tensor_copy(bparts[64:128], bres[64:128]),
                        lambda: ve.tensor_tensor(bres[64:128], bres[64:128], bparts[64:128], ALU.subtract),
                        lambda: ve.tensor_copy(bparts[64:128], bres[64:128]))):
                    f().then_inc(bvec, 1)
                    ve.wait_ge(bvec, k + 1)
                for h in hready:
                    ve.sem_inc(h, 1)
                ve.wait_ge(init, 6)

                def step(c, j, lo, hi):
                    s = c * SPC + j
                    q = j % 2
                    L = slice(lo, hi)
                    n = [0]

                    def inc(ins):
                        ins.then_inc(dve, 1)
                        n[0] += 1

                    def link(ins):
                        inc(ins)
                        ve.wait_ge(dve, c * SPC * PER + (j * PER + n[0]))

                    new, old = m[:, q, L], m[:, 1 - q, L]
                    ve.wait_ge(gates_if, s + 1)
                    link(ve.tensor_tensor(fm[:, L], gate(j, 1, lo, hi), old, ALU.add))
                    link(ve.tensor_tensor(new, gate(j, 0, lo, hi), fm[:, L], ALU.max))
                    ve.tensor_tensor(pre[:, 0, L], fm[:, L], new, ALU.subtract).then_inc(predone, 1)
                    ve.tensor_tensor(pre[:, 1, L], gate(j, 0, lo, hi), new, ALU.subtract).then_inc(predone, 1)
                    ve.wait_ge(gexp, 2 * s + 1)
                    link(ve.tensor_tensor(snorm[:, L], norm[:, L], ga[:, 0, L], ALU.mult))
                    ve.wait_ge(gexp, 2 * s + 2)
                    link(ve.tensor_tensor(norm[:, L], snorm[:, L], ga[:, 1, L], ALU.add))
                    ve.wait_ge(zexp, 2 * s + 2)
                    link(ve.scalar_tensor_tensor(den[:, L], eo[:, L], 1.0, norm[:, L], ALU.add, ALU.mult))
                    assert n[0] == PER
                    for k, layer in enumerate(range(lo, hi)):
                        ve.reciprocal(inv[:, layer], den[:, layer]).then_inc(inverted, 1)
                        ve.wait_ge(inverted, inversions(c, j, lo, hi) + (k + 1))
                        if k == 0:
                            ve.wait_ge(cready, s + 1)
                        ve.tensor_tensor(hs[:, layer, bass.ds(c * CH + (j + 1) * B, B)], cell[:, layer], inv[:, layer], ALU.mult).then_inc(hready[layer], 1)

                def mix(c):
                    n = [0]

                    def inc(ins):
                        ins.then_inc(mixv, 1)
                        n[0] += 1

                    def link(ins):
                        inc(ins)
                        ve.wait_ge(mixv, c * PERM + n[0])

                    for k in range(2):
                        cols = slice(k * HALF, (k + 1) * HALF)
                        ve.wait_ge(gelu, 2 * c + k + 1)
                        ve.tensor_tensor(z[:, cols], gl[:, cols], g.xT[:, bass.ds(c * CH + k * HALF, HALF)], ALU.add).then_inc(zready, 1)
                    ve.wait_ge(turned, c * TPC + TPC)
                    for j in range(TPC):
                        ve.bn_stats(st[:, j, :], bank_z[:, j * P:(j + 1) * P]).then_inc(stat, 1)
                    ve.wait_ge(stat, (c + 1) * TPC)
                    inc(ve.tensor_tensor(b[:], st[:, :, 1], st[:, :, 4], ALU.subtract))
                    link(ve.tensor_tensor(var[:], st[:, :, 2], st[:, :, 5], ALU.add))
                    ve.tensor_tensor(a[:], st[:, :, 1], st[:, :, 4], ALU.add).then_inc(stat_a, 1)
                    link(ve.scalar_tensor_tensor(b[:], b[:], 0.25, b[:], ALU.mult, ALU.mult))
                    link(ve.scalar_tensor_tensor(var[:], var[:], 1.0 / D, b[:], ALU.mult, ALU.add))
                    ve.wait_ge(stat_a, c + 1)
                    ve.tensor_scalar(mean[:], a[:], 0.5, None, ALU.mult).then_inc(mean_ready, 1)
                    ve.wait_ge(mean_ready, c + 1)
                    ve.tensor_scalar(a[:], var[:], EPS, None, ALU.add).then_inc(var_ready, 1)
                    ve.wait_ge(rstd_ready, c + 1)
                    for j in range(TPC):
                        ve.tensor_scalar(zn[:, j, :], bank_z[:, j * P:(j + 1) * P], mean[:, j:j + 1],
                                         rstd[:, j:j + 1], ALU.subtract, ALU.mult).then_inc(nready, 1)

                def wave(c, lo, hi, ahead):
                    for j in range(SPC):
                        step(c, j, lo, hi)
                    if lo == 0:
                        mix(c)

                run(ve, wave)


def final_norm(nc, g, tag, xin, hs):
    with ExitStack() as ctx:
        sem = sem_maker(nc, ctx, tag)
        sb = lambda name, shape, dt=F32: ctx.enter_context(nc.sbuf_tensor(f"{tag}_{name}", shape, dt))
        R = 4
        gl = sb("gl", [P, 2, CH])
        z = sb("z", [P, R, CH])
        zn = sb("zn", [P, R, TPC, D])
        zs = sb("zs", [P, R, TPC, D])
        st = sb("st", [P, R, TPC, 6])
        a, b, mean, var, rstd = (sb(n, [P, R, TPC]) for n in ("a", "b", "mean", "var", "rstd"))
        proj, gelu, zready, turned, stat, vch, var_ready, rstd_ready, nready, gained, shifted, added = (
            sem(n) for n in ("proj", "gelu", "zready", "turned", "stat", "vch", "var_ready", "rstd_ready", "nready", "gained", "shifted", "added"))

        def view(t, c):
            return t.rearrange("p (s b) -> p b s", b=B)[:, bass.ts(c, BPC), :]
        three = lambda t: t.rearrange("p (a k) -> p a k", k=S)
        bank_p, bank_z = g.bank[0:2], g.bank[2:6]
        with nc.Block() as block:

            @block.tensor
            def _(pe):
                def turn(c, r):
                    pe.wait_ge(zready, c + 3)
                    pe.wait_ge(nready, c + 1)
                    for j in range(TPC):
                        ins = pe.transpose(bank_z[r][:, j * P:(j + 1) * P], z[:, r, j * P:(j + 1) * P], g.ident)
                    ins.then_inc(turned, 1)

                with pe.Fori(0, NC // R) as group:
                    for r in range(R):
                        c = group * R + r
                        pe.wait_ge(gelu, c + 1)
                        pe.matmul(three(bank_p[r % 2]), g.w("sP1"), view(hs, c), start=True, stop=True).then_inc(proj, 1)
                        if r >= 1:
                            turn(group * R + (r - 1), r - 1)
                    turn(group * R + (R - 1), R - 1)

            @block.scalar
            def _(act):
                act.preload_act_table(ACT.Gelu)
                act.sem_inc(gelu, 2)
                with act.Fori(0, NC // R) as group:
                    for r in range(R):
                        c = group * R + r
                        act.wait_ge(proj, c + 1)
                        act.wait_ge(zready, c + 1)
                        act.activation(gl[:, r % 2, :], bank_p[r % 2], ACT.Gelu, bias=g.w("spb1")).then_inc(gelu, 1)

            @block.gpsimd
            def _(pool):
                row = lambda n: g.w(n).rearrange("p (o d) -> p o d", o=1).broadcast_to([P, TPC, D])

                def root(c, r):
                    pool.wait_ge(var_ready, c + 1)
                    pool.tensor_tensor(rstd[:, r, :], a[:, r, :], g.neghalf[:, 0:TPC], ALU.pow).then_inc(rstd_ready, 1)

                def gain(c, r):
                    pool.wait_ge(nready, c + (R + 1))
                    pool.tensor_tensor(zs[:, r], zn[:, r], row("garow"), ALU.mult).then_inc(gained, 1)
                    pool.wait_ge(gained, c + 1)
                    pool.tensor_tensor(zs[:, r], zs[:, r], row("berow"), ALU.add).then_inc(shifted, 1)

                with pool.Fori(0, NC // R) as group:
                    for r in range(R):
                        root(group * R + r, r)
                        if r >= 1:
                            gain(group * R + (r - 1), r - 1)
                    gain(group * R + (R - 1), R - 1)

            @block.vector
            def _(ve):
                PER = 6
                ve.sem_inc(zready, 2)
                ve.sem_inc(nready, R)

                def sum_up(c, r):
                    ve.wait_ge(gelu, c + 3)
                    ve.tensor_tensor(three(z[:, r, :]), three(gl[:, r % 2, :]), view(xin, c), ALU.add).then_inc(zready, 1)

                def moments(c, r):
                    n = [0]

                    def inc(ins):
                        ins.then_inc(vch, 1)
                        n[0] += 1

                    def link(ins):
                        inc(ins)
                        ve.wait_ge(vch, c * PER + n[0])

                    ve.wait_ge(turned, c + 1)
                    for j in range(TPC):
                        ve.bn_stats(st[:, r, j, :], bank_z[r][:, j * P:(j + 1) * P]).then_inc(stat, 1)
                    ve.wait_ge(stat, c * TPC + TPC)
                    ve_a, ve_b, ve_m, ve_v = a[:, r, :], b[:, r, :], mean[:, r, :], var[:, r, :]
                    inc(ve.tensor_tensor(ve_a, st[:, r, :, 1], st[:, r, :, 4], ALU.add))
                    inc(ve.tensor_tensor(ve_b, st[:, r, :, 1], st[:, r, :, 4], ALU.subtract))
                    link(ve.tensor_tensor(ve_v, st[:, r, :, 2], st[:, r, :, 5], ALU.add))
                    link(ve.scalar_tensor_tensor(ve_b, ve_b, 0.25, ve_b, ALU.mult, ALU.mult))
                    inc(ve.tensor_scalar(ve_m, ve_a, 0.5, None, ALU.mult))
                    link(ve.scalar_tensor_tensor(ve_v, ve_v, 1.0 / D, ve_b, ALU.mult, ALU.add))
                    assert n[0] == PER
                    ve.tensor_scalar(ve_a, ve_v, EPS, None, ALU.add).then_inc(var_ready, 1)

                def normalise(c, r):
                    ve.wait_ge(rstd_ready, c + 1)
                    for j in range(TPC):
                        ins = ve.tensor_scalar(zn[:, r, j, :], bank_z[r][:, j * P:(j + 1) * P], mean[:, r, j:j + 1],
                                               rstd[:, r, j:j + 1], ALU.subtract, ALU.mult)
                    ins.then_inc(nready, 1)

                def add(c, r):
                    ve.wait_ge(shifted, c + 1)
                    xc = g.X[:, bass.ts(c, TPC), :]
                    ve.tensor_tensor(xc, xc, zs[:, r], ALU.add).then_inc(added, 1)

                with ve.Fori(0, NC // R) as group:
                    for r in range(R + 3):
                        for lag, step in enumerate((sum_up, moments, normalise, add)):
                            if 0 <= r - lag < R:
                                step(group * R + (r - lag), r - lag)


def by_step(g):
    return lambda c: g.xT[:, :].rearrange("p (s b) -> p b s", b=B)[:, bass.ts(c, BPC), :]


def lstm_stage(nc, g):
    with ExitStack() as ctx:
        hs = ctx.enter_context(nc.sbuf_tensor("lstm_h", [P, 2, T + CH + B], F32))
        x1 = ctx.enter_context(nc.sbuf_tensor("lstm_x1", [P, T], F32))
        waves(nc, g, "rw", hs, x1)
        final_norm(nc, g, "m1", x1[:, :], hs[:, 1, CH + B:])


NX = 8
CAP = T * 5 // (4 * NX)
TILES = T // P + NX
PAD_TILES = TILES + 3
RING = 8
WAYS = 4
BITS = 30


class Router:

    def __init__(self, nc, g, ctx, tag):
        self.nc, self.g, self.tag = nc, g, tag
        self.sem = sem_maker(nc, ctx, tag)
        self.sb = lambda name, shape, dt=F32: ctx.enter_context(nc.sbuf_tensor(f"{tag}_{name}", shape, dt))
        self.p = self.sb("p", [P, NT, NX])
        self.oh = self.sb("oh", [P, NT, NX])
        self.t = self.sb("t", [P, NT, NX])
        self.pos = self.sb("pos", [P, NT, NX])
        self.incl = self.sb("incl", [P, NX, NT])
        self.m = self.sb("m", [P, NT])
        self.m2 = self.sb("m2", [P, NT])
        self.slot = self.sb("slot", [P, NT])
        self.slot_u = self.sb("slot_u", [P, NT], U32)
        self.weight = self.sb("weight", [P, NT])

    def over_experts(self, a):
        return a.rearrange("p (n o) -> p n o", o=1).broadcast_to([P, NT, NX])

    def over_tiles(self, a):
        return a.rearrange("p (o e) -> p o e", o=1).broadcast_to([P, NT, NX])

    def pick(self, ve, ch, score, best):
        over, r = self.over_experts, self
        ch.link(ve.tensor_tensor(r.t[:], score, over(best), ALU.is_ge))
        ch.link(ve.scalar_tensor_tensor(r.t[:], r.t[:], -float(NX), r.over_tiles(r.g.w("eidx")), ALU.mult, ALU.add))
        ch.link(ve.tensor_reduce(r.m2[:], r.t[:], AX_X, ALU.min))
        ch.link(ve.tensor_tensor(r.oh[:], r.t[:], over(r.m2[:]), ALU.is_equal))

    def ranks(self, ve, ch, counted, times):
        r, g = self, self.g
        ve.wait_ge(counted, times)
        cnt = g.bank[1][:, 0:NT * NX].rearrange("p (n e) -> p e n", e=NX)
        for e in range(NX):
            ch.inc(ve.tensor_tensor_scan(r.incl[:, e, :], g.w("onerow"), cnt[:, e, :], 0.0, ALU.mult, ALU.add))
        ve.wait_ge(ch.sem, ch.value())
        incl = r.incl[:].rearrange("p e n -> p n e")
        flat = lambda k: g.bank[k][:, 0:NT * NX].rearrange("p (n e) -> p n e", e=NX)
        ch.link(ve.tensor_tensor(r.pos[:], incl, flat(1), ALU.subtract))
        ch.link(ve.tensor_tensor(r.pos[:], r.pos[:], flat(0), ALU.add))


def count_flags(pe, g, flags):
    f = flags[:].rearrange("p n e -> p (n e)")
    pe.matmul(g.bank[0][:, 0:NT * NX], g.w("before"), f, start=True, stop=True)
    return pe.matmul(g.bank[1][:, 0:NT * NX], g.w("allones"), f, start=True, stop=True)


def softmax_block(nc, g, r, gate, bias):
    logits, chain, sub, exped = (r.sem(n) for n in ("logits", "chain", "sub", "exped"))
    with nc.Block() as block:

        @block.tensor
        def _(pe):
            for n in range(NT):
                ins = pe.matmul(g.bank[2][:, n * NX:(n + 1) * NX], g.xT[:, n * P:(n + 1) * P], gate, start=True, stop=True)
            ins.then_inc(logits, 1)

        @block.scalar
        def _(act):
            act.wait_ge(sub, 1)
            act.activation(r.p[:], r.p[:], ACT.Exp).then_inc(exped, 1)

        @block.vector
        def _(ve):
            ch = Chain(ve, chain)
            lg = g.bank[2][:, 0:NT * NX].rearrange("p (n e) -> p n e", e=NX)
            ve.wait_ge(logits, 1)
            if bias is not None:
                ch.link(ve.tensor_tensor(r.p[:], lg, r.over_tiles(bias), ALU.add))
            else:
                ch.link(ve.tensor_copy(r.p[:], lg))
            ch.link(ve.tensor_reduce(r.m[:], r.p[:], AX_X, ALU.max))
            ve.tensor_tensor(r.p[:], r.p[:], r.over_experts(r.m[:]), ALU.subtract).then_inc(sub, 1)
            ve.wait_ge(exped, 1)
            ch.link(ve.tensor_reduce(r.m[:], r.p[:], AX_X, ALU.add))
            ch.link(ve.reciprocal(r.m[:], r.m[:]))
            ch.link(ve.tensor_tensor(r.p[:], r.p[:], r.over_experts(r.m[:]), ALU.mult))
            ch.link(ve.tensor_reduce(r.m[:], r.p[:], AX_X, ALU.max))


def clear_places(sp, g):
    view = g.buf[0:PAD_TILES * P, :].rearrange("(a p) d -> p a d", p=P)
    for a in range(0, PAD_TILES, TPC):
        w = min(TPC, PAD_TILES - a)
        sp.dma_start(view[:, a:a + w, :], g.zero[:, 0:w * D].rearrange("p (a d) -> p a d", d=D)).then_inc(g.cleared, 16)
        g.clears += 16
    sp.wait_ge(g.cleared, g.clears)


def dispatch(nc, g, tag, r, slots, win, loads):
    with ExitStack() as ctx:
        sem = sem_maker(nc, ctx, tag)
        scattered = g.lasting(f"{tag}_scattered")
        with nc.Block() as block:

            @block.sync
            def _(sp):
                sp.wait_ge(win, 16 * loads)

            @block.gpsimd
            def _(pool):
                for n in range(NT):
                    pool.indirect_dma_start(g.buf, bass.IndirectOffsetOnAxis(ap=slots[:, n:n + 1], axis=0), g.rows[:, n, :], None).then_inc(scattered, 16)
                pool.wait_ge(scattered, 16 * NT)


def experts(nc, g, tag, F, w1, w2, owner, func, b1=None, b2=None):
    FB = F // P
    with ExitStack() as ctx:
        sem = sem_maker(nc, ctx, tag)
        sb = lambda name, shape, dt=F32: ctx.enter_context(nc.sbuf_tensor(f"{tag}_{name}", shape, dt))
        xr = sb("xr", [P, RING, D])
        xT = sb("xT", [P, 2, P])
        h = sb("h", [P, 2, F])
        hT = sb("hT", [P, 2, FB, P])
        y = sb("y", [P, RING, D])
        row_in = [sem(f"row_in{k}") for k in range(RING)]
        out_done = [sem(f"out_done{k}") for k in range(RING)]
        turned, xcopy, mm1, hready, hturned, hcopy, mm2, yready = (
            sem(n) for n in ("turned", "xcopy", "mm1", "hready", "hturned", "hcopy", "mm2", "yready"))
        bank_x, bank_h, bank_t, bank_y = g.bank[0:2], g.bank[2:4], g.bank[4:6], g.bank[6:8]
        with nc.Block() as block:

            @block.sync
            def _(sp):
                def load(k, r):
                    sp.dma_start(xr[:, r, :], g.buf[bass.ts(k, P), :]).then_inc(row_in[r], 16)

                for k in range(RING):
                    load(k, k)
                for r in range(RING):
                    sp.sem_inc(out_done[r], 16)

                def store(k, r):
                    sp.wait_ge(yready, k + 3)
                    sp.dma_start(g.out[bass.ts(k, P), :], y[:, r, :]).then_inc(out_done[r], 16)

                with sp.Fori(0, TILES // RING - 1) as i:
                    for r in range(RING):
                        sp.wait_ge(turned, i * RING + (r + 1))
                        load(i * RING + (RING + r), r)
                        store(i * RING + r, r)
                for r in range(RING):
                    if TILES + r < PAD_TILES:
                        sp.wait_ge(turned, TILES - RING + r + 1)
                        load(TILES + r, r)
                    store(TILES - RING + r, r)
                for r in range(RING):
                    sp.wait_ge(out_done[r], 16 * (TILES // RING) + 16)

            @block.tensor
            def _(pe):
                def turn(k, r, uses):
                    pe.wait_ge(row_in[r], uses * 16)
                    pe.wait_ge(xcopy, k + 1)
                    pe.transpose(bank_x[r % 2][:, 0:P], xr[:, r, :], g.ident).then_inc(turned, 1)

                expert = lambda k: pe.value_load(owner[0:1, bass.ds(k, 1)], min_val=0, max_val=NX - 1)

                def first(k, r, e):
                    pe.wait_ge(xcopy, k + 3)
                    pe.wait_ge(hready, k + 1)
                    pe.matmul(bank_h[r % 2][:, 0:F], xT[:, r % 2, :], w1[:, bass.ts(e, F)], start=True, stop=True).then_inc(mm1, 1)

                def turn_hidden(k, r):
                    pe.wait_ge(hready, k + 3)
                    pe.wait_ge(hcopy, k + 1)
                    for f in range(FB):
                        ins = pe.transpose(bank_t[r % 2][:, f * P:(f + 1) * P], h[:, r % 2, f * P:(f + 1) * P], g.ident)
                    ins.then_inc(hturned, 1)

                def second(k, r, e):
                    pe.wait_ge(hcopy, k + 3)
                    pe.wait_ge(yready, k + 1)
                    for f in range(FB):
                        ins = pe.matmul(bank_y[r % 2][:, 0:D], hT[:, r % 2, f, :], w2[:, bass.ds(e * (FB * D) + f * D, D)],
                                        start=(f == 0), stop=(f == FB - 1))
                    ins.then_inc(mm2, 1)

                turn(0, 0, 1)
                turn(1, 1, 1)
                first(0, 0, expert(0))
                turn(2, 2, 1)
                first(1, 1, expert(1))
                turn_hidden(0, 0)
                with pe.Fori(0, TILES // RING) as i:
                    owners = {}
                    for r in range(RING):
                        k = i * RING + r
                        owners[r + 2] = expert(k + 2)
                        first(k + 2, (r + 2) % RING, owners[r + 2])
                        second(k, r, owners[r] if r in owners else expert(k))
                        turn(k + 3, (r + 3) % RING, i + (1 if r + 3 < RING else 2))
                        turn_hidden(k + 1, (r + 1) % RING)

            @block.scalar
            def _(act):
                act.sem_inc(xcopy, 2)
                act.sem_inc(hcopy, 2)

                act.preload_act_table(func)

                def take_x(k, r):
                    act.wait_ge(turned, k + 1)
                    act.activation(xT[:, r % 2, :], bank_x[r % 2][:, 0:P], ACT.Copy).then_inc(xcopy, 1)

                def hidden(k, r):
                    act.wait_ge(mm1, k + 1)
                    act.activation(h[:, r % 2, :], bank_h[r % 2][:, 0:F], func).then_inc(hready, 1)

                def hidden_turned(k, r):
                    act.wait_ge(hturned, k + 1)
                    act.activation(hT[:, r % 2].rearrange("p f t -> p (f t)"), bank_t[r % 2][:, 0:F], func).then_inc(hcopy, 1)

                if b1 is None:
                    act.sem_inc(hready, 2)
                take_x(0, 0)
                take_x(1, 1)
                if b1 is None:
                    hidden(0, 0)
                take_x(2, 2)
                if b1 is None:
                    hidden(1, 1)
                else:
                    hidden_turned(0, 0)
                with act.Fori(0, TILES // RING) as i:
                    for r in range(RING):
                        k = i * RING + r
                        if b1 is None:
                            hidden(k + 2, (r + 2) % RING)
                        take_x(k + 3, (r + 3) % RING)
                        if b1 is not None:
                            hidden_turned(k + 1, (r + 1) % RING)

            @block.vector
            def _(ve):
                ve.sem_inc(yready, 2)
                if b1 is not None:
                    ve.sem_inc(hready, 2)

                def first(k, r):
                    e = ve.value_load(owner[0:1, bass.ds(k, 1)], min_val=0, max_val=NX - 1)
                    ve.wait_ge(mm1, k + 1)
                    ve.tensor_tensor(h[:, r % 2, :], bank_h[r % 2][:, 0:F], b1[:, bass.ts(e, F)], ALU.add).then_inc(hready, 1)

                def hidden_turned(k, r):
                    ve.wait_ge(hturned, k + 1)
                    ve.tensor_copy(hT[:, r % 2].rearrange("p f t -> p (f t)"), bank_t[r % 2][:, 0:F]).then_inc(hcopy, 1)

                def second(k, r, uses):
                    if b2 is not None:
                        e = ve.value_load(owner[0:1, bass.ds(k, 1)], min_val=0, max_val=NX - 1)
                    ve.wait_ge(out_done[r], uses * 16 + 16)
                    ve.wait_ge(mm2, k + 1)
                    if b2 is not None:
                        ve.tensor_tensor(y[:, r, :], bank_y[r % 2][:, 0:D], b2[:, bass.ts(e, D)], ALU.add).then_inc(yready, 1)
                    else:
                        ve.tensor_copy(y[:, r, :], bank_y[r % 2][:, 0:D]).then_inc(yready, 1)

                if b1 is not None:
                    first(0, 0)
                    first(1, 1)
                else:
                    hidden_turned(0, 0)
                with ve.Fori(0, TILES // RING) as i:
                    for r in range(RING):
                        k = i * RING + r
                        if b1 is not None:
                            first(k + 2, (r + 2) % RING)
                        second(k, r, i)
                        if b1 is None:
                            hidden_turned(k + 1, (r + 1) % RING)


class Combine:

    def __init__(self, nc, g, ctx, tag, places, weight):
        self.G = 8
        self.g, self.places, self.weight = g, places, weight
        self.row = ctx.enter_context(nc.sbuf_tensor(f"{tag}_row", [P, self.G, D], F32))
        self.got = [g.lasting(f"{tag}_got{k}") for k in range(self.G)]
        self.added = sem_maker(nc, ctx, tag)("added")

    def gather(self, pool, tiles):
        for n in tiles:
            if n >= self.G:
                pool.wait_ge(self.added, n - self.G + 1)
            pool.indirect_dma_start(self.row[:, n % self.G, :], None, self.g.out,
                                    bass.IndirectOffsetOnAxis(ap=self.places[:, n:n + 1], axis=0)).then_inc(self.got[n % self.G], 16)

    def add(self, ve, tiles):
        X = self.g.X
        for n in tiles:
            ve.wait_ge(self.got[n % self.G], 16 * (n // self.G + 1))
            ve.scalar_tensor_tensor(X[:, n, :], self.row[:, n % self.G, :], self.weight[:, n:n + 1], X[:, n, :],
                                    ALU.mult, ALU.add).then_inc(self.added, 1)


def switch_stage(nc, g):
    with ExitStack() as ctx:
        g.rows = ctx.enter_context(nc.sbuf_tensor("sw_rows", [P, NT, D], F32))
        r = Router(nc, g, ctx, "sw")
        sb = r.sb
        w1, w2, b1, b2 = sb("w1", [P, NX * 512]), sb("w2", [P, NX * 512]), sb("b1", [P, NX * 512]), sb("b2", [P, NX * D])
        place = sb("place", [P, NT])
        place_u = sb("place_u", [P, NT], U32)
        owner = sb("owner", [1, PAD_TILES], I32)
        win, picked, counted, chain = (r.sem(n) for n in ("win", "picked", "counted", "chain2"))

        def fetch(sp):
            clear_places(sp, g)
            for t, d in ((owner, g.moe0["owner"]), (w1, g.moe0["w1"]), (w2, g.moe0["w2"]), (b1, g.moe0["b1"]), (b2, g.moe0["b2"])):
                sp.dma_start(t[:], d).then_inc(win, 16)

        norm_stage(nc, g, "n2", keep=True, fetch=fetch)
        softmax_block(nc, g, r, g.w("gate0"), g.w("gateb0"))
        with nc.Block() as block:

            @block.tensor
            def _(pe):
                pe.wait_ge(picked, 1)
                count_flags(pe, g, r.oh).then_inc(counted, 1)

            @block.vector
            def _(ve):
                ch = Chain(ve, chain)
                r.pick(ve, ch, r.p[:], r.m[:])
                ve.sem_inc(picked, 1)
                r.ranks(ve, ch, counted, 1)
                ch.link(ve.tensor_tensor(r.t[:], r.oh[:], r.pos[:], ALU.mult))
                ch.link(ve.tensor_reduce(r.slot[:], r.t[:], AX_X, ALU.add))
                ch.link(ve.tensor_tensor(r.t[:], r.oh[:], r.over_tiles(g.w("eidx")), ALU.mult))
                ch.link(ve.tensor_reduce(r.m2[:], r.t[:], AX_X, ALU.add))
                ch.link(ve.tensor_scalar(r.weight[:], r.slot[:], float(CAP), None, ALU.is_lt))
                ch.link(ve.tensor_scalar(place[:], r.slot[:], float(CAP - 1), None, ALU.min))
                ch.link(ve.scalar_tensor_tensor(place[:], r.m2[:], float(CAP), place[:], ALU.mult, ALU.add))
                ch.link(ve.tensor_copy(place_u[:], place[:]))
                ch.link(ve.tensor_tensor(r.slot[:], place[:], g.w("spare"), ALU.subtract))
                ch.link(ve.tensor_tensor(r.slot[:], r.slot[:], r.weight[:], ALU.mult))
                ch.link(ve.tensor_tensor(r.slot[:], r.slot[:], g.w("spare"), ALU.add))
                ch.link(ve.tensor_copy(r.slot_u[:], r.slot[:]))
                ch.link(ve.tensor_tensor(r.weight[:], r.weight[:], r.m[:], ALU.mult))

        dispatch(nc, g, "sd", r, r.slot_u, win, 5)
        experts(nc, g, "se", 512, w1[:], w2[:], owner, ACT.Relu, b1=b1[:], b2=b2[:])
        norm_stage(nc, g, "n3", place=by_step(g), prior=Combine(nc, g, ctx, "sc", place_u, r.weight))


def choice_stage(nc, g):
    with ExitStack() as ctx:
        g.rows = ctx.enter_context(nc.sbuf_tensor("ec_rows", [P, NT, D], F32))
        r = Router(nc, g, ctx, "ec")
        sb = r.sb
        w1, w2 = sb("w1", [P, NX * 256]), sb("w2", [P, NX * 256])
        thr = sb("thr", [P, NX])
        trial = sb("trial", [P, WAYS, NX])
        reach = sb("reach", [P, WAYS - 1, NX, NT])
        reached = sb("reached", [P, WAYS - 1, NX])
        cand = sb("cand", [P, NX])
        part = sb("part", [P, NX])
        need = sb("need", [P, NX])
        gt = sb("gt", [P, NT, NX])
        eq = sb("eq", [P, NT, NX])
        tiles_i = sb("tiles_i", [P, NX], I32)
        ends = sb("ends", [P, NX])
        own = sb("own", [P, PAD_TILES, NX])
        ownf = sb("ownf", [P, PAD_TILES])
        owner = sb("owner", [P, PAD_TILES], I32)
        bits = sb("bits", [P, BITS // 2, WAYS], I32)
        K = float(T // NX)
        bits_in = r.sem("bits_in")
        win, parted, counted, chain, step, picked, ranked = (r.sem(n) for n in ("win", "parted", "counted", "chain2", "step", "picked", "ranked"))
        over = r.over_tiles
        by_expert = lambda a: a.rearrange("p n e -> p e n")

        def fetch(sp):
            sp.dma_start(bits[:], g.bits_dram.rearrange("p (i w) -> p i w", w=WAYS)).then_inc(bits_in, 16)
            sp.wait_ge(bits_in, 16)
            clear_places(sp, g)
            for t, d in ((w1, g.moe1["w1"]), (w2, g.moe1["w2"])):
                sp.dma_start(t[:], d).then_inc(win, 16)

        norm_stage(nc, g, "n5", keep=True, fetch=fetch)
        softmax_block(nc, g, r, g.w("gate1"), None)
        with nc.Block() as block:

            @block.tensor
            def _(pe):
                with pe.Fori(0, BITS // 2) as i:
                    pe.wait_ge(parted, i + 1)
                    pe.matmul(g.bank[3][:, 0:(WAYS - 1) * NX], g.w("allones"), reached[:].rearrange("p w e -> p (w e)"),
                              start=True, stop=True).then_inc(counted, 1)
                pe.wait_ge(parted, BITS // 2 + 1)
                pe.matmul(g.bank[3][:, 0:NX], g.w("allones"), part[:], start=True, stop=True).then_inc(counted, 1)
                for k in range(2):
                    pe.wait_ge(picked, k + 1)
                    count_flags(pe, g, (eq, r.oh)[k]).then_inc(ranked, 1)

            @block.vector
            def _(ve):
                ch = Chain(ve, chain)
                ch.link(ve.memset(thr[:], 0.0))
                by_trial = lambda a: a.rearrange("p (w e) -> p w e", e=NX)
                TRIALS = 3
                with ve.Fori(0, BITS // 2 // TRIALS) as group:
                    ch.enter(group, WAYS * TRIALS)
                    for i in (group * TRIALS + k for k in range(TRIALS)):
                        ways = bits[:, bass.ds(i, 1), :].rearrange("p o w -> p w o").broadcast_to([P, WAYS, NX])
                        ch.link(ve.tensor_tensor(trial[:].bitcast(I32), thr[:].bitcast(I32).rearrange("p (o e) -> p o e", o=1).broadcast_to([P, WAYS, NX]),
                                                 ways, ALU.bitwise_or))
                        for w in range(1, WAYS):
                            ins = ve.tensor_tensor(reach[:, w - 1].rearrange("p e n -> p n e"), r.p[:], over(trial[:, w, :]), ALU.is_ge)
                        ch.link(ins)
                        ve.tensor_reduce(reached[:], reach[:], AX_X, ALU.add).then_inc(parted, 1)
                        ve.wait_ge(counted, i + 1)
                        ch.link(ve.scalar_tensor_tensor(trial[:, 1:], by_trial(g.bank[3][:, 0:(WAYS - 1) * NX]), K, trial[:, 1:], ALU.is_ge, ALU.mult))
                        ch.link(ve.tensor_reduce(thr[:], trial[:].rearrange("p w e -> p e w"), AX_X, ALU.max))
                ch.leave(BITS // 2 // TRIALS)
                ch.link(ve.tensor_tensor(gt[:], r.p[:], over(thr[:]), ALU.is_gt))
                ve.tensor_tensor(eq[:], r.p[:], over(thr[:]), ALU.is_equal).then_inc(picked, 1)
                ve.tensor_reduce(part[:], by_expert(gt[:]), AX_X, ALU.add).then_inc(parted, 1)
                ve.wait_ge(counted, BITS // 2 + 1)
                ch.link(ve.tensor_scalar(need[:], g.bank[3][:, 0:NX], -1.0, K, ALU.mult, ALU.add))
                r.ranks(ve, ch, ranked, 1)
                ch.link(ve.tensor_tensor(r.pos[:], r.pos[:], over(need[:]), ALU.is_lt))
                ch.link(ve.tensor_tensor(eq[:], eq[:], r.pos[:], ALU.mult))
                ch.link(ve.tensor_tensor(gt[:], gt[:], eq[:], ALU.add))
                ch.link(ve.tensor_reduce(r.m[:], gt[:], AX_X, ALU.max))
                ch.link(ve.tensor_scalar(r.m[:], r.m[:], 0.0, None, ALU.is_equal))
                ch.link(ve.tensor_tensor(gt[:], gt[:], r.over_experts(r.m[:]), ALU.max))
                ch.link(ve.tensor_tensor(eq[:], r.p[:], gt[:], ALU.mult))
                ch.link(ve.scalar_tensor_tensor(eq[:], gt[:], -1.0, eq[:], ALU.add, ALU.add))
                ch.link(ve.tensor_reduce(r.weight[:], eq[:], AX_X, ALU.max))
                r.pick(ve, ch, eq[:], r.weight[:])
                ve.sem_inc(picked, 1)
                r.ranks(ve, ch, ranked, 2)
                ch.link(ve.tensor_tensor(r.t[:], r.oh[:], r.pos[:], ALU.mult))
                ch.link(ve.tensor_reduce(r.slot[:], r.t[:], AX_X, ALU.add))
                ch.link(ve.tensor_scalar(tiles_i[:], r.incl[:, :, NT - 1], float(P - 1), None, ALU.add))
                ch.link(ve.tensor_scalar(tiles_i[:], tiles_i[:], 7, None, ALU.arith_shift_right))
                ch.link(ve.tensor_copy(cand[:], tiles_i[:]))
                ch.link(ve.tensor_tensor_scan(ends[:], g.w("onerow")[:, 0:NX], cand[:], 0.0, ALU.mult, ALU.add))
                ch.link(ve.tensor_tensor(part[:], ends[:], cand[:], ALU.subtract))
                ch.link(ve.tensor_scalar(part[:], part[:], float(P), None, ALU.mult))
                ch.link(ve.tensor_tensor(r.t[:], r.oh[:], over(part[:]), ALU.mult))
                ch.link(ve.tensor_reduce(r.m2[:], r.t[:], AX_X, ALU.add))
                ch.link(ve.tensor_tensor(r.slot[:], r.slot[:], r.m2[:], ALU.add))
                ch.link(ve.tensor_copy(r.slot_u[:], r.slot[:]))
                ch.link(ve.tensor_tensor(own[:], ends[:].rearrange("p (o e) -> p o e", o=1).broadcast_to([P, PAD_TILES, NX]),
                                         g.w("tileidx").rearrange("p (n o) -> p n o", o=1).broadcast_to([P, PAD_TILES, NX]), ALU.is_le))
                ch.link(ve.tensor_reduce(ownf[:], own[:], AX_X, ALU.add))
                ch.link(ve.tensor_scalar(owner[:], ownf[:], float(NX - 1), None, ALU.min))

        dispatch(nc, g, "ed", r, r.slot_u, win, 2)
        experts(nc, g, "ee", 256, w1[:], w2[:], owner, ACT.Gelu)
        total = Combine(nc, g, ctx, "eo", r.slot_u, r.weight)
        with nc.Block() as block:
            parts = [range(k * NT // 4, (k + 1) * NT // 4) for k in range(4)]

            @block.gpsimd
            def _(pool):
                total.gather(pool, range(NT))

            @block.vector
            def _(ve):
                total.add(ve, range(NT))

            @block.sync
            def _(sp):
                for tiles in parts:
                    sp.wait_ge(total.added, tiles.stop)
                    h = slice(tiles.start, tiles.stop)
                    sp.dma_start(g.result.rearrange("(a p) d -> p a d", p=P)[:, h, :], g.X[:, h, :]).then_inc(g.stored, 16)
                sp.wait_ge(g.stored, 16 * len(parts))


FILL = -99999.0


def single_cross_stage(nc, g):
    with ExitStack() as ctx:
        sem = sem_maker(nc, ctx, "sa")
        sb = lambda name, shape, dt=F32: ctx.enter_context(nc.sbuf_tensor(f"sa_{name}", shape, dt))
        R = 2
        PPC = BPC // 2
        mask = sb("mask", [P, NT, P], I32)
        mask_in = sem("mask_in")

        def fetch(sp):
            for b in range(2):
                src = g.mask1_dram.rearrange("(o n) k -> o n k", o=1).broadcast_to([S, NT, P])
                sp.dma_start(mask[b * S:(b + 1) * S], src).then_inc(mask_in, 16)
            sp.wait_ge(mask_in, 32)

        norm_stage(nc, g, "n4", fetch=fetch)
        qT, kT, vT = sb("qT", [P, R, CH]), sb("kT", [P, R, CH]), sb("vT", [P, R, CH])
        v = sb("v", [P, R, PPC, D])
        on = sb("on", [P, R, PPC, P])
        low = sb("low", [P, R, PPC, P])
        sc = sb("sc", [P, R, PPC, P])
        pr = sb("pr", [P, R, PPC, P])
        pT = sb("pT", [P, R, PPC, P])
        nmx, rs, ri = sb("nmx", [P, R, PPC]), sb("rs", [P, R, PPC]), sb("ri", [P, R, PPC])
        proj, qkv, vt, vcopy, scored, vch, masked, exped, turned, tcopy, pv, added = (
            sem(n) for n in ("proj", "qkv", "vt", "vcopy", "scored", "vch", "masked", "exped", "turned", "tcopy", "pv", "added"))
        flat = lambda t, r: t[:, r].rearrange("p a k -> p (a k)")
        bank_p, bank_v, bank_s, bank_t, bank_o = g.bank[0:3], g.bank[3], g.bank[4:6], g.bank[6], g.bank[7]

        def run(eng, step):
            with eng.Fori(0, NC // R - 1) as i:
                for r in range(R):
                    step(i * R + r, r, False)
            for r in range(R):
                step(NC - R + r, r, r == R - 1)

        with nc.Block() as block:

            @block.tensor
            def _(pe):
                def project(c):
                    for k, (w, src) in enumerate((("Wq1", g.xT), ("Wk1", g.ctxT), ("Wv1", g.ctxT))):
                        pe.matmul(bank_p[k], g.w(w), src[:, bass.ts(c, CH)], start=True, stop=True).then_inc(proj, 1)

                def scores(c, r):
                    pe.wait_ge(qkv, c * 3 + 2)
                    for p in range(PPC):
                        ps = slice(p * P, (p + 1) * P)
                        ins = pe.matmul(bank_s[r][:, ps], qT[:, r, ps], kT[:, r, ps], start=True, stop=True)
                    ins.then_inc(scored, 1)

                def turn_v(c, r):
                    pe.wait_ge(qkv, c * 3 + 3)
                    pe.wait_ge(vcopy, c + 1)
                    for p in range(PPC):
                        ins = pe.transpose(bank_v[:, p * P:(p + 1) * P], vT[:, r, p * P:(p + 1) * P], g.ident)
                    ins.then_inc(vt, 1)

                def step(c, r, last):
                    if not last:
                        pe.wait_ge(qkv, c * 3 + 3)
                        project(c + 1)
                    pe.wait_ge(exped, c + 1)
                    for p in range(PPC):
                        ins = pe.transpose(bank_t[:, p * P:(p + 1) * P], pr[:, r, p, :], g.ident)
                    ins.then_inc(turned, 1)
                    if not last:
                        scores(c + 1, 1 - r)
                        turn_v(c + 1, 1 - r)
                    pe.wait_ge(tcopy, c + 1)
                    pe.wait_ge(vcopy, c + 2)
                    pe.wait_ge(added, c + 1)
                    for p in range(PPC):
                        ins = pe.matmul(bank_o[:, p * P:(p + 1) * P], pT[:, r, p, :], v[:, r, p, :], start=True, stop=True)
                    ins.then_inc(pv, 1)

                project(0)
                scores(0, 0)
                turn_v(0, 0)
                run(pe, step)

            @block.scalar
            def _(act):
                act.sem_inc(vcopy, 1)
                act.preload_act_table(ACT.Exp)

                def take(c, r):
                    for k, t in enumerate((qT, kT, vT)):
                        act.wait_ge(proj, c * 3 + (k + 1))
                        act.activation(t[:, r, :], bank_p[k], ACT.Copy).then_inc(qkv, 1)
                    act.wait_ge(vt, c + 1)
                    act.activation(flat(v, r), bank_v, ACT.Copy).then_inc(vcopy, 1)
                    act.wait_ge(masked, c + 1)
                    for p in range(PPC):
                        ins = act.activation(pr[:, r, p, :], sc[:, r, p, :], ACT.Exp, bias=nmx[:, r, p:p + 1],
                                             accum_out=rs[:, r, p:p + 1])
                    ins.then_inc(exped, 1)

                def step(c, r, last):
                    if not last:
                        take(c + 1, 1 - r)

                take(0, 0)
                run(act, step)

            @block.vector
            def _(ve):
                PER = 5
                ve.sem_inc(added, 1)

                def link(c, k, ins):
                    ins.then_inc(vch, 1)
                    ve.wait_ge(vch, c * PER + k)

                def mask_scores(c, r):
                    row = lambda w: g.w(w).rearrange("p (o k) -> p o k", o=1).broadcast_to([P, PPC, P])
                    link(c, 1, ve.scalar_tensor_tensor(on[:, r], mask[:, bass.ts(c, PPC), :], 0.0, row("same"), ALU.not_equal, ALU.mult))
                    link(c, 2, ve.scalar_tensor_tensor(low[:, r], on[:, r], 1.0, row("neglow"), ALU.subtract, ALU.mult))
                    ve.wait_ge(scored, c + 1)
                    link(c, 3, ve.tensor_tensor(flat(sc, r), bank_s[r], flat(on, r), ALU.mult))
                    link(c, 4, ve.tensor_tensor(flat(sc, r), flat(sc, r), flat(low, r), ALU.add))
                    ve.tensor_reduce(nmx[:, r, :], sc[:, r], AX_X, ALU.max, negate=True).then_inc(masked, 1)

                def step(c, r, last):
                    ve.wait_ge(turned, c + 1)
                    ve.tensor_copy(flat(pT, r), bank_t).then_inc(tcopy, 1)
                    ve.reciprocal(ri[:, r, :], rs[:, r, :]).then_inc(vch, 1)
                    if not last:
                        mask_scores(c + 1, 1 - r)
                    else:
                        ve.wait_ge(vch, NC * PER)
                    ve.wait_ge(pv, c + 1)
                    for p in range(PPC):
                        x = g.X[:, bass.ds(c * PPC + p, 1), :].rearrange("p a d -> p (a d)")
                        ins = ve.scalar_tensor_tensor(x, bank_o[:, p * P:(p + 1) * P], ri[:, r, p:p + 1], x, ALU.mult, ALU.add)
                    ins.then_inc(added, 1)

                mask_scores(0, 0)
                run(ve, step)


def layout():
    H = E0 // P
    items = [("ident", P), ("norm_w", 1), ("inT", E0), ("skipT", E0), ("convc", H * KC), ("conv_b", H), ("wd1T", H * DD),
             ("wd2T", E0), ("wd2_b", H), ("wbcT", H * P), ("A_log", H * NS), ("W_D", H), ("outT", H * D), ("big", 32),
             ("WQ0", D), ("WQ1", D), ("bq", NG), ("WK0", D), ("WK1", D), ("bK0", 1), ("bK1", 1), ("WV", D), ("bv", 1), ("Wo", D), ("bo", D), ("headrow", HG), ("ones", P)]
    for l in range(2):
        items += [(f"sW{l}", GATES * D), (f"sR{l}", GATES * D), (f"sP{l}", D), (f"spb{l}", 1), (f"sga{l}", 1), (f"sbe{l}", 1)]
    items += [("sbrow0", GATES * D), ("sbrow1", GATES * D), ("garow", D), ("berow", D)]
    items += [("Wq1", D), ("Wk1", D), ("Wv1", D), ("same", P), ("neglow", P)]
    items += [("gate0", NX), ("gateb0", NX), ("gate1", NX), ("eidx", NX), ("before", P), ("allones", P), ("onerow", NT), ("spare", NT),
              ("tileidx", PAD_TILES)]
    at, out = 0, {}
    for n, w in items:
        out[n] = (at, w)
        at += w
    return out, at


def program(nc, x, packed, sel, ctxT, bias, mask8, pairsel, moe0, moe1, bits, mask1, out):
    lay, width = layout()
    g = Core()
    g.lay = lay
    with ExitStack() as ctx:
        g.lasting = lambda name: ctx.enter_context(nc.semaphore(name))
        sb = lambda name, shape, dt=F32: ctx.enter_context(nc.sbuf_tensor(name, shape, dt))
        g.X = sb("X", [P, NT, D])
        g.xT = sb("xT", [P, T])
        g.wts = sb("wts", [P, width])
        g.w = lambda n: g.wts[:, lay[n][0]:lay[n][0] + lay[n][1]]
        g.ident = g.w("ident")
        g.zero = sb("zero", [P, CH])
        g.cleared, g.clears = ctx.enter_context(nc.semaphore("cleared")), 0
        g.neghalf = sb("neghalf", [P, NT])
        first, early = lay["inT"][0], lay["WQ0"][0]
        g.early_in, g.late_in = ctx.enter_context(nc.semaphore("early_in")), ctx.enter_context(nc.semaphore("late_in"))

        def fetch_weights(sp):
            sp.dma_start(g.wts[:, first:early], packed[:, first:early]).then_inc(g.early_in, 16)
            sp.dma_start(g.wts[:, early:], packed[:, early:]).then_inc(g.late_in, 16)
            sp.dma_start(g.pairsel[:], pairsel).then_inc(g.late_in, 16)
            sp.wait_ge(g.early_in, 16)

        g.fetch_weights = fetch_weights
        g.ctxT, g.ctxT_dram, g.ctxT_in = None, ctxT, ctx.enter_context(nc.semaphore("ctxT_in"))
        g.sel_dram, g.bias_dram, g.mask8_dram = sel, bias, mask8
        g.mask1_dram = mask1
        g.moe0, g.moe1, g.bits_dram = moe0, moe1, bits
        g.buf = nc.dram_tensor("places", (PAD_TILES * P + T, D), F32, kind="Internal").ap()
        g.out = nc.dram_tensor("place_results", (TILES * P, D), F32, kind="Internal").ap()
        g.pairsel = sb("pairsel", [2, P], BF16)
        g.ps = ctx.enter_context(nc.psum_tensor("ps", [P, 8, CH], F32))
        g.bank = [g.ps[:, i, :] for i in range(8)]
        loaded = ctx.enter_context(nc.semaphore("loaded"))
        consts = ctx.enter_context(nc.semaphore("consts"))
        g.result, g.stored = out, ctx.enter_context(nc.semaphore("stored"))
        with nc.Block() as block:

            @block.sync
            def _(sp):
                sp.dma_start(g.X[:], x.rearrange("(a p) d -> p a d", p=P)).then_inc(loaded, 16)
                sp.dma_start(g.wts[:, 0:first], packed[:, 0:first]).then_inc(loaded, 16)
                sp.wait_ge(loaded, 32)

            @block.vector
            def _(ve):
                ve.memset(g.neghalf[:], -0.5).then_inc(consts, 1)
                ve.memset(g.zero[:], 0.0).then_inc(consts, 1)

        stages = [scan_stage, cross_stage, switch_stage, lstm_stage, single_cross_stage, choice_stage]
        for f in stages:
            if g.ctxT is None and f is not scan_stage:
                g.ctxT = sb("ctxT", [P, T])
            f(nc, g)


def pack(inp):
    lay, width = layout()
    H = E0 // P
    arr = np.zeros((P, width), np.float32)

    def put(name, a):
        at, w = lay[name]
        a = np.asarray(a)
        arr[:a.shape[0], at:at + a.shape[1]] = a

    halves = lambda a: np.concatenate([a[h * P:(h + 1) * P] for h in range(H)], axis=1)
    rows3 = lambda a: np.where(np.isin(np.arange(P), (0, 32, 64))[:, None], a, np.float32(0.0))
    I = lambda n: np.asarray(inp["L0_attn_" + n])
    put("ident", np.eye(P, dtype=np.float32))
    put("norm_w", I("norm_w")[:, None])
    put("inT", I("in_w").T)
    put("skipT", I("skip_w").T)
    put("convc", halves(I("conv_w")[:, 0, :]))
    put("conv_b", halves(I("conv_b")[:, None]))
    put("wd1T", halves(I("wd1").T))
    put("wd2T", I("wd2").T)
    put("wd2_b", halves(I("wd2_b")[:, None]))
    bc = np.concatenate([I("wb").T, I("wc").T], axis=1)
    put("wbcT", halves(np.concatenate([bc, bc, bc, bc], axis=1)))
    put("A_log", halves(I("A_log")))
    put("W_D", halves(I("W_D")[:, None]))
    put("outT", halves(I("out_w").T))
    put("big", np.full((P, 32), BIG, np.float32))
    I = lambda n: np.asarray(inp["L0_xattn_" + n])
    twice = lambda a, k: np.concatenate([a[..., k * S:(k + 1) * S]] * 2, axis=-1)
    for k in range(NG):
        put(f"WQ{k}", twice(I("Wq"), k))
        put(f"WK{k}", twice(I("Wk"), k))
        put(f"bK{k}", twice(I("bk"), k)[:, None])
    put("WV", I("Wv"))
    put("Wo", I("Wo"))
    put("bq", np.stack([twice(I("bq"), k) for k in range(NG)], axis=1))
    put("bv", I("bv")[:, None])
    put("bo", I("bo")[None, :])
    put("headrow", (np.arange(P)[:, None] % S // DK == np.arange(HG)[None, :]).astype(np.float32))
    put("ones", np.ones((1, P), np.float32))
    I = lambda n: np.asarray(inp["L1_attn_" + n])
    for l in range(2):
        put(f"sW{l}", I(f"W{l}").T)
        put(f"sR{l}", I(f"R{l}").T)
        put(f"sbrow{l}", rows3(I(f"b{l}").reshape(1, GATES * P)))
        put(f"sP{l}", I(f"projW{l}").T)
        put(f"spb{l}", I(f"projb{l}")[:, None])
        put(f"sga{l}", I(f"gamma{l}")[:, None])
        put(f"sbe{l}", I(f"beta{l}")[:, None])
    for n in ("Wq", "Wk", "Wv"):
        put(n + "1", np.asarray(inp["L1_xattn_" + n]).T)
    same = np.arange(P)[:, None] // S == np.arange(P)[None, :] // S
    put("same", same.astype(np.float32))
    put("neglow", np.where(same, np.float32(-FILL), np.float32(1.0e30)))
    put("gate0", np.asarray(inp["L0_ffn_gate_w"]).T)
    put("gateb0", np.broadcast_to(np.asarray(inp["L0_ffn_gate_b"])[None, :], (P, NX)))
    put("gate1", inp["L1_ffn_Wg"])
    put("eidx", np.broadcast_to(np.arange(NX, dtype=np.float32)[None, :], (P, NX)))
    put("before", np.triu(np.ones((P, P), np.float32), 1))
    put("allones", np.ones((P, P), np.float32))
    put("onerow", np.ones((P, NT), np.float32))
    put("spare", (np.arange(NT)[None, :] * P + np.arange(P)[:, None] + PAD_TILES * P).astype(np.float32))
    put("tileidx", np.broadcast_to(np.arange(PAD_TILES, dtype=np.float32)[None, :], (P, PAD_TILES)))
    put("garow", np.broadcast_to(I("gamma1")[None, :], (P, D)))
    put("berow", np.broadcast_to(I("beta1")[None, :], (P, D)))
    return arr


def relative(rel_bias):
    rel = np.asarray(rel_bias)
    span = rel.shape[1] // 2
    at = np.arange(S)[:, None] - np.arange(S)[None, :] + span
    one = rel[:, at].transpose(1, 0, 2)
    return np.ascontiguousarray(np.concatenate([one, one], axis=0))


def selectors():
    s = np.zeros((P, 2 * NS, P), mybir.dt.np(BF16))
    for q in (0, 2, 3):
        for n in range(2 * NS):
            s[32 * q + n, n, :] = 1
    return s


def kernel(**inputs):
    import concourse.bacc as bacc
    from concourse.bass_utils import run_bass_kernel_spmd as run

    nc = bacc.Bacc("TRN2", target_bir_lowering=False, num_devices=1)
    arrays = {"x": np.ascontiguousarray(np.asarray(inputs["x"]).reshape(T, D)), "packed": pack(inputs), "sel": selectors()}
    arrays["ctxT"] = np.ascontiguousarray(np.asarray(inputs["ctx_1024"]).reshape(T, D).T)
    arrays["bias"] = relative(inputs["L0_xattn_rel_bias"])
    arrays["mask8"] = np.ascontiguousarray(np.asarray(inputs["mask_BxS2_bf0"]).view(np.uint8).reshape(NT, 2, S).transpose(1, 0, 2).reshape(2, T // 2)).view(np.int32)
    arrays["pairsel"] = np.repeat(np.eye(2), S, axis=1).astype(mybir.dt.np(BF16))
    arrays["mask1"] = np.ascontiguousarray(np.asarray(inputs["mask_BxS2_ik1"]).reshape(NT, 2 * S))
    I = lambda n: np.asarray(inputs[n])
    for l, F in ((0, 512), (1, 256)):
        w1, w2 = (I("L0_ffn_w1"), I("L0_ffn_w2")) if l == 0 else (I("L1_ffn_W1"), I("L1_ffn_W2"))
        arrays[f"w1_{l}"] = np.ascontiguousarray(w1.transpose(1, 0, 2).reshape(P, NX * F))
        arrays[f"w2_{l}"] = np.ascontiguousarray(w2.reshape(NX, F // P, P, D).transpose(2, 0, 1, 3).reshape(P, NX * F))
    arrays["b1_0"] = np.ascontiguousarray(np.broadcast_to(I("L0_ffn_b1").reshape(1, -1), (P, NX * 512)))
    arrays["b2_0"] = np.ascontiguousarray(np.broadcast_to(I("L0_ffn_b2").reshape(1, -1), (P, NX * D)))
    arrays["owner0"] = np.minimum(np.arange(PAD_TILES) // (CAP // P), NX - 1).astype(np.int32)[None, :]
    high = np.arange(BITS - 1, 0, -2)
    ways = np.stack([0 * high, 1 << (high - 1), 1 << high, (1 << high) | (1 << (high - 1))], axis=1)
    arrays["bits"] = np.ascontiguousarray(np.broadcast_to(ways.reshape(1, -1), (P, BITS // 2 * WAYS))).astype(np.int32)
    ap = {n: nc.dram_tensor("in_" + n, a.shape, mybir.dt.from_np(a.dtype), kind="ExternalInput").ap() for n, a in arrays.items()}
    out = nc.dram_tensor("out_0_dram", (T, D), F32, kind="ExternalOutput").ap()
    moe0 = {"w1": ap["w1_0"], "w2": ap["w2_0"], "b1": ap["b1_0"], "b2": ap["b2_0"], "owner": ap["owner0"]}
    moe1 = {"w1": ap["w1_1"], "w2": ap["w2_1"]}
    program(nc, ap["x"], ap["packed"], ap["sel"], ap["ctxT"], ap["bias"], ap["mask8"], ap["pairsel"], moe0, moe1, ap["bits"], ap["mask1"], out)
    r = run(nc, [{"in_" + n: a for n, a in arrays.items()}], core_ids=[0])
    return r.results[0]["out_0_dram"].reshape(B, S, D)
```
